# Optimizing a Trainium2 kernel written in Bass

```python
import numpy as np
import jax
import jax.numpy as jnp

def _softmax(x, axis=-1):
    return jax.nn.softmax(x, axis=axis)

def _gelu(x):
    return jax.nn.gelu(x, approximate=True)

def _silu(x):
    return jax.nn.silu(x)

def _sigmoid(x):
    return jax.nn.sigmoid(x)

def _layernorm(x, axis=-1, eps=1e-05):
    m = jnp.mean(x, axis=axis, keepdims=True)
    v = jnp.var(x, axis=axis, keepdims=True)
    return (x - m) / jnp.sqrt(v + eps)

def _scatter_add(tgt, idx, src, axis=0):
    return tgt.at[idx].add(src)

def _segment_sum(src, seg, n):
    return jax.ops.segment_sum(src, seg, n)
kernel_name = 'mk_recurrent_d4_jaxref_r8_cec5b2'

def setup_inputs(seed: int=0):
    np.random.seed(seed)
    _w = jnp.asarray

    def _L0_attn_setup():
        import jax, jax.numpy as jnp
        import numpy as np
        HEADS = 16
        DIM_HEAD = 64
        SCALE = 8.0
        NUM_NULL_KV = 2
        NON_CAUSAL_PREFIX = 64
        LN_EPS = 1e-05

        def _l2norm(t):
            n = jnp.sqrt(jnp.sum(t * t, axis=-1, keepdims=True))
            return t / jnp.maximum(n, 1e-12)

        def _layer_norm(x, gamma):
            mu = jnp.mean(x, axis=-1, keepdims=True)
            var = jnp.mean((x - mu) ** 2, axis=-1, keepdims=True)
            return (x - mu) * jax.lax.rsqrt(var + LN_EPS) * gamma
        key = jax.random.key(seed)
        ks = jax.random.split(key, 6)
        b, n, dim = (2, 256, 128)
        inner = HEADS * DIM_HEAD
        return {'x': jax.random.normal(ks[0], (b, n, dim), jnp.float32), 'gamma': jnp.ones((dim,), jnp.float32), 'Wq': jax.random.normal(ks[1], (dim, inner), jnp.float32) * dim ** (-0.5), 'Wkv': jax.random.normal(ks[2], (dim, 2 * DIM_HEAD), jnp.float32) * dim ** (-0.5), 'q_scale': jnp.ones((DIM_HEAD,), jnp.float32), 'k_scale': jnp.ones((DIM_HEAD,), jnp.float32), 'null_kv': jax.random.normal(ks[3], (2, NUM_NULL_KV, DIM_HEAD), jnp.float32), 'Wout': jax.random.normal(ks[4], (inner, dim), jnp.float32) * inner ** (-0.5)}
    _L0_attn_in = _L0_attn_setup()

    def _L0_ffn_setup():
        import jax, jax.numpy as jnp
        import numpy as np
        B, S, D, E, TOP_K = (2, 128, 128, 8, 2)
        H = 4 * D
        key = jax.random.key(seed)
        ks = jax.random.split(key, 12)
        sc = 0.02
        return {'x': jax.random.normal(ks[0], (B, S, D), jnp.float32), 'Wg': jax.random.normal(ks[1], (E, D), jnp.float32) * sc, 'bg': jnp.zeros((E,), jnp.float32), 'bias': jnp.zeros((E,), jnp.float32), 'W1': jax.random.normal(ks[2], (E, H, D), jnp.float32) * sc, 'b1': jnp.zeros((E, H), jnp.float32), 'W2': jax.random.normal(ks[3], (E, D, H), jnp.float32) * sc, 'b2': jnp.zeros((E, D), jnp.float32), 'Ws1': jax.random.normal(ks[4], (H, D), jnp.float32) * sc, 'bs1': jnp.zeros((H,), jnp.float32), 'Ws2': jax.random.normal(ks[5], (D, H), jnp.float32) * sc, 'bs2': jnp.zeros((D,), jnp.float32)}
    _L0_ffn_in = _L0_ffn_setup()

    def _L1_attn_setup():
        import jax, jax.numpy as jnp
        import numpy as np
        B, S, D, H, A = (2, 256, 128, 16, 64)
        INIT_STD = 0.02
        key = jax.random.key(seed)
        ks = jax.random.split(key, 5)
        return {'residual': jax.random.normal(ks[0], (B, S, D), dtype=jnp.float32), 'Wq': jax.random.normal(ks[1], (H, D, A), dtype=jnp.float32) * INIT_STD, 'Wk': jax.random.normal(ks[2], (H, D, A), dtype=jnp.float32) * INIT_STD, 'Wv': jax.random.normal(ks[3], (H, D, A), dtype=jnp.float32) * INIT_STD, 'Wo': jax.random.normal(ks[4], (H, A, D), dtype=jnp.float32) * INIT_STD, 'bq': jnp.zeros((H, A), dtype=jnp.float32), 'bk': jnp.zeros((H, A), dtype=jnp.float32), 'bv': jnp.zeros((H, A), dtype=jnp.float32), 'bo': jnp.zeros((D,), dtype=jnp.float32)}
    _L1_attn_in = _L1_attn_setup()

    def _L1_ffn_setup():
        import jax, jax.numpy as jnp
        import numpy as np
        D_MODEL = 128
        FFN = 128
        N_EXPERTS = 8
        N_SHARED = 1
        TOP_K = 2
        B, S = (2, 256)

        def _swiglu(h):
            a, b = jnp.split(h, 2, axis=-1)
            return jax.nn.silu(a) * b
        key = jax.random.key(seed)
        ks = jax.random.split(key, 12)
        sc = 0.02
        return {'x': jax.random.normal(ks[0], (B, S, D_MODEL), dtype=jnp.float32), 'gate_w': jax.random.normal(ks[1], (D_MODEL, N_EXPERTS), dtype=jnp.float32) * sc, 'gate_b': jnp.zeros((N_EXPERTS,), dtype=jnp.float32), 'sw1': jax.random.normal(ks[2], (N_SHARED, D_MODEL, 2 * FFN), dtype=jnp.float32) * sc, 'sb1': jnp.zeros((N_SHARED, 2 * FFN), dtype=jnp.float32), 'sw2': jax.random.normal(ks[3], (N_SHARED, FFN, D_MODEL), dtype=jnp.float32) * sc, 'sb2': jnp.zeros((N_SHARED, D_MODEL), dtype=jnp.float32), 'rw1': jax.random.normal(ks[4], (N_EXPERTS, D_MODEL, 2 * FFN), dtype=jnp.float32) * sc, 'rb1': jnp.zeros((N_EXPERTS, 2 * FFN), dtype=jnp.float32), 'rw2': jax.random.normal(ks[5], (N_EXPERTS, FFN, D_MODEL), dtype=jnp.float32) * sc, 'rb2': jnp.zeros((N_EXPERTS, D_MODEL), dtype=jnp.float32)}
    _L1_ffn_in = _L1_ffn_setup()

    def _L2_attn_setup():
        import jax, jax.numpy as jnp
        import numpy as np
        B, L, DIM = (8, 128, 128)
        D_MODEL = DIM // 2
        D_INNER = 2 * D_MODEL
        D_STATE = 16
        D_CONV = 4
        DT_RANK = D_MODEL // 16

        def _mamba_params(key, scale=0.02):
            ks = jax.random.split(key, 7)
            p = {'Win': jax.random.normal(ks[0], (DIM, 2 * D_INNER), jnp.float32) * scale, 'Wconv': jax.random.normal(ks[1], (D_INNER, D_CONV), jnp.float32) * scale, 'bconv': jnp.zeros((D_INNER,), jnp.float32), 'Wx': jax.random.normal(ks[2], (D_INNER, DT_RANK + 2 * D_STATE), jnp.float32) * scale, 'Wdt': jax.random.normal(ks[3], (DT_RANK, D_INNER), jnp.float32) * scale, 'bdt': jax.random.normal(ks[4], (D_INNER,), jnp.float32) * 0.1, 'Alog': jnp.log(jnp.broadcast_to(jnp.arange(1, D_STATE + 1, dtype=jnp.float32), (D_INNER, D_STATE))), 'Dp': jnp.ones((D_INNER,), jnp.float32), 'Wout': jax.random.normal(ks[5], (D_INNER, D_MODEL), jnp.float32) * scale}
            return p

        def _layernorm(x, g, b, eps=1e-05):
            mu = jnp.mean(x, axis=-1, keepdims=True)
            var = jnp.var(x, axis=-1, keepdims=True)
            return (x - mu) * jax.lax.rsqrt(var + eps) * g + b

        def _mamba(h, Win, Wconv, bconv, Wx, Wdt, bdt, Alog, Dp, Wout):
            xz = h @ Win
            x, z = jnp.split(xz, 2, axis=-1)
            xp = jnp.pad(x, ((0, 0), (D_CONV - 1, 0), (0, 0)))
            x = sum((xp[:, k:k + h.shape[1], :] * Wconv[None, None, :, k] for k in range(D_CONV))) + bconv
            x = jax.nn.silu(x)
            dbc = x @ Wx
            dt = jax.nn.softplus(dbc[..., :DT_RANK] @ Wdt + bdt)
            Bm = dbc[..., DT_RANK:DT_RANK + D_STATE]
            Cm = dbc[..., DT_RANK + D_STATE:]
            A = -jnp.exp(Alog)
            dA = jnp.exp(dt[..., None] * A)
            dBx = dt[..., None] * Bm[:, :, None, :] * x[..., None]

            def step(hc, ins):
                dA_t, dBx_t, C_t = ins
                hc = dA_t * hc + dBx_t
                y = jnp.einsum('bdn,bn->bd', hc, C_t)
                return (hc, y)
            h0 = jnp.zeros((x.shape[0], D_INNER, D_STATE), x.dtype)
            _, ys = jax.lax.scan(step, h0, (dA.transpose(1, 0, 2, 3), dBx.transpose(1, 0, 2, 3), Cm.transpose(1, 0, 2)))
            y = ys.transpose(1, 0, 2)
            y = (y + Dp * x) * jax.nn.silu(z)
            return y @ Wout
        key = jax.random.key(seed)
        kx, k1, k2 = jax.random.split(key, 3)
        inp = {'x': jax.random.normal(kx, (B, L, DIM), jnp.float32), 'ln_g': jnp.ones((DIM,), jnp.float32), 'ln_b': jnp.zeros((DIM,), jnp.float32)}
        for tag, k in (('m1', k1), ('m2', k2)):
            for name, v in _mamba_params(k).items():
                inp[f'{tag}_{name}'] = v
        return inp
    _L2_attn_in = _L2_attn_setup()

    def _L2_ffn_setup():
        import jax, jax.numpy as jnp
        import numpy as np
        DIM = 128
        DEPTH = 6
        HEADS = 16
        DIM_HEAD = 64
        WINDOW = 32
        INNER = HEADS * DIM_HEAD
        DIM_INNER = int(DIM * 4 * 2 / 3)
        QK_SCALE = 8.0

        def shift_tokens(t):
            a, s = jnp.split(t, 2, -1)
            s = jnp.pad(s, ((0, 0), (1, 0), (0, 0)))[:, :-1]
            return jnp.concatenate([a, s], -1)

        def l2norm(t):
            return t / jnp.maximum(jnp.linalg.norm(t, axis=-1, keepdims=True), 1e-12)

        def rotate_half(x):
            x1, x2 = jnp.split(x, 2, -1)
            return jnp.concatenate([-x2, x1], -1)

        def rotary_tables(n):
            half = jnp.arange(0, DIM_HEAD, 2, dtype=jnp.float32)
            inv_freq = 1.0 / 10000.0 ** (half / DIM_HEAD)
            t = jnp.arange(n, dtype=jnp.float32)
            freqs = t[:, None] * inv_freq[None, :]
            freqs = jnp.concatenate([freqs, freqs], -1)
            base_scale = (half + 0.4 * DIM_HEAD) / (1.4 * DIM_HEAD)
            power = (t - n // 2) / (WINDOW // 2)
            scale = base_scale[None, :] ** power[:, None]
            scale = jnp.concatenate([scale, scale], -1)
            return (freqs, scale)

        def local_attention(q, k, v):
            b, h, n, d = q.shape
            w = WINDOW
            nw = n // w
            bq = q.reshape(b, h, nw, w, d)
            bk = k.reshape(b, h, nw, w, d)
            bv = v.reshape(b, h, nw, w, d)

            def look(t):
                p = jnp.pad(t, ((0, 0), (0, 0), (1, 0), (0, 0), (0, 0)))
                return jnp.concatenate([p[:, :, :nw], p[:, :, 1:]], axis=3)
            bk2, bv2 = (look(bk), look(bv))
            seq = jnp.arange(n).reshape(nw, w)
            seq_p = jnp.pad(seq, ((1, 0), (0, 0)), constant_values=-1)
            jt = jnp.concatenate([seq_p[:nw], seq_p[1:]], axis=1)
            it = seq[:, :, None]
            jb = jt[:, None, :]
            mask = (it < jb) | (it > jb + w) | (jb == -1)
            sim = jnp.einsum('bhwie,bhwje->bhwij', bq, bk2) * QK_SCALE
            sim = jnp.where(mask, -jnp.finfo(sim.dtype).max, sim)
            attn = jax.nn.softmax(sim, -1)
            out = jnp.einsum('bhwij,bhwje->bhwie', attn, bv2)
            return out.reshape(b, h, n, d)

        def attn_layer(x, Wqkv, qs, ksc, Wo):
            b, n, _ = x.shape
            qkv = x @ Wqkv
            q, k, v = jnp.split(qkv, 3, -1)
            sh = lambda t: t.reshape(b, n, HEADS, DIM_HEAD).transpose(0, 2, 1, 3)
            q, k, v = (sh(q), sh(k), sh(v))
            q = l2norm(q) * qs
            k = l2norm(k) * ksc
            freqs, scale = rotary_tables(n)
            cos, sin = (jnp.cos(freqs), jnp.sin(freqs))
            q = q * cos * scale + rotate_half(q) * sin * scale
            inv = 1.0 / scale
            k = k * cos * inv + rotate_half(k) * sin * inv
            out = local_attention(q, k, v)
            out = out.transpose(0, 2, 1, 3).reshape(b, n, INNER)
            return out @ Wo

        def ffn_layer(x, g, bln, W1, b1, W2, b2):
            mu = x.mean(-1, keepdims=True)
            var = ((x - mu) ** 2).mean(-1, keepdims=True)
            xn = (x - mu) / jnp.sqrt(var + 1e-05) * g + bln
            hg = xn @ W1 + b1
            a, gate = jnp.split(hg, 2, -1)
            return a * jax.nn.gelu(gate, approximate=False) @ W2 + b2
        key = jax.random.key(seed)
        ks = jax.random.split(key, 8)
        B, N = (2, 256)
        init = lambda k, shape: jax.random.normal(k, shape, jnp.float32) * 0.02
        return {'x': jax.random.normal(ks[0], (B, N, DIM), jnp.float32), 'Wqkv': init(ks[1], (DEPTH, DIM, 3 * INNER)), 'q_scale': jnp.ones((DEPTH, DIM_HEAD), jnp.float32), 'k_scale': jnp.ones((DEPTH, DIM_HEAD), jnp.float32), 'Wo': init(ks[2], (DEPTH, INNER, DIM)), 'ln_g': jnp.ones((DEPTH, DIM), jnp.float32), 'ln_b': jnp.zeros((DEPTH, DIM), jnp.float32), 'W1': init(ks[3], (DEPTH, DIM, 2 * DIM_INNER)), 'b1': jnp.zeros((DEPTH, 2 * DIM_INNER), jnp.float32), 'W2': init(ks[4], (DEPTH, DIM_INNER, DIM)), 'b2': jnp.zeros((DEPTH, DIM), jnp.float32)}
    _L2_ffn_in = _L2_ffn_setup()

    def _L3_attn_setup():
        import jax, jax.numpy as jnp
        import numpy as np
        NUM_HEADS = 16
        USE_MASKING = True
        NEG_INF = -1000000000.0
        key = jax.random.key(seed)
        k1, k2 = jax.random.split(key)
        B, S, D = (2, 256, 128)
        x = jax.random.normal(k1, (B, S, D), dtype=jnp.float32)
        qkv_weights = jax.random.normal(k2, (D, 3 * D), dtype=jnp.float32) * (1.0 / np.sqrt(D))
        return {'x': x, 'qkv_weights': qkv_weights}
    _L3_attn_in = _L3_attn_setup()

    def _L3_ffn_setup():
        import jax, jax.numpy as jnp
        import numpy as np
        TOP_K = 2
        key = jax.random.key(seed)
        k0, k1, k2, k3 = jax.random.split(key, 4)
        B, T, C, E, F = (4, 256, 128, 8, 512)
        x = jax.random.normal(k0, (B, T, C), dtype=jnp.float32)
        gate_w = jax.random.normal(k1, (C, E), dtype=jnp.float32) * 0.02
        w1 = jax.random.normal(k2, (E, C, F), dtype=jnp.float32) * 0.02
        w2 = jax.random.normal(k3, (E, F, C), dtype=jnp.float32) * 0.02
        return {'x': x, 'gate_w': gate_w, 'w1': w1, 'w2': w2}
    _L3_ffn_in = _L3_ffn_setup()
    _d = {'L0_attn_x': _L0_attn_in['x'], 'L0_attn_gamma': _L0_attn_in['gamma'], 'L0_attn_Wq': _L0_attn_in['Wq'], 'L0_attn_Wkv': _L0_attn_in['Wkv'], 'L0_attn_q_scale': _L0_attn_in['q_scale'], 'L0_attn_k_scale': _L0_attn_in['k_scale'], 'L0_attn_null_kv': _L0_attn_in['null_kv'], 'L0_attn_Wout': _L0_attn_in['Wout'], 'L0_ffn_Wg': _L0_ffn_in['Wg'], 'L0_ffn_bg': _L0_ffn_in['bg'], 'L0_ffn_bias': _L0_ffn_in['bias'], 'L0_ffn_W1': _L0_ffn_in['W1'], 'L0_ffn_b1': _L0_ffn_in['b1'], 'L0_ffn_W2': _L0_ffn_in['W2'], 'L0_ffn_b2': _L0_ffn_in['b2'], 'L0_ffn_Ws1': _L0_ffn_in['Ws1'], 'L0_ffn_bs1': _L0_ffn_in['bs1'], 'L0_ffn_Ws2': _L0_ffn_in['Ws2'], 'L0_ffn_bs2': _L0_ffn_in['bs2'], 'L1_attn_Wq': _L1_attn_in['Wq'], 'L1_attn_Wk': _L1_attn_in['Wk'], 'L1_attn_Wv': _L1_attn_in['Wv'], 'L1_attn_Wo': _L1_attn_in['Wo'], 'L1_attn_bq': _L1_attn_in['bq'], 'L1_attn_bk': _L1_attn_in['bk'], 'L1_attn_bv': _L1_attn_in['bv'], 'L1_attn_bo': _L1_attn_in['bo'], 'L1_ffn_gate_w': _L1_ffn_in['gate_w'], 'L1_ffn_gate_b': _L1_ffn_in['gate_b'], 'L1_ffn_sw1': _L1_ffn_in['sw1'], 'L1_ffn_sb1': _L1_ffn_in['sb1'], 'L1_ffn_sw2': _L1_ffn_in['sw2'], 'L1_ffn_sb2': _L1_ffn_in['sb2'], 'L1_ffn_rw1': _L1_ffn_in['rw1'], 'L1_ffn_rb1': _L1_ffn_in['rb1'], 'L1_ffn_rw2': _L1_ffn_in['rw2'], 'L1_ffn_rb2': _L1_ffn_in['rb2'], 'L2_attn_ln_g': _L2_attn_in['ln_g'], 'L2_attn_ln_b': _L2_attn_in['ln_b'], 'L2_attn_m1_Win': _L2_attn_in['m1_Win'], 'L2_attn_m1_Wconv': _L2_attn_in['m1_Wconv'], 'L2_attn_m1_bconv': _L2_attn_in['m1_bconv'], 'L2_attn_m1_Wx': _L2_attn_in['m1_Wx'], 'L2_attn_m1_Wdt': _L2_attn_in['m1_Wdt'], 'L2_attn_m1_bdt': _L2_attn_in['m1_bdt'], 'L2_attn_m1_Alog': _L2_attn_in['m1_Alog'], 'L2_attn_m1_Dp': _L2_attn_in['m1_Dp'], 'L2_attn_m1_Wout': _L2_attn_in['m1_Wout'], 'L2_attn_m2_Win': _L2_attn_in['m2_Win'], 'L2_attn_m2_Wconv': _L2_attn_in['m2_Wconv'], 'L2_attn_m2_bconv': _L2_attn_in['m2_bconv'], 'L2_attn_m2_Wx': _L2_attn_in['m2_Wx'], 'L2_attn_m2_Wdt': _L2_attn_in['m2_Wdt'], 'L2_attn_m2_bdt': _L2_attn_in['m2_bdt'], 'L2_attn_m2_Alog': _L2_attn_in['m2_Alog'], 'L2_attn_m2_Dp': _L2_attn_in['m2_Dp'], 'L2_attn_m2_Wout': _L2_attn_in['m2_Wout'], 'L2_ffn_Wqkv': _L2_ffn_in['Wqkv'], 'L2_ffn_q_scale': _L2_ffn_in['q_scale'], 'L2_ffn_k_scale': _L2_ffn_in['k_scale'], 'L2_ffn_Wo': _L2_ffn_in['Wo'], 'L2_ffn_ln_g': _L2_ffn_in['ln_g'], 'L2_ffn_ln_b': _L2_ffn_in['ln_b'], 'L2_ffn_W1': _L2_ffn_in['W1'], 'L2_ffn_b1': _L2_ffn_in['b1'], 'L2_ffn_W2': _L2_ffn_in['W2'], 'L2_ffn_b2': _L2_ffn_in['b2'], 'L3_attn_qkv_weights': _L3_attn_in['qkv_weights'], 'L3_ffn_gate_w': _L3_ffn_in['gate_w'], 'L3_ffn_w1': _L3_ffn_in['w1'], 'L3_ffn_w2': _L3_ffn_in['w2']}
    _x0 = _d['L0_attn_x']
    _d['L0_attn_x'] = jax.random.normal(jax.random.fold_in(jax.random.key(seed), 1), (4, 512, 128), dtype=_x0.dtype)
    del _x0
    return _d

def reference(L0_attn_x, L0_attn_gamma, L0_attn_Wq, L0_attn_Wkv, L0_attn_q_scale, L0_attn_k_scale, L0_attn_null_kv, L0_attn_Wout, L0_ffn_Wg, L0_ffn_bg, L0_ffn_bias, L0_ffn_W1, L0_ffn_b1, L0_ffn_W2, L0_ffn_b2, L0_ffn_Ws1, L0_ffn_bs1, L0_ffn_Ws2, L0_ffn_bs2, L1_attn_Wq, L1_attn_Wk, L1_attn_Wv, L1_attn_Wo, L1_attn_bq, L1_attn_bk, L1_attn_bv, L1_attn_bo, L1_ffn_gate_w, L1_ffn_gate_b, L1_ffn_sw1, L1_ffn_sb1, L1_ffn_sw2, L1_ffn_sb2, L1_ffn_rw1, L1_ffn_rb1, L1_ffn_rw2, L1_ffn_rb2, L2_attn_ln_g, L2_attn_ln_b, L2_attn_m1_Win, L2_attn_m1_Wconv, L2_attn_m1_bconv, L2_attn_m1_Wx, L2_attn_m1_Wdt, L2_attn_m1_bdt, L2_attn_m1_Alog, L2_attn_m1_Dp, L2_attn_m1_Wout, L2_attn_m2_Win, L2_attn_m2_Wconv, L2_attn_m2_bconv, L2_attn_m2_Wx, L2_attn_m2_Wdt, L2_attn_m2_bdt, L2_attn_m2_Alog, L2_attn_m2_Dp, L2_attn_m2_Wout, L2_ffn_Wqkv, L2_ffn_q_scale, L2_ffn_k_scale, L2_ffn_Wo, L2_ffn_ln_g, L2_ffn_ln_b, L2_ffn_W1, L2_ffn_b1, L2_ffn_W2, L2_ffn_b2, L3_attn_qkv_weights, L3_ffn_gate_w, L3_ffn_w1, L3_ffn_w2):

    def _L0_attn_ref(x, gamma, Wq, Wkv, q_scale, k_scale, null_kv, Wout):
        import jax, jax.numpy as jnp
        import numpy as np
        HEADS = 16
        DIM_HEAD = 64
        SCALE = 8.0
        NUM_NULL_KV = 2
        NON_CAUSAL_PREFIX = 64
        LN_EPS = 1e-05

        def _l2norm(t):
            n = jnp.sqrt(jnp.sum(t * t, axis=-1, keepdims=True))
            return t / jnp.maximum(n, 1e-12)

        def _layer_norm(x, gamma):
            mu = jnp.mean(x, axis=-1, keepdims=True)
            var = jnp.mean((x - mu) ** 2, axis=-1, keepdims=True)
            return (x - mu) * jax.lax.rsqrt(var + LN_EPS) * gamma
        b, n, dim = x.shape
        kv = jnp.einsum('bnd,de->bne', x, Wkv)
        k, v = (kv[..., :DIM_HEAD], kv[..., DIM_HEAD:])
        xn = _layer_norm(x, gamma)
        q = jnp.einsum('bnd,de->bne', xn, Wq)
        null_k = jnp.broadcast_to(null_kv[0], (b, NUM_NULL_KV, DIM_HEAD))
        null_v = jnp.broadcast_to(null_kv[1], (b, NUM_NULL_KV, DIM_HEAD))
        k = jnp.concatenate([null_k, k], axis=1)
        v = jnp.concatenate([null_v, v], axis=1)
        q = q.reshape(b, n, HEADS, DIM_HEAD).transpose(0, 2, 1, 3)
        q = _l2norm(q) * q_scale
        k = _l2norm(k) * k_scale
        sim = jnp.einsum('bhid,bjd->bhij', q, k) * SCALE
        i, j = (n, k.shape[1])
        rows = jnp.arange(i)[:, None]
        cols = jnp.arange(j)[None, :]
        causal_mask = cols > rows + (j - i)
        prefix_free = (rows < NON_CAUSAL_PREFIX) & (cols < NON_CAUSAL_PREFIX + (j - i))
        causal_mask = causal_mask & ~prefix_free
        neg = -jnp.finfo(sim.dtype).max
        sim = jnp.where(causal_mask, neg, sim)
        attn = jax.nn.softmax(sim, axis=-1)
        out = jnp.einsum('bhij,bjd->bhid', attn, v)
        out = out.transpose(0, 2, 1, 3).reshape(b, n, HEADS * DIM_HEAD)
        return jnp.einsum('bne,ed->bnd', out, Wout)

    def _L0_ffn_ref(x, Wg, bg, bias, W1, b1, W2, b2, Ws1, bs1, Ws2, bs2):
        import jax, jax.numpy as jnp
        import numpy as np
        B, S, D, E, TOP_K = (2, 128, 128, 8, 2)
        H = 4 * D
        b, s, d = x.shape
        xf = x.reshape(-1, d)
        T = xf.shape[0]
        scores = jax.nn.sigmoid(xf @ Wg.T + bg + bias)
        top_scores, top_idx = jax.lax.top_k(scores, TOP_K)
        weights = jnp.zeros((T, E), scores.dtype)
        weights = weights.at[jnp.arange(T)[:, None], top_idx].add(top_scores)
        h = jax.nn.gelu(jnp.einsum('td,ehd->teh', xf, W1) + b1, approximate=False)
        eo = jnp.einsum('teh,edh->ted', h, W2) + b2
        combined = jnp.einsum('ted,te->td', eo, weights)
        shared = jax.nn.gelu(xf @ Ws1.T + bs1, approximate=False) @ Ws2.T + bs2
        return (shared + combined).reshape(b, s, d)

    def _L1_attn_ref(residual, Wq, Wk, Wv, Wo, bq, bk, bv, bo):
        import jax, jax.numpy as jnp
        import numpy as np
        B, S, D, H, A = (2, 256, 128, 16, 64)
        INIT_STD = 0.02
        q = jnp.einsum('bsd,hda->bhsa', residual, Wq) + bq[None, :, None, :]
        k = jnp.einsum('bsd,hda->bhsa', residual, Wk) + bk[None, :, None, :]
        v = jnp.einsum('bsd,hda->bhsa', residual, Wv) + bv[None, :, None, :]
        scale = 1.0 / jnp.sqrt(jnp.float32(q.shape[-1]))
        scores = jnp.einsum('bhsa,bhta->bhst', q, k) * scale
        s = scores.shape[-1]
        causal = jnp.tril(jnp.ones((s, s), dtype=bool))
        masked = jnp.where(causal, scores, jnp.float32(-100000.0))
        pattern = jax.nn.softmax(masked, axis=-1)
        z = jnp.einsum('bhst,bhta->bshа'.replace('а', 'a'), pattern, v)
        out = jnp.einsum('bsha,had->bsd', z, Wo) + bo
        return out

    def _L1_ffn_ref(x, gate_w, gate_b, sw1, sb1, sw2, sb2, rw1, rb1, rw2, rb2):
        import jax, jax.numpy as jnp
        import numpy as np
        D_MODEL = 128
        FFN = 128
        N_EXPERTS = 8
        N_SHARED = 1
        TOP_K = 2
        B, S = (2, 256)

        def _swiglu(h):
            a, b = jnp.split(h, 2, axis=-1)
            return jax.nn.silu(a) * b
        hs = jnp.einsum('bsd,ndf->nbsf', x, sw1) + sb1[:, None, None, :]
        shared_out = jnp.einsum('nbsf,nfd->bsd', _swiglu(hs), sw2) + sb2.sum(0)
        probs = jax.nn.softmax(x @ gate_w + gate_b, axis=-1)
        topk_probs, topk_idx = jax.lax.top_k(probs, TOP_K)
        cw = jnp.sum(jax.nn.one_hot(topk_idx, N_EXPERTS, dtype=x.dtype) * topk_probs[..., None], axis=2)
        hr = jnp.einsum('bsd,edf->ebsf', x, rw1) + rb1[:, None, None, :]
        out_e = jnp.einsum('ebsf,efd->ebsd', _swiglu(hr), rw2) + rb2[:, None, None, :]
        routed_out = jnp.einsum('ebsd,bse->bsd', out_e, cw)
        return shared_out + routed_out

    def _L2_attn_ref(x, ln_g, ln_b, m1_Win, m1_Wconv, m1_bconv, m1_Wx, m1_Wdt, m1_bdt, m1_Alog, m1_Dp, m1_Wout, m2_Win, m2_Wconv, m2_bconv, m2_Wx, m2_Wdt, m2_bdt, m2_Alog, m2_Dp, m2_Wout):
        import jax, jax.numpy as jnp
        import numpy as np
        B, L, DIM = (8, 128, 128)
        D_MODEL = DIM // 2
        D_INNER = 2 * D_MODEL
        D_STATE = 16
        D_CONV = 4
        DT_RANK = D_MODEL // 16

        def _mamba_params(key, scale=0.02):
            ks = jax.random.split(key, 7)
            p = {'Win': jax.random.normal(ks[0], (DIM, 2 * D_INNER), jnp.float32) * scale, 'Wconv': jax.random.normal(ks[1], (D_INNER, D_CONV), jnp.float32) * scale, 'bconv': jnp.zeros((D_INNER,), jnp.float32), 'Wx': jax.random.normal(ks[2], (D_INNER, DT_RANK + 2 * D_STATE), jnp.float32) * scale, 'Wdt': jax.random.normal(ks[3], (DT_RANK, D_INNER), jnp.float32) * scale, 'bdt': jax.random.normal(ks[4], (D_INNER,), jnp.float32) * 0.1, 'Alog': jnp.log(jnp.broadcast_to(jnp.arange(1, D_STATE + 1, dtype=jnp.float32), (D_INNER, D_STATE))), 'Dp': jnp.ones((D_INNER,), jnp.float32), 'Wout': jax.random.normal(ks[5], (D_INNER, D_MODEL), jnp.float32) * scale}
            return p

        def _layernorm(x, g, b, eps=1e-05):
            mu = jnp.mean(x, axis=-1, keepdims=True)
            var = jnp.var(x, axis=-1, keepdims=True)
            return (x - mu) * jax.lax.rsqrt(var + eps) * g + b

        def _mamba(h, Win, Wconv, bconv, Wx, Wdt, bdt, Alog, Dp, Wout):
            xz = h @ Win
            x, z = jnp.split(xz, 2, axis=-1)
            xp = jnp.pad(x, ((0, 0), (D_CONV - 1, 0), (0, 0)))
            x = sum((xp[:, k:k + h.shape[1], :] * Wconv[None, None, :, k] for k in range(D_CONV))) + bconv
            x = jax.nn.silu(x)
            dbc = x @ Wx
            dt = jax.nn.softplus(dbc[..., :DT_RANK] @ Wdt + bdt)
            Bm = dbc[..., DT_RANK:DT_RANK + D_STATE]
            Cm = dbc[..., DT_RANK + D_STATE:]
            A = -jnp.exp(Alog)
            dA = jnp.exp(dt[..., None] * A)
            dBx = dt[..., None] * Bm[:, :, None, :] * x[..., None]

            def step(hc, ins):
                dA_t, dBx_t, C_t = ins
                hc = dA_t * hc + dBx_t
                y = jnp.einsum('bdn,bn->bd', hc, C_t)
                return (hc, y)
            h0 = jnp.zeros((x.shape[0], D_INNER, D_STATE), x.dtype)
            _, ys = jax.lax.scan(step, h0, (dA.transpose(1, 0, 2, 3), dBx.transpose(1, 0, 2, 3), Cm.transpose(1, 0, 2)))
            y = ys.transpose(1, 0, 2)
            y = (y + Dp * x) * jax.nn.silu(z)
            return y @ Wout
        h = _layernorm(x, ln_g, ln_b)
        fwd = _mamba(h, m1_Win, m1_Wconv, m1_bconv, m1_Wx, m1_Wdt, m1_bdt, m1_Alog, m1_Dp, m1_Wout)
        bwd = _mamba(h[:, ::-1, :], m2_Win, m2_Wconv, m2_bconv, m2_Wx, m2_Wdt, m2_bdt, m2_Alog, m2_Dp, m2_Wout)
        out = jnp.concatenate([fwd, bwd], axis=-1) + x
        return jax.nn.gelu(out, approximate=False)

    def _L2_ffn_ref(x, Wqkv, q_scale, k_scale, Wo, ln_g, ln_b, W1, b1, W2, b2):
        import jax, jax.numpy as jnp
        import numpy as np
        DIM = 128
        DEPTH = 6
        HEADS = 16
        DIM_HEAD = 64
        WINDOW = 32
        INNER = HEADS * DIM_HEAD
        DIM_INNER = int(DIM * 4 * 2 / 3)
        QK_SCALE = 8.0

        def shift_tokens(t):
            a, s = jnp.split(t, 2, -1)
            s = jnp.pad(s, ((0, 0), (1, 0), (0, 0)))[:, :-1]
            return jnp.concatenate([a, s], -1)

        def l2norm(t):
            return t / jnp.maximum(jnp.linalg.norm(t, axis=-1, keepdims=True), 1e-12)

        def rotate_half(x):
            x1, x2 = jnp.split(x, 2, -1)
            return jnp.concatenate([-x2, x1], -1)

        def rotary_tables(n):
            half = jnp.arange(0, DIM_HEAD, 2, dtype=jnp.float32)
            inv_freq = 1.0 / 10000.0 ** (half / DIM_HEAD)
            t = jnp.arange(n, dtype=jnp.float32)
            freqs = t[:, None] * inv_freq[None, :]
            freqs = jnp.concatenate([freqs, freqs], -1)
            base_scale = (half + 0.4 * DIM_HEAD) / (1.4 * DIM_HEAD)
            power = (t - n // 2) / (WINDOW // 2)
            scale = base_scale[None, :] ** power[:, None]
            scale = jnp.concatenate([scale, scale], -1)
            return (freqs, scale)

        def local_attention(q, k, v):
            b, h, n, d = q.shape
            w = WINDOW
            nw = n // w
            bq = q.reshape(b, h, nw, w, d)
            bk = k.reshape(b, h, nw, w, d)
            bv = v.reshape(b, h, nw, w, d)

            def look(t):
                p = jnp.pad(t, ((0, 0), (0, 0), (1, 0), (0, 0), (0, 0)))
                return jnp.concatenate([p[:, :, :nw], p[:, :, 1:]], axis=3)
            bk2, bv2 = (look(bk), look(bv))
            seq = jnp.arange(n).reshape(nw, w)
            seq_p = jnp.pad(seq, ((1, 0), (0, 0)), constant_values=-1)
            jt = jnp.concatenate([seq_p[:nw], seq_p[1:]], axis=1)
            it = seq[:, :, None]
            jb = jt[:, None, :]
            mask = (it < jb) | (it > jb + w) | (jb == -1)
            sim = jnp.einsum('bhwie,bhwje->bhwij', bq, bk2) * QK_SCALE
            sim = jnp.where(mask, -jnp.finfo(sim.dtype).max, sim)
            attn = jax.nn.softmax(sim, -1)
            out = jnp.einsum('bhwij,bhwje->bhwie', attn, bv2)
            return out.reshape(b, h, n, d)

        def attn_layer(x, Wqkv, qs, ksc, Wo):
            b, n, _ = x.shape
            qkv = x @ Wqkv
            q, k, v = jnp.split(qkv, 3, -1)
            sh = lambda t: t.reshape(b, n, HEADS, DIM_HEAD).transpose(0, 2, 1, 3)
            q, k, v = (sh(q), sh(k), sh(v))
            q = l2norm(q) * qs
            k = l2norm(k) * ksc
            freqs, scale = rotary_tables(n)
            cos, sin = (jnp.cos(freqs), jnp.sin(freqs))
            q = q * cos * scale + rotate_half(q) * sin * scale
            inv = 1.0 / scale
            k = k * cos * inv + rotate_half(k) * sin * inv
            out = local_attention(q, k, v)
            out = out.transpose(0, 2, 1, 3).reshape(b, n, INNER)
            return out @ Wo

        def ffn_layer(x, g, bln, W1, b1, W2, b2):
            mu = x.mean(-1, keepdims=True)
            var = ((x - mu) ** 2).mean(-1, keepdims=True)
            xn = (x - mu) / jnp.sqrt(var + 1e-05) * g + bln
            hg = xn @ W1 + b1
            a, gate = jnp.split(hg, 2, -1)
            return a * jax.nn.gelu(gate, approximate=False) @ W2 + b2
        for i in range(DEPTH):
            x = attn_layer(shift_tokens(x), Wqkv[i], q_scale[i], k_scale[i], Wo[i]) + x
            x = ffn_layer(shift_tokens(x), ln_g[i], ln_b[i], W1[i], b1[i], W2[i], b2[i]) + x
        return x

    def _L3_attn_ref(x, qkv_weights):
        import jax, jax.numpy as jnp
        import numpy as np
        NUM_HEADS = 16
        USE_MASKING = True
        NEG_INF = -1000000000.0
        B, S, D = x.shape
        H = NUM_HEADS
        Dh = D // H
        qkv = jnp.einsum('bsd,de->bse', x, qkv_weights)
        qkv = qkv.reshape(-1, 3 * D)
        pre_q = qkv[:, 0 * D:1 * D].reshape(-1, S, H, Dh)
        pre_k = qkv[:, 1 * D:2 * D].reshape(-1, S, H, Dh)
        pre_v = qkv[:, 2 * D:3 * D].reshape(-1, S, H, Dh)
        q = jnp.transpose(pre_q, (0, 2, 1, 3)).reshape(-1, S, Dh)
        v = jnp.transpose(pre_v, (0, 2, 1, 3)).reshape(-1, S, Dh)
        k = jnp.transpose(pre_k, (0, 2, 3, 1)).reshape(-1, S, Dh)
        scale = jnp.asarray(np.sqrt(Dh), dtype=x.dtype)
        a = jnp.einsum('aib,ajb->aij', q, k) / scale
        if USE_MASKING:
            tril = jnp.tril(jnp.ones((S, S), dtype=x.dtype))[None]
            a = tril * a + NEG_INF * (1.0 - tril)
        a = jax.nn.softmax(a, axis=-1)
        heads = jnp.einsum('aij,ajb->aib', a, v)
        heads = heads.reshape(-1, H, S, Dh)
        heads = jnp.transpose(heads, (0, 2, 1, 3)).reshape(-1, S, D)
        return heads

    def _L3_ffn_ref(x, gate_w, w1, w2):
        import jax, jax.numpy as jnp
        import numpy as np
        TOP_K = 2
        E = gate_w.shape[-1]
        probs = jax.nn.softmax(x @ gate_w, axis=-1)
        topw, topi = jax.lax.top_k(probs, TOP_K)
        topw = topw / topw.sum(axis=-1, keepdims=True)
        combine = (jax.nn.one_hot(topi, E, dtype=x.dtype) * topw[..., None]).sum(axis=-2)

        def body(acc, params):
            w1_i, w2_i, cw = params
            h = jax.nn.gelu(x @ w1_i, approximate=False)
            return (acc + cw[..., None] * (h @ w2_i), None)
        acc0 = jnp.zeros_like(x)
        out, _ = jax.lax.scan(body, acc0, (w1, w2, jnp.moveaxis(combine, -1, 0)))
        return out
    x = L0_attn_x
    xn = _layernorm(x, axis=-1)
    s = _L0_attn_ref(xn, L0_attn_gamma, L0_attn_Wq, L0_attn_Wkv, L0_attn_q_scale, L0_attn_k_scale, L0_attn_null_kv, L0_attn_Wout)
    g = _silu(_L0_ffn_ref(xn, L0_ffn_Wg, L0_ffn_bg, L0_ffn_bias, L0_ffn_W1, L0_ffn_b1, L0_ffn_W2, L0_ffn_b2, L0_ffn_Ws1, L0_ffn_bs1, L0_ffn_Ws2, L0_ffn_bs2))
    x = x + s * g
    xn = _layernorm(x, axis=-1)
    s = _L1_attn_ref(xn, L1_attn_Wq, L1_attn_Wk, L1_attn_Wv, L1_attn_Wo, L1_attn_bq, L1_attn_bk, L1_attn_bv, L1_attn_bo)
    g = _silu(_L1_ffn_ref(xn, L1_ffn_gate_w, L1_ffn_gate_b, L1_ffn_sw1, L1_ffn_sb1, L1_ffn_sw2, L1_ffn_sb2, L1_ffn_rw1, L1_ffn_rb1, L1_ffn_rw2, L1_ffn_rb2))
    x = x + s * g
    xn = _layernorm(x, axis=-1)
    s = _L2_attn_ref(xn, L2_attn_ln_g, L2_attn_ln_b, L2_attn_m1_Win, L2_attn_m1_Wconv, L2_attn_m1_bconv, L2_attn_m1_Wx, L2_attn_m1_Wdt, L2_attn_m1_bdt, L2_attn_m1_Alog, L2_attn_m1_Dp, L2_attn_m1_Wout, L2_attn_m2_Win, L2_attn_m2_Wconv, L2_attn_m2_bconv, L2_attn_m2_Wx, L2_attn_m2_Wdt, L2_attn_m2_bdt, L2_attn_m2_Alog, L2_attn_m2_Dp, L2_attn_m2_Wout)
    g = _silu(_L2_ffn_ref(xn, L2_ffn_Wqkv, L2_ffn_q_scale, L2_ffn_k_scale, L2_ffn_Wo, L2_ffn_ln_g, L2_ffn_ln_b, L2_ffn_W1, L2_ffn_b1, L2_ffn_W2, L2_ffn_b2))
    x = x + s * g
    xn = _layernorm(x, axis=-1)
    s = _L3_attn_ref(xn, L3_attn_qkv_weights)
    g = _silu(_L3_ffn_ref(xn, L3_ffn_gate_w, L3_ffn_w1, L3_ffn_w2))
    x = x + s * g
    return x

_drawn_inputs = setup_inputs


def setup_inputs(seed=0):
    import zlib

    import numpy as np

    out = dict(_drawn_inputs(seed))
    spreads = {'L0_attn_gamma': (1.0, 0.6),
     'L0_attn_q_scale': (1.0, 0.6),
     'L0_attn_k_scale': (1.0, 0.6),
     'L0_ffn_bg': (0.0, 0.8),
     'L0_ffn_bias': (0.0, 0.8),
     'L0_ffn_b1': (0.0, 0.8),
     'L0_ffn_b2': (0.0, 0.8),
     'L0_ffn_bs1': (0.0, 0.8),
     'L0_ffn_bs2': (0.0, 0.8),
     'L1_attn_bq': (0.0, 0.8),
     'L1_attn_bk': (0.0, 0.8),
     'L1_attn_bv': (0.0, 0.8),
     'L1_attn_bo': (0.0, 0.8),
     'L1_ffn_gate_b': (0.0, 0.8),
     'L1_ffn_sb1': (0.0, 0.8),
     'L1_ffn_sb2': (0.0, 0.8),
     'L1_ffn_rb1': (0.0, 0.8),
     'L1_ffn_rb2': (0.0, 0.8),
     'L2_attn_ln_g': (1.0, 0.6),
     'L2_attn_ln_b': (0.0, 0.8),
     'L2_attn_m1_bconv': (0.0, 0.8),
     'L2_attn_m1_Dp': (1.0, 0.6),
     'L2_attn_m2_bconv': (0.0, 0.8),
     'L2_attn_m2_Dp': (1.0, 0.6),
     'L2_ffn_q_scale': (1.0, 0.6),
     'L2_ffn_k_scale': (1.0, 0.6),
     'L2_ffn_ln_g': (1.0, 0.6),
     'L2_ffn_ln_b': (0.0, 0.8),
     'L2_ffn_b1': (0.0, 0.8),
     'L2_ffn_b2': (0.0, 0.1)}
    factors = {'L0_attn_Wq': 5.272,
     'L0_attn_Wkv': 4.713,
     'L0_attn_null_kv': 8.0,
     'L0_attn_Wout': 4.669,
     'L0_ffn_Wg': 8.0,
     'L0_ffn_W1': 8.0,
     'L0_ffn_W2': 8.0,
     'L0_ffn_Ws1': 8.0,
     'L0_ffn_Ws2': 8.0,
     'L1_attn_Wq': 8.0,
     'L1_attn_Wk': 8.0,
     'L1_attn_Wv': 8.0,
     'L1_attn_Wo': 8.0,
     'L1_ffn_gate_w': 8.0,
     'L1_ffn_sw1': 8.0,
     'L1_ffn_sw2': 8.0,
     'L1_ffn_rw1': 8.0,
     'L1_ffn_rw2': 8.0,
     'L2_attn_m1_Win': 8.0,
     'L2_attn_m1_Wconv': 8.0,
     'L2_attn_m1_Wx': 8.0,
     'L2_attn_m1_bdt': 8.0,
     'L2_attn_m1_Alog': 8.0,
     'L2_attn_m1_Wout': 8.0,
     'L2_attn_m2_Win': 8.0,
     'L2_attn_m2_Wconv': 8.0,
     'L2_attn_m2_Wx': 8.0,
     'L2_attn_m2_Wdt': 8.0,
     'L2_attn_m2_bdt': 8.0,
     'L2_attn_m2_Alog': 8.0,
     'L2_attn_m2_Wout': 8.0,
     'L2_ffn_W1': 4.993,
     'L2_ffn_W2': 4.919,
     'L3_attn_qkv_weights': 8.0,
     'L3_ffn_gate_w': 8.0,
     'L3_ffn_w1': 8.0,
     'L3_ffn_w2': 8.0}
    for name, (base, spread) in spreads.items():
        noise = np.random.default_rng([zlib.crc32(name.encode()), seed]).standard_normal(out[name].shape)
        drawn = base * np.exp(spread * noise) if base else spread * noise
        out[name] = jnp.asarray(drawn.astype(out[name].dtype))
    for name, factor in factors.items():
        out[name] = (out[name] * factor).astype(out[name].dtype)
    return out
```

```python
import numpy as np

import concourse.bass as bass
from concourse import mybir
from contextlib import ExitStack

ALU = mybir.AluOpType
ACT = mybir.ActivationFunctionType
F32 = mybir.dt.float32
BF16 = mybir.dt.bfloat16
U32 = mybir.dt.uint32
AX_X = mybir.AxisListType.X

P = 128
BATCH, SEQ, D = 4, 512, 128
TILES = SEQ // P
NT = BATCH * TILES
HEADS, DH = 16, 64
PAIRS = HEADS // 2
LN_EPS = 1e-5
EXPERTS = 8
STEPS = HEADS * TILES
CREDIT = 4


def head_tile(n):
    return n // TILES, n % TILES


class Ctx:
    pass


def scope(nc, stack, tag):
    made = []

    def end():
        nc.clear_and_free_semaphores(made)
        nc.all_engine_barrier()

    stack.callback(end)

    def sb(name, shape, dt=F32):
        return stack.enter_context(nc.sbuf_tensor(f"{tag}_{name}", shape, dt))

    def once(name):
        made.append(nc.alloc_semaphore(f"{tag}_{name}"))
        return made[-1]

    def counted(name):
        counted.made.append(once(name))
        return counted.made[-1]

    counted.made = []
    return sb, once, counted


def start_counts(eng, counted):
    for s in counted.made:
        eng.sem_inc(s, CREDIT)


class Chain:

    def __init__(self, eng, semaphore):
        self.eng, self.sem, self.n = eng, semaphore, 0

    def done(self, ins):
        self.n += 1
        ins.then_inc(self.sem, 1)

    def join(self):
        self.eng.wait_ge(self.sem, self.n)

    def restart(self):
        self.join()
        self.eng.sem_clear(self.sem)
        self.n = 0


def load_stage(g):
    nc = g.nc
    with ExitStack() as stack:
        sb, sem, _ = scope(nc, stack, "load")
        landed = sem("landed")
        block = stack.enter_context(nc.Block())

        @block.sync
        def _(sp):
            sp.dma_start(g.x[:], g.x_in.rearrange("b (t p) d -> p (b t) d", p=P)).then_inc(landed, 16)
            sp.dma_start(g.ident[:], g.c["ident"]).then_inc(landed, 16)
            sp.dma_start(g.maskf[:], g.c["masks"]).then_inc(landed, 16)
            sp.wait_ge(landed, 48)

        @block.vector
        def _(dve):
            dve.memset(g.neghalf[:], -0.5)
            dve.wait_ge(landed, 48)
            nc.vector.tensor_copy(g.identb[:], g.ident[:])
            nc.vector.tensor_copy(g.maskb[:], g.maskf[:])


def norm_stage(g, tag):
    nc = g.nc
    with ExitStack() as stack:
        sb, sem, _ = scope(nc, stack, tag)
        stats = sb("stats", [P, NT, 6])
        mv = sb("mv", [P, NT, 2])
        rstd = sb("rstd", [P, NT])
        stats_done = sem("stats_done")
        mean_done = sem("mean_done")
        var_ready = sem("var_ready")
        rstd_ready = sem("rstd_ready")
        xn_ready = sem("xn_ready")
        turned = sem("turned")
        copied = sem("copied")
        block = stack.enter_context(nc.Block())

        @block.vector
        def _(dve):
            for n in range(NT):
                nc.vector.bn_stats(stats[:, n], g.x[:, n]).then_inc(stats_done, 1)
            for n in range(NT):
                dve.wait_ge(stats_done, n + 1)
                nc.vector.bn_aggr(mv[:, n], stats[:, n]).then_inc(mean_done, 1)
            dve.wait_ge(mean_done, NT)
            nc.vector.tensor_scalar(mv[:, :, 1], mv[:, :, 1], LN_EPS, None, ALU.add).then_inc(var_ready, 1)
            dve.wait_ge(rstd_ready, 1)
            for n in range(NT):
                nc.vector.tensor_scalar(g.xn[:, n], g.x[:, n], mv[:, n, 0:1], rstd[:, n:n + 1],
                                        ALU.subtract, ALU.mult).then_inc(xn_ready, 1)

        @block.gpsimd
        def _(pool):
            pool.wait_ge(var_ready, 1)
            nc.gpsimd.tensor_tensor(rstd[:], mv[:, :, 1], g.neghalf[:, 0:NT], ALU.pow).then_inc(rstd_ready, 1)

        @block.tensor
        def _(pe):
            for b in range(BATCH):
                if b >= 2:
                    pe.wait_ge(copied, b - 1)
                for t in range(TILES):
                    n = b * TILES + t
                    pe.wait_ge(xn_ready, n + 1)
                    ins = nc.tensor.transpose(g.ps[:, b % 2, t * P:(t + 1) * P], g.xn[:, n], g.ident[:])
                ins.then_inc(turned, 1)

        @block.scalar
        def _(act):
            for b in range(BATCH):
                act.wait_ge(turned, b + 1)
                nc.scalar.copy(g.xnT[:, b * SEQ:(b + 1) * SEQ], g.ps[:, b % 2]).then_inc(copied, 1)


class Softmax:

    def __init__(self, g, sb, sem, q, k, v, o, width, nulls=None, v_null=None):
        self.g, self.nc = g, g.nc
        self.q, self.k, self.v, self.o, self.width = q, k, v, o, width
        self.nulls, self.v_null = nulls, v_null
        self.extra = 0 if nulls is None else 2
        self.p = sb("p", [P, 2, SEQ + self.extra])
        self.pT = sb("pT", [P, 2, SEQ])
        self.pTn = sb("pTn", [2, 2, P]) if self.extra else None
        self.negmax = sb("negmax", [P, STEPS])
        self.rowsum = sb("rowsum", [P, STEPS])
        self.rinv = sb("rinv", [P, STEPS])
        self.scores_ready = sem("scores_ready")
        self.negmax_ready = sem("negmax_ready")
        self.probs_ready = sem("probs_ready")
        self.turned = sem("turned")
        self.copied_dve = sem("copied_dve")
        self.copied_act = sem("copied_act")
        self.null_copied = sem("null_copied")
        self.pv_done = sem("pv_done")
        self.rinv_ready = sem("rinv_ready")
        self.o_ready = sem("o_ready")

    def copied(self, b, n):
        h, t = head_tile(n)
        if t < 2:
            return self.copied_dve, CREDIT + b * 2 * HEADS + 2 * h + t + 1
        return self.copied_act, CREDIT + b * 2 * HEADS + 2 * h + t - 1

    def pe_scores(self, pe, b, n):
        nc, g = self.nc, self.g
        h, t = head_tile(n)
        keys = (t + 1) * P
        s = g.ps[:, 2 * (n % 2):2 * (n % 2) + 2].rearrange("p a c -> p (a c)")
        pe.wait_ge(self.probs_ready, CREDIT + b * STEPS + n - 1)
        if self.extra:
            pe.wait_ge(self.null_copied, CREDIT + b * STEPS + n - 1)
        nc.tensor.matmul(s[:, 0:keys], self.q(h, t), self.k(h, keys), start=True, stop=False)
        ins = nc.tensor.matmul(s[:, keys - P:keys], g.identb[:],
                               g.maskb[:, 1 if (self.extra and t == 0) else 0], start=False, stop=True)
        if self.extra:
            ins = nc.tensor.matmul(s[:, keys:keys + 2], self.q(h, t), self.nulls(h), start=True, stop=True)
        ins.then_inc(self.scores_ready, 1)

    def pe_turn(self, pe, b, n):
        nc, g = self.nc, self.g
        h, t = head_tile(n)
        pe.wait_ge(self.probs_ready, CREDIT + b * STEPS + n + 1)
        if n >= 2:
            pe.wait_ge(*self.copied(b, n - 2))
        for c in range(t + 1):
            ins = nc.tensor.transpose(g.ps[:, 4 + n % 2, c * P:(c + 1) * P],
                                      self.p[:, n % 2, c * P:(c + 1) * P], g.ident[:])
        if self.extra:
            ins = nc.tensor.transpose(g.ps[0:2, 2 * (n % 2) + 1, 256:256 + P],
                                      self.p[:, n % 2, (t + 1) * P:(t + 1) * P + 2], g.ident[:])
        ins.then_inc(self.turned, 1)

    def pe_pv(self, pe, b, n):
        nc, g = self.nc, self.g
        h, t = head_tile(n)
        pe.wait_ge(*self.copied(b, n))
        if self.extra:
            pe.wait_ge(self.null_copied, CREDIT + b * STEPS + n + 1)
        if t == 0:
            pe.wait_ge(self.o_ready, CREDIT + b * HEADS + h - 1)
        out = g.ps[:, 6 + h % 2, t * self.width:(t + 1) * self.width]
        for c in range(t + 1):
            ins = nc.tensor.matmul(out, self.pT[:, n % 2, c * P:(c + 1) * P], self.v(h, c),
                                   start=(c == 0), stop=(c == t and not self.extra))
        if self.extra:
            ins = nc.tensor.matmul(out, self.pTn[:, n % 2], self.v_null(h), start=False, stop=True)
        ins.then_inc(self.pv_done, 1)

    def tensor(self, pe, b):
        self.pe_scores(pe, b, 0)
        for n in range(STEPS):
            if n + 1 < STEPS:
                self.pe_scores(pe, b, n + 1)
            self.pe_turn(pe, b, n)
            if n >= 1:
                self.pe_pv(pe, b, n - 1)
        self.pe_pv(pe, b, STEPS - 1)

    def copy_turned(self, eng, copy, b, n, signal):
        t = n % TILES
        eng.wait_ge(self.turned, CREDIT + b * STEPS + n + 1)
        eng.wait_ge(self.pv_done, CREDIT + b * STEPS + n - 1)
        copy(self.pT[:, n % 2, 0:(t + 1) * P], self.g.ps[:, 4 + n % 2, 0:(t + 1) * P]).then_inc(signal, 1)

    def dve_out(self, dve, b, h):
        nc, g = self.nc, self.g
        cols = slice(h * TILES, (h + 1) * TILES)
        dve.wait_ge(self.probs_ready, CREDIT + b * STEPS + (h + 1) * TILES)
        nc.vector.reciprocal(self.rinv[:, cols], self.rowsum[:, cols]).then_inc(self.rinv_ready, 1)
        dve.wait_ge(self.pv_done, CREDIT + b * STEPS + (h + 1) * TILES)
        dve.wait_ge(self.rinv_ready, CREDIT + b * HEADS + h + 1)
        ps = g.ps[:, 6 + h % 2, 0:TILES * self.width].rearrange("p (t w) -> p t w", t=TILES)
        nc.vector.tensor_tensor(self.o(h), ps, self.rinv[:, cols].unsqueeze(2).broadcast_to([P, TILES, self.width]),
                                ALU.mult).then_inc(self.o_ready, 1)

    def vector(self, dve, b):
        nc, g = self.nc, self.g
        for n in range(STEPS + 2):
            if n < STEPS:
                t = n % TILES
                s = g.ps[:, 2 * (n % 2):2 * (n % 2) + 2].rearrange("p a c -> p (a c)")
                dve.wait_ge(self.scores_ready, CREDIT + b * STEPS + n + 1)
                nc.vector.tensor_reduce(self.negmax[:, n:n + 1], s[:, 0:(t + 1) * P + self.extra], AX_X, ALU.max,
                                        negate=True).then_inc(self.negmax_ready, 1)
            if 1 <= n <= STEPS and (n - 1) % TILES < 2:
                self.copy_turned(dve, nc.vector.tensor_copy, b, n - 1, self.copied_dve)
            if n >= TILES and n % TILES == 1:
                self.dve_out(dve, b, n // TILES - 1)

    def scalar(self, act, b):
        nc, g = self.nc, self.g
        for n in range(STEPS + 1):
            if n < STEPS:
                t = n % TILES
                keys = (t + 1) * P + self.extra
                s = g.ps[:, 2 * (n % 2):2 * (n % 2) + 2].rearrange("p a c -> p (a c)")
                act.wait_ge(self.negmax_ready, CREDIT + b * STEPS + n + 1)
                if n >= 2:
                    act.wait_ge(self.turned, CREDIT + b * STEPS + n - 1)
                nc.scalar.activation(self.p[:, n % 2, 0:keys], s[:, 0:keys], ACT.Exp,
                                     bias=self.negmax[:, n:n + 1],
                                     accum_out=self.rowsum[:, n:n + 1]).then_inc(self.probs_ready, 1)
            if n >= 1:
                if self.extra:
                    act.wait_ge(self.turned, CREDIT + b * STEPS + n)
                    act.wait_ge(self.pv_done, CREDIT + b * STEPS + n - 2)
                    nc.scalar.copy(self.pTn[:, (n - 1) % 2],
                                   g.ps[0:2, 2 * ((n - 1) % 2) + 1, 256:256 + P]).then_inc(self.null_copied, 1)
                if (n - 1) % TILES >= 2:
                    self.copy_turned(act, nc.scalar.copy, b, n - 1, self.copied_act)


class OutProduct:

    def __init__(self, g, sb, sem, o, wo):
        self.g, self.nc, self.o, self.wo = g, g.nc, o, wo
        self.oT = sb("oT", [P, PAIRS, P])
        self.oT_turned = sem("oT_turned")
        self.oT_copied = sem("oT_copied")
        self.s_ready = sem("s_ready")
        self.s_copied = sem("s_copied") 

    def tensor(self, pe, b, wo=None):
        nc, g = self.nc, self.g
        wo = wo or (lambda c: self.wo[:, c])
        for t in range(TILES):
            pe.wait_ge(self.oT_copied, CREDIT + b * 2 * TILES + 2 * t)
            for c in range(PAIRS):
                ins = nc.tensor.transpose(g.ps[:, 4 + c // 4, (c % 4) * P:(c % 4 + 1) * P],
                                          self.o[:, t, c * P:(c + 1) * P], g.ident[:])
                if c % 4 == 3:
                    ins.then_inc(self.oT_turned, 1)
            pe.wait_ge(self.oT_copied, CREDIT + b * 2 * TILES + 2 * t + 2)
            pe.wait_ge(self.s_copied, CREDIT + b * TILES + t - 1)
            for c in range(PAIRS):
                ins = nc.tensor.matmul(g.ps[:, t % 2, 0:D], self.oT[:, c], wo(c),
                                       start=(c == 0), stop=(c == PAIRS - 1))
            ins.then_inc(self.s_ready, 1)
        pe.wait_ge(self.s_copied, CREDIT + (b + 1) * TILES )

    def scalar(self, act, b):
        for i in range(2 * TILES):
            act.wait_ge(self.oT_turned, CREDIT + b * 2 * TILES + i + 1)
            act.wait_ge(self.s_ready, CREDIT + b * TILES + i // 2)
            self.nc.scalar.copy(self.oT[:, 4 * (i % 2):4 * (i % 2) + 4].rearrange("p c n -> p (c n)"),
                                self.g.ps[:, 4 + i % 2]).then_inc(self.oT_copied, 1)


def l0_attn_stage(g):
    nc = g.nc
    HD = HEADS * DH
    SCALE = 8.0
    with ExitStack() as stack:
        sb, once, sem = scope(nc, stack, "l0a")
        wq = sb("wq", [P, HD])
        wkv = sb("wkv", [P, 2 * DH])
        wo = sb("wo", [P, PAIRS, D])
        gamma = sb("gamma", [P, 1])
        qks = sb("qks", [P, 3])
        nk = sb("nk", [2, 2, DH])
        nsq = sb("nsq", [2, DH])
        nss = sb("nss", [2, 1])
        nrk = sb("nrk", [2, 1])
        nkT = sb("nkT", [P, 2])
        v_null = sb("v_null", [2, DH])
        stats = sb("stats", [P, NT, 6])
        mv = sb("mv", [P, NT, 2])
        rstd = sb("rstd", [P, NT])
        xg = g.gate
        xgT = sb("xgT", [P, NT, D])
        xb = sb("xb", [P, SEQ])
        qb = sb("qb", [P, SEQ])
        kraw = sb("kraw", [P, TILES, DH])
        ksq = sb("ksq", [P, TILES, DH])
        kd = sb("kd", [P, TILES, 2, DH])
        kT = sb("kT", [P, SEQ])
        v = sb("v", [P, TILES, DH])
        sq = sb("sq", [P, 2, 512])
        qn = sb("qn", [P, 2, HD])
        ss = sb("ss", [P, TILES + 1, HEADS])
        rn = sb("rn", [P, TILES + 1, HEADS])
        qT = sb("qT", [P, PAIRS, SEQ])
        o = sb("o", [P, TILES, HD])
        loaded = once("loaded")
        dve_step = once("dve_step")
        pre = once("pre")
        nss_ready = once("nss_ready")
        nrk_ready = once("nrk_ready")
        nk_turned = once("nk_turned")
        nkT_ready = once("nkT_ready")
        var_ready = once("var_ready")
        rstd_ready = once("rstd_ready")
        xg_ready = once("xg_ready")
        xg_turned = once("xg_turned")
        xgT_ready = once("xgT_ready")
        xb_ready = sem("xb_ready")
        kv_ready = sem("kv_ready")
        ss_ready = sem("ss_ready")
        rn_ready = sem("rn_ready")
        kd_ready = sem("kd_ready")
        k_turned = sem("k_turned")
        kT_ready = sem("kT_ready")
        q_ready = sem("q_ready")
        sq_ready = sem("sq_ready")
        sq_summed = sem("sq_summed")
        q_normed = sem("q_normed")
        q_turned = sem("q_turned")
        q_copied = sem("q_copied")
        op = OutProduct(g, sb, sem, o, wo)
        at = Softmax(g, sb, sem,
                     q=lambda h, t: qT[64 * (h % 2):64 * (h % 2) + 64, h // 2, t * P:(t + 1) * P],
                     k=lambda h, n: kT[64 * (h % 2):64 * (h % 2) + 64, 0:n],
                     v=lambda h, c: v[:, c], o=lambda h: o[:, :, h * DH:(h + 1) * DH], width=DH,
                     nulls=lambda h: nkT[64 * (h % 2):64 * (h % 2) + 64, :], v_null=lambda h: v_null[:])
        block = stack.enter_context(nc.Block())
        LOADED = 16 * 11
        Q = 2 * TILES

        @block.sync
        def _(sp):
            start_counts(sp, sem)
            w = g.w
            for dst, src in ((nk[:, 0], w["L0_attn_null_kv"][0]), (nk[:, 1], w["L0_attn_null_kv"][0]),
                             (v_null[:], w["L0_attn_null_kv"][1]), (gamma[:], w["L0_attn_gamma"]),
                             (wkv[:], w["L0_attn_Wkv"]), (wq[:], w["L0_attn_Wq"]), (wo[:], w["L0_attn_Wout"])):
                sp.dma_start(dst, src).then_inc(loaded, 16)
            for i, n in enumerate(("L0_attn_q_scale", "L0_attn_k_scale")):
                for half in range(2):
                    sp.dma_start(qks[half * DH:half * DH + DH, i:i + 1], w[n]).then_inc(loaded, 16)

        @block.vector
        def _(dve):
            ch = Chain(dve, pre)
            for n in range(NT):
                ch.done(nc.vector.bn_stats(stats[:, n], g.xn[:, n]))
            ch.join()
            for n in range(NT):
                ch.done(nc.vector.bn_aggr(mv[:, n], stats[:, n]))
            ch.join()
            nc.vector.tensor_scalar(mv[:, :, 1], mv[:, :, 1], LN_EPS, None, ALU.add).then_inc(var_ready, 1)
            dve.wait_ge(loaded, LOADED)
            ch.done(nc.vector.tensor_tensor(nsq[:], nk[:, 0], nk[:, 0], ALU.mult))
            ch.done(nc.vector.tensor_scalar(qks[:, 2:3], qks[:, 0:1], qks[:, 1:2], SCALE, ALU.mult, ALU.mult))
            ch.join()
            ch.done(nc.vector.tensor_reduce(nss[:], nsq[:], AX_X, ALU.add))
            ch.join()
            nc.vector.tensor_scalar(nss[:], nss[:], 1e-24, None, ALU.max).then_inc(nss_ready, 1)
            dve.wait_ge(nrk_ready, 1)
            ch.done(nc.vector.tensor_scalar(nk[:], nk[:], nrk[:], None, ALU.mult))
            dve.wait_ge(rstd_ready, 1)
            for n in range(NT):
                nc.vector.tensor_scalar(xg[:, n], g.xn[:, n], mv[:, n, 0:1], rstd[:, n:n + 1],
                                        ALU.subtract, ALU.mult).then_inc(xg_ready, 1)
            dve.wait_ge(nk_turned, 1)
            nc.vector.tensor_scalar(nkT[:], g.ps[:, 7, 0:2], qks[:, 2:3], None, ALU.mult).then_inc(nkT_ready, 1)
            assert ch.n == NK_STEPS, ch.n
            with dve.Fori(0, BATCH) as b:
                ch = Chain(dve, dve_step)
                dve.sem_clear(dve_step)
                dve.wait_ge(kv_ready, CREDIT + b + 1)
                kv = g.ps[:, 6].rearrange("p (t c) -> p t c", t=TILES)
                ch.done(nc.vector.tensor_copy(kraw[:], kv[:, :, 0:DH]))
                ch.done(nc.vector.tensor_copy(v[:], kv[:, :, DH:2 * DH]))
                ch.join()
                ch.done(nc.vector.tensor_tensor(ksq[:], kraw[:], kraw[:], ALU.mult))
                ch.join()
                ch.done(nc.vector.tensor_reduce(ss[:, 0, 0:TILES], ksq[:], AX_X, ALU.add))
                ch.join()
                nc.vector.tensor_scalar(ss[:, 0, 0:TILES], ss[:, 0, 0:TILES], 1e-24, None, ALU.max).then_inc(ss_ready, 1)

                def sum_squares(t):
                    for i in (2 * t, 2 * t + 1):
                        dve.wait_ge(sq_ready, CREDIT + b * Q + i + 1)
                        nc.vector.tensor_reduce(ss[:, 1 + t, 8 * (i % 2):8 * (i % 2) + 8],
                                                sq[:, i % 2].rearrange("p (h d) -> p h d", d=DH), AX_X,
                                                ALU.add).then_inc(sq_summed, 1)
                    dve.wait_ge(sq_summed, CREDIT + b * Q + 2 * t + 2)
                    nc.vector.tensor_scalar(ss[:, 1 + t], ss[:, 1 + t], 1e-24, None, ALU.max).then_inc(ss_ready, 1)

                def normalize(t):
                    dve.wait_ge(rn_ready, CREDIT + b * (TILES + 1) + t + 2)
                    dve.wait_ge(q_turned, CREDIT + b * Q + 2 * t - 2)
                    for i in (2 * t, 2 * t + 1):
                        hs = slice(8 * (i % 2), 8 * (i % 2) + 8)
                        nc.vector.tensor_tensor(
                            qn[:, t % 2, 512 * (i % 2):512 * (i % 2) + 512].rearrange("p (h d) -> p h d", d=DH),
                            g.ps[:, i % 4].rearrange("p (h d) -> p h d", d=DH),
                            rn[:, 1 + t, hs].unsqueeze(2).broadcast_to([P, 8, DH]), ALU.mult).then_inc(q_normed, 1)

                sum_squares(0)
                dve.wait_ge(rn_ready, CREDIT + b * (TILES + 1) + 1)
                for half in range(2):
                    nc.vector.tensor_tensor(kd[:, :, half], kraw[:],
                                            rn[:, 0, 0:TILES].unsqueeze(2).broadcast_to([P, TILES, DH]),
                                            ALU.mult).then_inc(kd_ready, 1)
                for t in range(TILES):
                    if t + 1 < TILES:
                        sum_squares(t + 1)
                    normalize(t)
                at.vector(dve, b)
                for t in range(TILES):
                    dve.wait_ge(op.s_ready, CREDIT + b * TILES + t + 1)
                    nc.vector.tensor_copy(g.s[:, bass.ds(b * TILES + t, 1), :].rearrange("p a d -> p (a d)"),
                                          g.ps[:, t % 2, 0:D]).then_inc(op.s_copied, 1)
                ch.join()

        @block.gpsimd
        def _(pool):
            pool.wait_ge(var_ready, 1)
            nc.gpsimd.tensor_tensor(rstd[:], mv[:, :, 1], g.neghalf[:, 0:NT], ALU.pow).then_inc(rstd_ready, 1)
            pool.wait_ge(nss_ready, 1)
            nc.gpsimd.tensor_tensor(nrk[:], nss[:], g.neghalf[0:2, 0:1], ALU.pow).then_inc(nrk_ready, 1)
            pool.wait_ge(xgT_ready, BATCH)
            with pool.Fori(0, BATCH) as b:
                pool.wait_ge(q_ready, CREDIT + b * Q)
                nc.gpsimd.tensor_copy(xb[:], g.xnT[:, bass.ds(b * SEQ, SEQ)]).then_inc(xb_ready, 1)
                nc.gpsimd.tensor_copy(qb[:], xgT[:].rearrange("p t d -> p (t d)")[:, bass.ds(b * SEQ, SEQ)])\
                    .then_inc(xb_ready, 1)
                for j in range(TILES + 1):
                    n = TILES if j == 0 else HEADS
                    pool.wait_ge(ss_ready, CREDIT + b * (TILES + 1) + j + 1)
                    nc.gpsimd.tensor_tensor(rn[:, j, 0:n], ss[:, j, 0:n], g.neghalf[:, 0:n], ALU.pow).then_inc(rn_ready, 1)

        @block.tensor
        def _(pe):
            pe.wait_ge(loaded, LOADED)
            pe.wait_ge(pre, NK_STEPS)
            nc.tensor.transpose(g.ps[:, 7, 0:2], nk[:].rearrange("k a d -> k (a d)"), g.ident[0:2, 0:2]).then_inc(nk_turned, 1)
            for b in range(BATCH):
                if b >= 2:
                    pe.wait_ge(xgT_ready, b - 1)
                pe.wait_ge(xg_ready, (b + 1) * TILES)
                for t in range(TILES):
                    ins = nc.tensor.transpose(g.ps[:, b % 2, t * P:(t + 1) * P], xg[:, b * TILES + t], g.ident[:])
                ins.then_inc(xg_turned, 1)
            pe.wait_ge(xgT_ready, BATCH)
            pe.wait_ge(nkT_ready, 1)

            def query_product(b, t):
                for i in (2 * t, 2 * t + 1):
                    pe.wait_ge(q_normed, CREDIT + b * Q + i - 3)
                    nc.tensor.matmul(g.ps[:, i % 4], qb[:, t * P:(t + 1) * P], wq[:, 512 * (i % 2):512 * (i % 2) + 512],
                                     start=True, stop=True).then_inc(q_ready, 1)

            with pe.Fori(0, BATCH) as b:
                pe.wait_ge(xb_ready, CREDIT + 2 * b + 2)
                for t in range(TILES):
                    ins = nc.tensor.matmul(g.ps[:, 6, t * P:(t + 1) * P], xb[:, t * P:(t + 1) * P], wkv[:],
                                           start=True, stop=True)
                ins.then_inc(kv_ready, 1)
                query_product(b, 0)
                query_product(b, 1)
                pe.wait_ge(kd_ready, CREDIT + 2 * b + 2)
                for t in range(TILES):
                    ins = nc.tensor.transpose(g.ps[:, 7, t * P:(t + 1) * P], kd[:, t].rearrange("p a d -> p (a d)"), g.ident[:])
                ins.then_inc(k_turned, 1)
                for t in range(TILES):
                    for half in range(2):
                        i = 2 * t + half
                        pe.wait_ge(q_normed, CREDIT + b * Q + i + 1)
                        pe.wait_ge(q_copied, CREDIT + b * Q + i - 1)
                        for c in range(4):
                            ins = nc.tensor.transpose(g.ps[:, 4 + half, c * P:(c + 1) * P],
                                                      qn[:, t % 2, (4 * half + c) * P:(4 * half + c + 1) * P], g.ident[:])
                        ins.then_inc(q_turned, 1)
                    if t + 2 < TILES:
                        query_product(b, t + 2)
                pe.wait_ge(q_copied, CREDIT + b * Q + Q)
                pe.wait_ge(kT_ready, CREDIT + b + 1)
                at.tensor(pe, b)
                pe.wait_ge(at.o_ready, CREDIT + (b + 1) * HEADS)
                op.tensor(pe, b)

        @block.scalar
        def _(act):
            act.wait_ge(loaded, LOADED)
            for b in range(BATCH):
                act.wait_ge(xg_turned, b + 1)
                nc.scalar.activation(xgT[:].rearrange("p t d -> p (t d)")[:, b * SEQ:(b + 1) * SEQ], g.ps[:, b % 2],
                                     ACT.Copy, scale=gamma[:]).then_inc(xgT_ready, 1)
            with act.Fori(0, BATCH) as b:
                def copy_queries(t):
                    for half in range(2):
                        act.wait_ge(q_turned, CREDIT + b * Q + 2 * t + half + 1)
                        nc.scalar.copy(qT[:, 4 * half:4 * half + 4, t * P:(t + 1) * P],
                                       g.ps[:, 4 + half].rearrange("p (c n) -> p c n", c=4)).then_inc(q_copied, 1)

                for t in range(TILES):
                    for i in (2 * t, 2 * t + 1):
                        act.wait_ge(q_ready, CREDIT + b * Q + i + 1)
                        act.wait_ge(sq_summed, CREDIT + b * Q + i - 1)
                        nc.scalar.activation(sq[:, i % 2], g.ps[:, i % 4], ACT.Square).then_inc(sq_ready, 1)
                    if t == 1:
                        act.wait_ge(k_turned, CREDIT + b + 1)
                        nc.scalar.activation(kT[:], g.ps[:, 7], ACT.Copy, scale=qks[:, 2:3]).then_inc(kT_ready, 1)
                    if t >= 1:
                        copy_queries(t - 1)
                copy_queries(TILES - 1)
                at.scalar(act, b)
                op.scalar(act, b)


NK_STEPS = 2 * NT + 4


def l1_attn_stage(g):
    nc = g.nc
    HD = HEADS * DH
    with ExitStack() as stack:
        sb, once, sem = scope(nc, stack, "l1a")
        wq, wk, wv = (sb(n, [P, HD]) for n in ("wq", "wk", "wv"))
        wo = sb("wo", [P, PAIRS, D])
        bq, bk = (sb(n, [P, PAIRS]) for n in ("bq", "bk"))
        bv = sb("bv", [P, HD])
        bo = sb("bo", [P, D])
        xb = sb("xb", [P, SEQ])
        qT = sb("qT", [P, PAIRS, SEQ])
        kT = sb("kT", [P, PAIRS, SEQ])
        v = sb("v", [P, TILES, HD])
        o = sb("o", [P, TILES, HD])
        loaded = once("loaded")
        bq_scaled = once("bq_scaled")
        xb_ready = sem("xb_ready")
        proj_ready = sem("proj_ready")
        proj_copied = sem("proj_copied")
        v_ready = sem("v_ready")
        v_copied = sem("v_copied")
        op = OutProduct(g, sb, sem, o, wo)
        at = Softmax(g, sb, sem,
                     q=lambda h, t: qT[64 * (h % 2):64 * (h % 2) + 64, h // 2, t * P:(t + 1) * P],
                     k=lambda h, n: kT[64 * (h % 2):64 * (h % 2) + 64, h // 2, 0:n],
                     v=lambda h, c: v[:, c, h * DH:(h + 1) * DH],
                     o=lambda h: o[:, :, h * DH:(h + 1) * DH], width=DH)
        block = stack.enter_context(nc.Block())

        @block.sync
        def _(sp):
            start_counts(sp, sem)
            for dst, src in ((wq, "L1_attn_Wq"), (wk, "L1_attn_Wk"), (wv, "L1_attn_Wv"), (wo, "L1_attn_Wo"),
                             (bq, "L1_attn_bq"), (bk, "L1_attn_bk")):
                sp.dma_start(dst[:], g.w[src]).then_inc(loaded, 16)
            sp.dma_start(bv[:], g.w["L1_attn_bv"].partition_broadcast(P)).then_inc(loaded, 16)
            sp.dma_start(bo[:], g.w["L1_attn_bo"].partition_broadcast(P)).then_inc(loaded, 16)

        LOADED = 16 * 8

        @block.gpsimd
        def _(pool):
            with pool.Fori(0, BATCH) as b:
                pool.wait_ge(v_ready, CREDIT + b * 2 * TILES)
                nc.gpsimd.tensor_copy(xb[:], g.xnT[:, bass.ds(b * SEQ, SEQ)]).then_inc(xb_ready, 1)

        @block.tensor
        def _(pe):
            pe.wait_ge(loaded, LOADED)
            with pe.Fori(0, BATCH) as b:
                pe.wait_ge(xb_ready, CREDIT + b + 1)
                for i in range(2 * PAIRS):
                    w, c = (wq, wk)[i % 2], i // 2
                    pe.wait_ge(proj_copied, CREDIT + b * 2 * PAIRS + i - 1)
                    nc.tensor.matmul(g.ps[:, i % 2], w[:, c * P:(c + 1) * P], xb[:],
                                     start=True, stop=True).then_inc(proj_ready, 1)
                for i in range(2 * TILES):
                    t, half = i // 2, i % 2
                    pe.wait_ge(v_copied, CREDIT + b * 2 * TILES + i - 1)
                    nc.tensor.matmul(g.ps[:, 2 + i % 2], xb[:, t * P:(t + 1) * P], wv[:, half * 512:half * 512 + 512],
                                     start=True, stop=True).then_inc(v_ready, 1)
                pe.wait_ge(proj_copied, CREDIT + (b + 1) * 2 * PAIRS )
                pe.wait_ge(v_copied, CREDIT + (b + 1) * 2 * TILES)
                at.tensor(pe, b)
                pe.wait_ge(at.o_ready, CREDIT + (b + 1) * HEADS )
                op.tensor(pe, b)

        @block.vector
        def _(dve):
            dve.wait_ge(loaded, LOADED)
            nc.vector.tensor_scalar(bq[:], bq[:], DH ** -0.5, None, ALU.mult).then_inc(bq_scaled, 1)
            with dve.Fori(0, BATCH) as b:
                for i in range(2 * TILES):
                    t, half = i // 2, i % 2
                    dve.wait_ge(v_ready, CREDIT + b * 2 * TILES + i + 1)
                    cols = slice(half * 512, half * 512 + 512)
                    nc.vector.tensor_tensor(v[:, t, cols], g.ps[:, 2 + i % 2], bv[:, cols], ALU.add).then_inc(v_copied, 1)
                at.vector(dve, b)
                for t in range(TILES):
                    dve.wait_ge(op.s_ready, CREDIT + b * TILES + t + 1)
                    nc.vector.tensor_tensor(g.s[:, bass.ds(b * TILES + t, 1), :].rearrange("p a d -> p (a d)"),
                                            g.ps[:, t % 2, 0:D], bo[:], ALU.add).then_inc(op.s_copied, 1)

        @block.scalar
        def _(act):
            act.wait_ge(bq_scaled, 1)
            with act.Fori(0, BATCH) as b:
                for i in range(2 * PAIRS):
                    c = i // 2
                    dst, bias, scale = ((qT, bq, DH ** -0.5), (kT, bk, 1.0))[i % 2]
                    act.wait_ge(proj_ready, CREDIT + b * 2 * PAIRS + i + 1)
                    nc.scalar.activation(dst[:, c], g.ps[:, i % 2], ACT.Identity, bias=bias[:, c:c + 1],
                                         scale=scale).then_inc(proj_copied, 1)
                at.scalar(act, b)
                op.scalar(act, b)


STATES, TAPS, DT_RANK, HALF = 16, 4, 4, D // 2


def l2_attn_stage(g):
    nc = g.nc
    PAD = TAPS - 1
    with ExitStack() as stack:
        sb, once, sem = scope(nc, stack, "l2a")
        par = {n: sb(n, [P, 2, c]) for n, c in (("win", 2 * P), ("wx", DT_RANK + 2 * STATES), ("wout", HALF),
                                                ("wconv", TAPS), ("alog", STATES), ("vec", 3))}
        wdt = sb("wdt", [DT_RANK, 2, P])
        A = sb("A", [P, 2, STATES])
        lnp = sb("lnp", [P, 2])
        pick = sb("pick", [96, 2 * STATES])
        sel = sb("sel", [96, 2 * STATES, P], BF16)
        stats = sb("stats", [P, NT, 6])
        mv = sb("mv", [P, NT, 2])
        rstd = sb("rstd", [P, NT])
        hn = g.gate
        hT = sb("hT", [P, BATCH * SEQ])
        xp = sb("xp", [P, SEQ + 2 * PAD])
        cv = sb("cv", [P, TAPS, SEQ])
        xc = sb("xc", [P, SEQ])
        zs = sb("zs", [P, SEQ])
        dt4 = sb("dt4", [DT_RANK, SEQ])
        sp_a = sb("sp_a", [P, SEQ])
        sp_e = sb("sp_e", [P, SEQ])
        sp_l = sb("sp_l", [P, SEQ])
        sp_m = sb("sp_m", [P, SEQ])
        dt = sb("dt", [P, SEQ])
        dtx = sb("dtx", [P, SEQ])
        rest = sb("rest", [2 * STATES, 2, SEQ])
        part = sb("part", [2 * STATES, 3, SEQ], BF16)
        split = sb("split", [96, SEQ], BF16)
        dA = sb("dA", [P, 2, SEQ])
        dBx = sb("dBx", [P, 2, SEQ])
        hs = sb("hs", [P, 2, SEQ])
        hc = sb("hc", [P, 2, SEQ])
        yg = sb("yg", [P, SEQ])
        y = sb("y", [P, SEQ])
        res = sb("res", [P, TILES, D])
        loaded = once("loaded")
        pre = once("pre")
        var_ready = once("var_ready")
        rstd_ready = once("rstd_ready")
        hn_ready = once("hn_ready")
        h_turned = once("h_turned")
        hT_ready = once("hT_ready")
        A_ready = once("A_ready")
        dve_step = once("dve_step")
        act_step = once("act_step")
        in_ready = sem("in_ready")
        xp_ready = sem("xp_ready")
        zs_ready = sem("zs_ready")
        conv_ready = sem("conv_ready")
        xc_ready = sem("xc_ready")
        dbc_ready = sem("dbc_ready")
        dt4_ready = sem("dt4_ready")
        dt_product = sem("dt_product")
        soft_ready = sem("soft_ready")
        dt_ready = sem("dt_ready")
        split_ready = sem("split_ready")
        bc_ready = sem("bc_ready")
        dA_ready = sem("dA_ready")
        dBx_ready = sem("dBx_ready")
        hs_ready = sem("hs_ready")
        hc_ready = sem("hc_ready")
        y_added = sem("y_added")
        y_ready = sem("y_ready")
        out_ready = sem("out_ready")
        res_ready = sem("res_ready")
        s_ready = sem("s_ready")
        block = stack.enter_context(nc.Block())
        names = ("Win", "Wx", "Wout", "Wconv", "Alog", "vec", "Wdt")
        LOADED = 16 * (2 * len(names) + 2)
        N = STATES

        def at(b, u, per, k):
            return CREDIT + u * per + k + b * 2 * per

        @block.sync
        def _(sp):
            start_counts(sp, sem)
            for u in range(2):
                for n in names:
                    dst = wdt[:, u] if n == "Wdt" else par[n.lower()][:, u]
                    sp.dma_start(dst, g.w[f"L2_m{u + 1}_{n}"]).then_inc(loaded, 16)
            sp.dma_start(lnp[:], g.w["L2_attn_ln"]).then_inc(loaded, 16)
            sp.dma_start(pick[:], g.c["pick"]).then_inc(loaded, 16)

        @block.gpsimd
        def _(pool):
            pool.wait_ge(var_ready, 1)
            nc.gpsimd.tensor_tensor(rstd[:], mv[:, :, 1], g.neghalf[:, 0:NT], ALU.pow).then_inc(rstd_ready, 1)

        @block.tensor
        def _(pe):
            for b in range(BATCH):
                if b >= 2:
                    pe.wait_ge(hT_ready, b - 1)
                pe.wait_ge(hn_ready, (b + 1) * TILES)
                for t in range(TILES):
                    ins = nc.tensor.transpose(g.ps[:, b % 2, t * P:(t + 1) * P], hn[:, b * TILES + t], g.ident[:])
                ins.then_inc(h_turned, 1)
            pe.wait_ge(hT_ready, BATCH)
            pe.wait_ge(loaded, LOADED)
            pe.wait_ge(pre, MAMBA_PRE)
            with pe.Fori(0, BATCH) as b:
                for u in range(2):
                    pe.wait_ge(out_ready, at(b, u, 1, 0))
                    for c in range(2):
                        ins = nc.tensor.matmul(g.ps[:, c], par["win"][:, u, c * P:(c + 1) * P],
                                               hT[:, bass.ds(b * SEQ, SEQ)], start=True, stop=True)
                    ins.then_inc(in_ready, 1)
                    pe.wait_ge(xc_ready, at(b, u, 1, 1))
                    pe.wait_ge(zs_ready, at(b, u, 1, 1))
                    nc.tensor.matmul(g.ps[0:DT_RANK, 2], par["wx"][:, u, 0:DT_RANK], xc[:], start=True, stop=True)
                    nc.tensor.matmul(g.ps[0:2 * N, 3], par["wx"][:, u, DT_RANK:], xc[:],
                                     start=True, stop=True).then_inc(dbc_ready, 1)
                    pe.wait_ge(dt4_ready, at(b, u, 1, 1))
                    nc.tensor.matmul(g.ps[:, 4], wdt[:, u], dt4[:], start=True, stop=True).then_inc(dt_product, 1)
                    pe.wait_ge(split_ready, at(b, u, 1, 1))

                    def spread(n):
                        pe.wait_ge(hc_ready, at(b, u, N, n - 1))
                        nc.tensor.matmul(g.ps[:, n % 2], sel[:, n], split[:], start=True, stop=True)
                        nc.tensor.matmul(g.ps[:, 2 + n % 2], sel[:, N + n], split[:],
                                         start=True, stop=True).then_inc(bc_ready, 1)

                    spread(0)
                    for n in range(N):
                        if n + 1 < N:
                            spread(n + 1)
                        pe.wait_ge(hc_ready, at(b, u, N, n + 1))
                        nc.tensor.matmul(g.ps[:, 5], g.ident[:], hc[:, n % 2], start=(n == 0),
                                         stop=(n == N - 1)).then_inc(y_added, 1)
                    pe.wait_ge(y_ready, at(b, u, 1, 1))
                    if u == 0:
                        pe.wait_ge(res_ready, CREDIT + b)
                    for t in range(TILES):
                        c0 = t * D + u * HALF
                        ins = nc.tensor.matmul(g.ps[:, 6, c0:c0 + HALF], y[:, t * P:(t + 1) * P], par["wout"][:, u],
                                               start=True, stop=True)
                    ins.then_inc(out_ready, 1)

        @block.vector
        def _(dve):
            ch = Chain(dve, pre)
            for n in range(NT):
                ch.done(nc.vector.bn_stats(stats[:, n], g.xn[:, n]))
            ch.join()
            for n in range(NT):
                ch.done(nc.vector.bn_aggr(mv[:, n], stats[:, n]))
            ch.join()
            nc.vector.tensor_scalar(mv[:, :, 1], mv[:, :, 1], LN_EPS, None, ALU.add).then_inc(var_ready, 1)
            ch.done(nc.vector.memset(xp[:], 0.0))
            dve.wait_ge(loaded, LOADED)
            ch.done(nc.vector.tensor_copy(sel[:], pick[:].unsqueeze(2).broadcast_to([96, 2 * N, P])))
            dve.wait_ge(A_ready, 1)
            ch.done(nc.vector.tensor_scalar(A[:], A[:], -1.0, None, ALU.mult))
            dve.wait_ge(rstd_ready, 1)
            for n in range(NT):
                nc.vector.tensor_scalar(hn[:, n], g.xn[:, n], mv[:, n, 0:1], rstd[:, n:n + 1],
                                        ALU.subtract, ALU.mult).then_inc(hn_ready, 1)
            ch.join()
            assert ch.n == MAMBA_PRE
            with dve.Fori(0, BATCH) as b:
                for u in range(2):
                    ch = Chain(dve, dve_step)
                    dve.sem_clear(dve_step)
                    dve.wait_ge(xp_ready, at(b, u, 1, 1))
                    for k in range(TAPS):
                        k0 = 2 * PAD - k if u else k
                        w = par["wconv"][:, u, k:k + 1]
                        if k == 0:
                            ch.done(nc.vector.tensor_scalar(cv[:, 0], xp[:, k0:k0 + SEQ], w, None, ALU.mult))
                        else:
                            ch.join()
                            ins = nc.vector.scalar_tensor_tensor(cv[:, k], xp[:, k0:k0 + SEQ], w, cv[:, k - 1],
                                                                 ALU.mult, ALU.add)
                            if k < TAPS - 1:
                                ch.done(ins)
                    ins.then_inc(conv_ready, 1)
                    dve.wait_ge(dbc_ready, at(b, u, 1, 1))
                    rows = g.ps[0:2 * N, 3]
                    ch.done(nc.vector.tensor_copy(part[:, 0], rows))
                    ch.join()
                    ch.done(nc.vector.tensor_tensor(rest[:, 0], rows, part[:, 0], ALU.subtract))
                    ch.join()
                    ch.done(nc.vector.tensor_copy(part[:, 1], rest[:, 0]))
                    ch.join()
                    ch.done(nc.vector.tensor_tensor(rest[:, 1], rest[:, 0], part[:, 1], ALU.subtract))
                    ch.join()
                    ch.done(nc.vector.tensor_copy(split[64:96], rest[:, 1]))
                    ch.done(nc.vector.tensor_copy(split[32:64], part[:, 1]))
                    ch.join()
                    nc.vector.tensor_copy(split[0:32], part[:, 0]).then_inc(split_ready, 1)
                    dve.wait_ge(dt_product, at(b, u, 1, 1))
                    dve.wait_ge(soft_ready, at(b, u, 1, 1))
                    ch.done(nc.vector.tensor_scalar(sp_m[:], g.ps[:, 4], par["vec"][:, u, 1:2], 0.0, ALU.add, ALU.max))
                    ch.join()
                    nc.vector.tensor_tensor(dt[:], sp_m[:], sp_l[:], ALU.add).then_inc(dt_ready, 1)
                    dve.wait_ge(dt_ready, at(b, u, 1, 1))
                    ch.done(nc.vector.tensor_tensor(dtx[:], dt[:], xc[:], ALU.mult))
                    ch.join()
                    way = slice(None, None, -1) if u else slice(None)
                    for n in range(N):
                        dve.wait_ge(bc_ready, at(b, u, N, n + 1))
                        nc.vector.tensor_tensor(dBx[:, n % 2], g.ps[:, n % 2], dtx[:], ALU.mult).then_inc(dBx_ready, 1)
                        dve.wait_ge(dBx_ready, at(b, u, N, n + 1))
                        dve.wait_ge(dA_ready, at(b, u, N, n + 1))
                        nc.vector.tensor_tensor_scan(hs[:, n % 2, way], dA[:, n % 2, way], dBx[:, n % 2, way], 0.0,
                                                     ALU.mult, ALU.add).then_inc(hs_ready, 1)
                        dve.wait_ge(hs_ready, at(b, u, N, n + 1))
                        dve.wait_ge(y_added, at(b, u, N, n - 1))
                        nc.vector.tensor_tensor(hc[:, n % 2], g.ps[:, 2 + n % 2], hs[:, n % 2], ALU.mult).then_inc(hc_ready, 1)
                    dve.wait_ge(y_added, at(b, u, N, N))
                    ch.done(nc.vector.scalar_tensor_tensor(yg[:], xc[:], par["vec"][:, u, 2:3], g.ps[:, 5],
                                                           ALU.mult, ALU.add))
                    ch.join()
                    dve.wait_ge(out_ready, at(b, u, 1, 0))
                    nc.vector.tensor_tensor(y[:, way], yg[:], zs[:], ALU.mult).then_inc(y_ready, 1)
                dve.wait_ge(out_ready, at(b, 1, 1, 1))
                dve.wait_ge(s_ready, CREDIT + b)
                nc.vector.tensor_tensor(res[:], g.ps[:, 6].rearrange("p (t d) -> p t d", t=TILES),
                                        g.xn[:, bass.ds(b * TILES, TILES), :], ALU.add).then_inc(res_ready, 1)

        @block.scalar
        def _(act):
            act.wait_ge(loaded, LOADED)
            nc.scalar.activation(A[:], par["alog"][:], ACT.Exp).then_inc(A_ready, 1)
            for b in range(BATCH):
                act.wait_ge(h_turned, b + 1)
                nc.scalar.activation(hT[:, b * SEQ:(b + 1) * SEQ], g.ps[:, b % 2], ACT.Identity,
                                     bias=lnp[:, 1:2], scale=lnp[:, 0:1]).then_inc(hT_ready, 1)
            act.wait_ge(pre, MAMBA_PRE)
            with act.Fori(0, BATCH) as b:
                for u in range(2):
                    ch = Chain(act, act_step)
                    act.sem_clear(act_step)
                    act.wait_ge(in_ready, at(b, u, 1, 1))
                    nc.scalar.copy(xp[:, PAD:PAD + SEQ], g.ps[:, 0]).then_inc(xp_ready, 1)
                    act.wait_ge(y_ready, at(b, u, 1, 0))
                    nc.scalar.activation(zs[:], g.ps[:, 1], ACT.Silu).then_inc(zs_ready, 1)
                    act.wait_ge(conv_ready, at(b, u, 1, 1))
                    nc.scalar.activation(xc[:], cv[:, TAPS - 1], ACT.Silu, bias=par["vec"][:, u, 0:1]).then_inc(xc_ready, 1)
                    act.wait_ge(dbc_ready, at(b, u, 1, 1))
                    nc.scalar.copy(dt4[:], g.ps[0:DT_RANK, 2]).then_inc(dt4_ready, 1)
                    act.wait_ge(dt_product, at(b, u, 1, 1))
                    ch.done(nc.scalar.activation(sp_a[:], g.ps[:, 4], ACT.Abs, bias=par["vec"][:, u, 1:2]))
                    ch.join()
                    ch.done(nc.scalar.activation(sp_e[:], sp_a[:], ACT.Exp, scale=-1.0))
                    ch.join()
                    nc.scalar.activation(sp_l[:], sp_e[:], ACT.Ln, bias=1.0).then_inc(soft_ready, 1)
                    act.wait_ge(dt_ready, at(b, u, 1, 1))
                    for n in range(N):
                        act.wait_ge(hs_ready, at(b, u, N, n - 1))
                        nc.scalar.activation(dA[:, n % 2], dt[:], ACT.Exp, scale=A[:, u, n:n + 1]).then_inc(dA_ready, 1)
                act.wait_ge(res_ready, CREDIT + b + 1)
                nc.scalar.activation(g.s[:, bass.ds(b * TILES, TILES), :], res[:], ACT.Gelu).then_inc(s_ready, 1)


MAMBA_PRE = 2 * NT + 3


DEPTH, WINDOW, DI = 6, 32, int(D * 4 * 2 / 3)


def l2_ffn_stage(g):
    nc = g.nc
    HD = HEADS * DH
    KW = WINDOW + P
    STEPS2 = TILES * PAIRS
    CH = [(0, P), (P, P), (2 * P, DI - 2 * P)]
    NLOAD = 12
    with ExitStack() as stack:
        sb, once, sem = scope(nc, stack, "l2f")
        wqkv = sb("wqkv", [P, 2, 3 * HD])
        wo = sb("wo", [P, 2, PAIRS, D])
        w1 = sb("w1", [P, 2, 2 * DI])
        w2 = sb("w2", [P, 2, 3, D])
        b1 = sb("b1", [P, 2, 2 * DI])
        b2 = sb("b2", [P, 2, D])
        qks = sb("qks", [P, 2, 2, DH])
        lnp = sb("lnp", [P, DEPTH, 2])
        lnd = sb("lnd", [P, 2])
        rope = sb("rope", [P, 2, 2, TILES, DH])
        rot = sb("rot", [P, 2, 2, TILES, DH])
        band_f = sb("band_f", [P, KW])
        band = sb("band", [P, KW], BF16)
        yb = sb("yb", [P, TILES, D])
        xsT = sb("xsT", [P, SEQ + 1])
        nrm = g.xnT[:, 0:2 * HD]
        swp = g.xn[:].rearrange("p t d -> p (t d)")
        cosd = sb("cosd", [P, 2, 2 * HD])
        qT = sb("qT", [P, PAIRS, SEQ])
        kT = sb("kT", [P, PAIRS, SEQ])
        v = sb("v", [P, TILES, HD])
        o = cosd[:].rearrange("p s (t c) -> p (s t) c", c=HD)
        p = sb("p", [P, 2, 2, KW])
        pT = sb("pT", [P, 2, 2, P])
        pTw = sb("pTw", [P, 2, 2, P])
        ss = sb("ss", [P, 2 * HEADS])
        rn = sb("rn", [P, 2 * HEADS])
        negmax = sb("negmax", [P, TILES * HEADS])
        rowsum = sb("rowsum", [P, TILES * HEADS])
        rinv = sb("rinv", [P, TILES * HEADS])
        stats = sb("stats", [P, TILES, 6])
        mv = sb("mv", [P, TILES, 2])
        rstd = sb("rstd", [P, TILES])
        xn2 = sb("xn2", [P, TILES, D])
        xnT2 = sb("xnT2", [P, SEQ])
        ha = sb("ha", [P, 2, DI])
        hg = sb("hg", [P, 2, DI])
        hh = sb("hh", [P, 2, DI])
        hT = sb("hT", [P, 2, 3, P])
        yt = sb("yt", [P, 2, D])
        const_loaded = once("const_loaded")
        loaded = once("loaded")
        y_started = once("y_started")
        band_ready = once("band_ready")
        pad_ready = once("pad_ready")
        dve_step = once("dve_step")
        act_step = once("act_step")
        rot_ready = sem("rot_ready")
        yb_ready = sem("yb_ready")
        y_turned = sem("y_turned")
        xs_ready = sem("xs_ready")
        qkv_ready = sem("qkv_ready")
        sq_ready = sem("sq_ready")
        v_copied = sem("v_copied")
        ss_ready = sem("ss_ready")
        rn_ready = sem("rn_ready")
        nrm_ready = sem("nrm_ready")
        cosq_ready = sem("cosq_ready")
        rotated = sem("rotated")
        qk_turned = sem("qk_turned")
        qk_copied = sem("qk_copied")
        scores_ready = sem("scores_ready")
        negmax_ready = sem("negmax_ready")
        probs_ready = sem("probs_ready")
        turned = sem("turned")
        copied_dve = sem("copied_dve")
        copied_act = sem("copied_act")
        pv_done = sem("pv_done")
        rinv_ready = sem("rinv_ready")
        o_ready = sem("o_ready")
        unshifted = sem("unshifted")
        moments = sem("moments")
        rstd_ready = sem("rstd_ready")
        xn2_ready = sem("xn2_ready")
        xn2_turned = sem("xn2_turned")
        xnT2_ready = sem("xnT2_ready")
        hid_ready = sem("hid_ready")
        hg_ready = sem("hg_ready")
        gelu_ready = sem("gelu_ready")
        hh_ready = sem("hh_ready")
        hh_turned = sem("hh_turned")
        hT_ready = sem("hT_ready")
        ff_ready = sem("ff_ready")
        yt_ready = sem("yt_ready")
        y_ready = sem("y_ready")
        y_final = once("y_final")

        def at(it, per, k):
            return CREDIT + k + it * per

        def copied(it, n):
            return (copied_act if n % 2 else copied_dve), at(it, STEPS2 // 2, n // 2 + 1)

        def banks(b0, n):
            return g.ps[:, b0:b0 + n].rearrange("p a c -> p (a c)")

        def copy_turned(eng, copy, it, n, signal, ch):
            t = n // PAIRS
            eng.wait_ge(turned, at(it, STEPS2, n + 1))
            eng.wait_ge(pv_done, at(it, STEPS2, n - 1))
            if t:
                ch.done(copy(pTw[P - WINDOW:P, n % 2].rearrange("p h q -> p (h q)"),
                             g.ps[0:WINDOW, 4 + n % 2, 2 * P:4 * P]))
                ch.join()
            copy(pT[:, n % 2].rearrange("p h q -> p (h q)"), g.ps[:, 4 + n % 2, 0:2 * P]).then_inc(signal, 1)

        def tile_out(dve, it, t):
            cols = slice(t * HEADS, (t + 1) * HEADS)
            dve.wait_ge(probs_ready, at(it, STEPS2, (t + 1) * PAIRS))
            nc.vector.reciprocal(rinv[:, cols], rowsum[:, cols]).then_inc(rinv_ready, 1)
            dve.wait_ge(pv_done, at(it, STEPS2, (t + 1) * PAIRS))
            dve.wait_ge(rinv_ready, at(it, TILES, t + 1))
            nc.vector.tensor_tensor(o[:, t].rearrange("p (h d) -> p h d", d=DH),
                                    banks(6, 2).rearrange("p (h d) -> p h d", d=DH),
                                    rinv[:, cols].unsqueeze(2).broadcast_to([P, HEADS, DH]), ALU.mult).then_inc(o_ready, 1)

        def feed_out(dve, it, b, s, t):
            dve.wait_ge(ff_ready, at(it, TILES, t + 1))
            nc.vector.tensor_tensor(yt[:, t % 2], g.ps[:, 4 + t % 2, 0:D], yb[:, t], ALU.add).then_inc(yt_ready, 1)
            dve.wait_ge(yt_ready, at(it, TILES, t + 1))
            nc.vector.tensor_tensor(g.gate[:, bass.ds(b * TILES + t, 1), :].rearrange("p a d -> p (a d)"),
                                    yt[:, t % 2], b2[:, bass.ds(s, 1), :].rearrange("p a d -> p (a d)"),
                                    ALU.add).then_inc(y_ready, 1)

        op = OutProduct(g, sb, sem, o, wo)
        block = stack.enter_context(nc.Block())

        @block.sync
        def _(sp):
            start_counts(sp, sem)
            sp.dma_start(rope[:], g.c["rope"]).then_inc(const_loaded, 16)
            sp.dma_start(band_f[:], g.c["band"]).then_inc(const_loaded, 16)
            sp.dma_start(lnp[:], g.w["L2_ffn_ln"]).then_inc(const_loaded, 16)
            for d in range(DEPTH):
                s = d % 2
                if d >= 1:
                    sp.wait_ge(loaded, 16 * NLOAD * d)
                if d >= 2:
                    sp.wait_ge(y_ready, CREDIT + (d - 1) * BATCH * TILES)
                for i, n in enumerate(("q_scale", "k_scale")):
                    sp.dma_start(qks[:, s, i], g.w[f"L2_ffn_{n}"][d].partition_broadcast(P)).then_inc(loaded, 16)
                for c in range(3):
                    sp.dma_start(wqkv[:, s, c * HD:(c + 1) * HD],
                                 g.w["L2_ffn_Wqkv"][d, :, c * HD:(c + 1) * HD]).then_inc(loaded, 16)
                sp.dma_start(wo[:, s], g.w["L2_ffn_Wo"][d]).then_inc(loaded, 16)
                sp.dma_start(w1[:, s], g.w["L2_ffn_W1"][d]).then_inc(loaded, 16)
                for c, (r0, rows) in enumerate(CH):
                    sp.dma_start(w2[0:rows, s, c], g.w["L2_ffn_W2"][d, r0:r0 + rows]).then_inc(loaded, 16)
                sp.dma_start(b1[:, s], g.w["L2_ffn_b1"][d].partition_broadcast(P)).then_inc(loaded, 16)
                sp.dma_start(b2[:, s], g.w["L2_ffn_b2"][d].partition_broadcast(P)).then_inc(loaded, 16)

        @block.gpsimd
        def _(pool):
            with pool.Fori(0, DEPTH) as d:
                with pool.Fori(0, BATCH) as b:
                    pool.wait_ge(rot_ready, CREDIT + 1 + d)
                    it = d * BATCH + b
                    for t in range(TILES):
                        pool.wait_ge(ss_ready, at(it, TILES, t + 1))
                        nc.gpsimd.tensor_tensor(rn[:], ss[:], g.neghalf[:, 0:2 * HEADS], ALU.pow).then_inc(rn_ready, 1)
                        pool.wait_ge(nrm_ready, at(it, TILES, t + 1))
                        nc.gpsimd.tensor_tensor(
                            cosd[:, t % 2, 0:HD].rearrange("p (h d) -> p h d", d=DH),
                            nrm[:, 0:HD].rearrange("p (h d) -> p h d", d=DH),
                            rot[:, 0, 0, t].unsqueeze(1).broadcast_to([P, HEADS, DH]), ALU.mult).then_inc(cosq_ready, 1)
                    pool.wait_ge(moments, at(it, 1, 1))
                    nc.gpsimd.tensor_tensor(rstd[:], mv[:, :, 1], g.neghalf[:, 0:TILES], ALU.pow).then_inc(rstd_ready, 1)

        @block.tensor
        def _(pe):
            pe.wait_ge(band_ready, 1)

            def qkv(it, s, t):
                for c in range(3):
                    if c < 2:
                        pe.wait_ge(nrm_ready, at(it, TILES, t))
                    else:
                        pe.wait_ge(v_copied, at(it, TILES, t))
                    for hf in range(2):
                        c0 = c * HD + hf * 512
                        ins = nc.tensor.matmul(g.ps[:, 2 * c + hf], xsT[:, t * P:(t + 1) * P],
                                               wqkv[:, bass.ds(s, 1), c0:c0 + 512].rearrange("p a c -> p (a c)"),
                                               start=True, stop=True)
                    ins.then_inc(qkv_ready, 1)

            def turn_qk(it, t):
                pe.wait_ge(rotated, at(it, TILES, t + 1))
                for i in range(4):
                    pe.wait_ge(qk_copied, at(it, 4 * TILES, 4 * t + i - 1))
                    for c in range(4):
                        c0 = (4 * i + c) * P
                        ins = nc.tensor.transpose(g.ps[:, 6 + i % 2, c * P:(c + 1) * P],
                                                  cosd[:, t % 2, c0:c0 + P], g.ident[:])
                    ins.then_inc(qk_turned, 1)

            def scores(it, n):
                t, c = n // PAIRS, n % PAIRS
                w = WINDOW if t else 0
                pe.wait_ge(probs_ready, at(it, STEPS2, n - 1))
                for hf in range(2):
                    rows = slice(64 * hf, 64 * hf + 64)
                    out = g.ps[:, 2 * (n % 2) + hf, WINDOW - w:KW]
                    nc.tensor.matmul(out, qT[rows, c, t * P:(t + 1) * P], kT[rows, c, t * P - w:(t + 1) * P],
                                     start=True, stop=False)
                    ins = nc.tensor.matmul(out, g.identb[:], band[:, WINDOW - w:KW], start=False, stop=True)
                ins.then_inc(scores_ready, 1)

            def turn(it, n):
                t = n // PAIRS
                pe.wait_ge(probs_ready, at(it, STEPS2, n + 1))
                if n >= 2:
                    pe.wait_ge(*copied(it, n - 2))
                for hf in range(2):
                    ins = nc.tensor.transpose(g.ps[:, 4 + n % 2, hf * P:(hf + 1) * P],
                                              p[:, n % 2, hf, WINDOW:KW], g.ident[:])
                if t:
                    for hf in range(2):
                        ins = nc.tensor.transpose(g.ps[0:WINDOW, 4 + n % 2, (2 + hf) * P:(3 + hf) * P],
                                                  p[:, n % 2, hf, 0:WINDOW], g.ident[:])
                ins.then_inc(turned, 1)

            def pv(it, n):
                t, c = n // PAIRS, n % PAIRS
                pe.wait_ge(*copied(it, n))
                if c == 0:
                    pe.wait_ge(o_ready, at(it, TILES, t))
                for hf in range(2):
                    hd = slice((2 * c + hf) * DH, (2 * c + hf + 1) * DH)
                    out = g.ps[:, 6 + c // 4, (2 * (c % 4) + hf) * DH:(2 * (c % 4) + hf + 1) * DH]
                    ins = nc.tensor.matmul(out, pT[:, n % 2, hf], v[:, t, hd], start=True, stop=(t == 0))
                    if t:
                        ins = nc.tensor.matmul(out, pTw[P - WINDOW:P, n % 2, hf], v[P - WINDOW:P, t - 1, hd],
                                               start=False, stop=True)
                ins.then_inc(pv_done, 1)

            def shift(it, k):
                for t in range(TILES):
                    ins = nc.tensor.transpose(g.ps[:, 2, t * P:(t + 1) * P], yb[:, t], g.ident[:])
                ins.then_inc(y_turned, 1)
                pe.wait_ge(xs_ready, at(it, 4, 2 * k + 2))

            def hidden(it, s, t):
                pe.wait_ge(hg_ready, at(it, TILES, t - 1))
                for hf in range(2):
                    ins = nc.tensor.matmul(g.ps[:, 6 * hf + t % 2, 0:DI], xnT2[:, t * P:(t + 1) * P],
                                           w1[:, bass.ds(s, 1), hf * DI:(hf + 1) * DI].rearrange("p a c -> p (a c)"),
                                           start=True, stop=True)
                ins.then_inc(hid_ready, 1)

            def hidden_out(it, s, t):
                pe.wait_ge(hh_ready, at(it, TILES, t + 1))
                pe.wait_ge(hT_ready, at(it, 2 * TILES, 2 * t - 2))
                for c, (r0, rows) in enumerate(CH):
                    ins = nc.tensor.transpose(g.ps[0:rows, 2 + t % 2, c * P:(c + 1) * P],
                                              hh[:, t % 2, r0:r0 + rows], g.ident[:])
                ins.then_inc(hh_turned, 1)
                pe.wait_ge(hT_ready, at(it, 2 * TILES, 2 * t + 2))
                pe.wait_ge(yt_ready, at(it, TILES, t - 1))
                for c, (r0, rows) in enumerate(CH):
                    ins = nc.tensor.matmul(g.ps[:, 4 + t % 2, 0:D], hT[0:rows, t % 2, c],
                                           w2[0:rows, bass.ds(s, 1), c].rearrange("p a c -> p (a c)"),
                                           start=(c == 0), stop=(c == 2))
                ins.then_inc(ff_ready, 1)

            with pe.Fori(0, DEPTH // 2) as d2:
                with pe.Fori(0, 2) as s:
                    d = d2 * 2 + s
                    with pe.Fori(0, BATCH) as b:
                        pe.wait_ge(loaded, 16 * NLOAD + d * (16 * NLOAD))
                        it = d * BATCH + b
                        pe.wait_ge(yb_ready, at(it, 1, 1))
                        shift(it, 0)
                        qkv(it, s, 0)
                        for t in range(TILES):
                            if t + 1 < TILES:
                                qkv(it, s, t + 1)
                            turn_qk(it, t)
                        pe.wait_ge(qk_copied, at(it, 4 * TILES, 4 * TILES))
                        pe.wait_ge(v_copied, at(it, TILES, TILES))
                        scores(it, 0)
                        for n in range(STEPS2):
                            if n + 1 < STEPS2:
                                scores(it, n + 1)
                            turn(it, n)
                            if n >= 1:
                                pv(it, n - 1)
                        pv(it, STEPS2 - 1)
                        pe.wait_ge(o_ready, at(it, TILES, TILES))
                        op.tensor(pe, it, wo=lambda c: wo[:, bass.ds(s, 1), c].rearrange("p a c -> p (a c)"))
                        shift(it, 1)
                        for t in range(TILES):
                            ins = nc.tensor.transpose(g.ps[:, 3, t * P:(t + 1) * P], xsT[:, t * P:(t + 1) * P], g.ident[:])
                        ins.then_inc(unshifted, 1)
                        pe.wait_ge(xn2_ready, at(it, 1, 1))
                        for t in range(TILES):
                            ins = nc.tensor.transpose(g.ps[:, 4, t * P:(t + 1) * P], xn2[:, t], g.ident[:])
                        ins.then_inc(xn2_turned, 1)
                        pe.wait_ge(xnT2_ready, at(it, 1, 1))
                        hidden(it, s, 0)
                        hidden(it, s, 1)
                        for t in range(TILES):
                            hidden_out(it, s, t)
                            if t + 2 < TILES:
                                hidden(it, s, t + 2)
                        pe.wait_ge(yt_ready, at(it, TILES, TILES))

        @block.vector
        def _(dve):
            nc.vector.tensor_copy(g.gate[:], g.xn[:]).then_inc(y_started, 1)
            nc.vector.memset(xsT[:], 0.0).then_inc(pad_ready, 1)
            dve.wait_ge(const_loaded, 48)
            nc.vector.tensor_copy(band[:], band_f[:]).then_inc(band_ready, 1)
            dve.wait_ge(y_started, 1)
            dve.wait_ge(pad_ready, 1)
            SW = ((0, 32), (32, 0))

            def heads(x):
                return x.rearrange("p (a h d) -> p a h d", a=2, d=DH)

            def rotate(it, ch, t):
                sl = t % 2
                for k in range(2):
                    dve.wait_ge(sq_ready, at(it, 2 * TILES, 2 * t + k + 1))
                    ch.done(nc.vector.tensor_reduce(ss[:, k * HEADS:(k + 1) * HEADS],
                                                    cosd[:, sl, k * HD:(k + 1) * HD].rearrange("p (h d) -> p h d", d=DH),
                                                    AX_X, ALU.add))
                ch.join()
                nc.vector.tensor_scalar(ss[:], ss[:], 1e-24, None, ALU.max).then_inc(ss_ready, 1)
                dve.wait_ge(rn_ready, at(it, TILES, t + 1))
                nc.vector.tensor_tensor(nrm.rearrange("p (h d) -> p h d", d=DH),
                                        banks(0, 4).rearrange("p (h d) -> p h d", d=DH),
                                        rn[:].unsqueeze(2).broadcast_to([P, 2 * HEADS, DH]), ALU.mult).then_inc(nrm_ready, 1)
                dve.wait_ge(nrm_ready, at(it, TILES, t + 1))
                for to, frm in SW:
                    ch.done(nc.vector.tensor_tensor(
                        heads(swp)[:, :, :, to:to + 32], heads(nrm)[:, :, :, frm:frm + 32],
                        rot[:, :, 1, t, to:to + 32].unsqueeze(2).broadcast_to([P, 2, HEADS, 32]), ALU.mult))
                ch.done(nc.vector.tensor_tensor(
                    cosd[:, sl, HD:2 * HD].rearrange("p (h d) -> p h d", d=DH),
                    nrm[:, HD:2 * HD].rearrange("p (h d) -> p h d", d=DH),
                    rot[:, 1, 0, t].unsqueeze(1).broadcast_to([P, HEADS, DH]), ALU.mult))
                ch.join()
                dve.wait_ge(cosq_ready, at(it, TILES, t + 1))
                nc.vector.tensor_tensor(cosd[:, sl], cosd[:, sl], swp, ALU.add).then_inc(rotated, 1)

            with dve.Fori(0, DEPTH // 2) as d2:
                with dve.Fori(0, 2) as s:
                    d = d2 * 2 + s
                    ch = Chain(dve, dve_step)
                    dve.sem_clear(dve_step)
                    dve.wait_ge(loaded, 16 * NLOAD + d * (16 * NLOAD))
                    ch.done(nc.vector.tensor_copy(lnd[:], lnp[:, bass.ds(d, 1)].rearrange("p a c -> p (a c)")))
                    for k in range(2):
                        sc = qks[:, bass.ds(s, 1), k].broadcast_to([P, TILES, DH])
                        ch.done(nc.vector.tensor_tensor(rot[:, k, 0], rope[:, k, 0], sc, ALU.mult))
                        for to, frm in SW:
                            sc = qks[:, bass.ds(s, 1), k, frm:frm + 32].broadcast_to([P, TILES, 32])
                            ch.done(nc.vector.tensor_tensor(rot[:, k, 1, :, to:to + 32], rope[:, k, 1, :, to:to + 32],
                                                            sc, ALU.mult))
                    ch.join()
                    nc.vector.tensor_copy(lnd[:], lnd[:]).then_inc(rot_ready, 1)
                    with dve.Fori(0, BATCH) as b:
                        it = d * BATCH + b
                        ch = Chain(dve, dve_step)
                        dve.sem_clear(dve_step)
                        dve.wait_ge(y_ready, at(it, TILES, 0))
                        nc.vector.tensor_copy(yb[:], g.gate[:, bass.ds(b * TILES, TILES), :]).then_inc(yb_ready, 1)
                        for t in range(TILES):
                            rotate(it, ch, t)
                        for n in range(STEPS2 + 1):
                            if n < STEPS2:
                                t, c = n // PAIRS, n % PAIRS
                                w = WINDOW if t else 0
                                h0 = t * HEADS + 2 * c
                                dve.wait_ge(scores_ready, at(it, STEPS2, n + 1))
                                nc.vector.tensor_reduce(
                                    negmax[:, h0:h0 + 2],
                                    g.ps[:, 2 * (n % 2):2 * (n % 2) + 2, WINDOW - w:KW],
                                    AX_X, ALU.max, negate=True).then_inc(negmax_ready, 1)
                            if n >= 1 and (n - 1) % 2 == 0:
                                copy_turned(dve, nc.vector.tensor_copy, it, n - 1, copied_dve, ch)
                            if n >= PAIRS and n % PAIRS == 1:
                                tile_out(dve, it, n // PAIRS - 1)
                        tile_out(dve, it, TILES - 1)
                        for t in range(TILES):
                            dve.wait_ge(op.s_ready, at(it, TILES, t + 1))
                            nc.vector.tensor_tensor(yb[:, t], yb[:, t], g.ps[:, t % 2, 0:D], ALU.add).then_inc(op.s_copied, 1)
                        dve.wait_ge(unshifted, at(it, 1, 1))
                        for t in range(TILES):
                            ch.done(nc.vector.bn_stats(stats[:, t], g.ps[:, 3, t * P:(t + 1) * P]))
                        ch.join()
                        for t in range(TILES):
                            ch.done(nc.vector.bn_aggr(mv[:, t], stats[:, t]))
                        ch.join()
                        nc.vector.tensor_scalar(mv[:, :, 1], mv[:, :, 1], LN_EPS, None, ALU.add).then_inc(moments, 1)
                        dve.wait_ge(rstd_ready, at(it, 1, 1))
                        for t in range(TILES):
                            ins = nc.vector.tensor_scalar(xn2[:, t], g.ps[:, 3, t * P:(t + 1) * P], mv[:, t, 0:1],
                                                          rstd[:, t:t + 1], ALU.subtract, ALU.mult)
                            if t < TILES - 1:
                                ch.done(ins)
                        ins.then_inc(xn2_ready, 1)
                        for t in range(TILES + 1):
                            if t < TILES:
                                dve.wait_ge(hid_ready, at(it, TILES, t + 1))
                                ch.done(nc.vector.tensor_tensor(ha[:, t % 2], g.ps[:, t % 2, 0:DI],
                                                                b1[:, bass.ds(s, 1), 0:DI].rearrange("p a c -> p (a c)"),
                                                                ALU.add))
                                nc.vector.tensor_tensor(hg[:, t % 2], g.ps[:, 6 + t % 2, 0:DI],
                                                        b1[:, bass.ds(s, 1), DI:2 * DI].rearrange("p a c -> p (a c)"),
                                                        ALU.add).then_inc(hg_ready, 1)
                                ch.join()
                            if t >= 1:
                                feed_out(dve, it, b, s, t - 1)
                            if t < TILES:
                                dve.wait_ge(gelu_ready, at(it, TILES, t + 1))
                                dve.wait_ge(hh_turned, at(it, TILES, t - 1))
                                nc.vector.tensor_tensor(hh[:, t % 2], ha[:, t % 2], hg[:, t % 2], ALU.mult).then_inc(hh_ready, 1)
                        ch.join()
            dve.wait_ge(y_ready, CREDIT + DEPTH * BATCH * TILES)

        @block.scalar
        def _(act):
            act.wait_ge(pad_ready, 1)

            def shift_copies(it, k):
                act.wait_ge(y_turned, at(it, 2, k + 1))
                nc.scalar.copy(xsT[0:64, 0:SEQ], g.ps[0:64, 2]).then_inc(xs_ready, 1)
                nc.scalar.copy(xsT[64:P, 1:SEQ + 1], g.ps[64:P, 2]).then_inc(xs_ready, 1)

            def squares(it, t):
                for k in range(2):
                    act.wait_ge(qkv_ready, at(it, 3 * TILES, 3 * t + k + 1))
                    act.wait_ge(qk_turned, at(it, 4 * TILES, 4 * (t - 1)))
                    nc.scalar.activation(cosd[:, t % 2, k * HD:(k + 1) * HD], banks(2 * k, 2), ACT.Square).then_inc(sq_ready, 1)
                act.wait_ge(qkv_ready, at(it, 3 * TILES, 3 * t + 3))
                nc.scalar.copy(v[:, t], banks(4, 2)).then_inc(v_copied, 1)

            def qk_copies(it, t):
                for i in range(4):
                    act.wait_ge(qk_turned, at(it, 4 * TILES, 4 * t + i + 1))
                    dst = (qT, kT)[i // 2]
                    nc.scalar.copy(dst[:, 4 * (i % 2):4 * (i % 2) + 4, t * P:(t + 1) * P],
                                   g.ps[:, 6 + i % 2].rearrange("p (c n) -> p c n", c=4)).then_inc(qk_copied, 1)

            with act.Fori(0, DEPTH) as d:
                with act.Fori(0, BATCH) as b:
                    it = d * BATCH + b
                    ch = Chain(act, act_step)
                    act.sem_clear(act_step)
                    act.wait_ge(rot_ready, CREDIT + 1 + d)
                    shift_copies(it, 0)
                    squares(it, 0)
                    for t in range(TILES):
                        if t + 1 < TILES:
                            squares(it, t + 1)
                        qk_copies(it, t)
                    for n in range(STEPS2 + 1):
                        if n < STEPS2:
                            t, c = n // PAIRS, n % PAIRS
                            w = WINDOW if t else 0
                            h0 = t * HEADS + 2 * c
                            act.wait_ge(negmax_ready, at(it, STEPS2, n + 1))
                            act.wait_ge(turned, at(it, STEPS2, n - 1))
                            for hf in range(2):
                                ins = nc.scalar.activation(p[:, n % 2, hf, WINDOW - w:KW],
                                                           g.ps[:, 2 * (n % 2) + hf, WINDOW - w:KW], ACT.Exp,
                                                           bias=negmax[:, h0 + hf:h0 + hf + 1],
                                                           accum_out=rowsum[:, h0 + hf:h0 + hf + 1])
                                if hf == 0:
                                    ch.done(ins)
                            ins.then_inc(probs_ready, 1)
                        if n >= 1 and (n - 1) % 2 == 1:
                            copy_turned(act, nc.scalar.copy, it, n - 1, copied_act, ch)
                    ch.join()
                    op.scalar(act, it)
                    shift_copies(it, 1)
                    act.wait_ge(xn2_turned, at(it, 1, 1))
                    nc.scalar.activation(xnT2[:], g.ps[:, 4], ACT.Identity, bias=lnd[:, 1:2],
                                         scale=lnd[:, 0:1]).then_inc(xnT2_ready, 1)
                    for t in range(TILES + 1):
                        if t < TILES:
                            act.wait_ge(hg_ready, at(it, TILES, t + 1))
                            nc.scalar.activation(hg[:, t % 2], hg[:, t % 2], ACT.Gelu).then_inc(gelu_ready, 1)
                        if t >= 1:
                            act.wait_ge(hh_turned, at(it, TILES, t))
                            act.wait_ge(ff_ready, at(it, TILES, t - 2))
                            nc.scalar.copy(hT[:, (t - 1) % 2, 0:2], g.ps[:, 2 + (t - 1) % 2, 0:2 * P]
                                           .rearrange("p (c n) -> p c n", c=2)).then_inc(hT_ready, 1)
                            nc.scalar.copy(hT[0:CH[2][1], (t - 1) % 2, 2],
                                           g.ps[0:CH[2][1], 2 + (t - 1) % 2, 2 * P:3 * P]).then_inc(hT_ready, 1)
            act.wait_ge(y_ready, CREDIT + DEPTH * BATCH * TILES)
            nc.scalar.activation(g.gate[:], g.gate[:], ACT.Silu).then_inc(y_final, 1)


def l3_attn_stage(g):
    nc = g.nc
    W = D // HEADS
    GR = HEADS // 4
    M = SEQ // W
    with ExitStack() as stack:
        sb, once, sem = scope(nc, stack, "l3a")
        wq = sb("wq", [P, GR, 4, 32])
        wk = sb("wk", [P, D])
        wv = sb("wv", [P, D])
        kF = sb("kF", [P, BATCH, W, M])
        kT_all = sb("kT_all", [P, BATCH, GR, SEQ])
        xb = sb("xb", [P, SEQ])
        qT = sb("qT", [P, GR, SEQ])
        kT = sb("kT", [P, GR, SEQ])
        v = sb("v", [P, TILES, D])
        o = sb("o", [P, TILES, D])
        kd = nc.dram_tensor("k_turn", (BATCH, P, W, M), F32).ap()
        loaded = once("loaded")
        zeroed = once("zeroed")
        kF_product = once("kF_product")
        kF_ready = once("kF_ready")
        kd_stored = once("kd_stored")
        kT_loaded = once("kT_loaded")
        xb_ready = sem("xb_ready")
        kT_ready = sem("kT_ready")
        q_ready = sem("q_ready")
        q_copied = sem("q_copied")
        v_ready = sem("v_ready")
        v_copied = sem("v_copied")
        o_stored = sem("o_stored")
        at = Softmax(g, sb, sem,
                     q=lambda h, t: qT[32 * (h % 4):32 * (h % 4) + W, h // 4, t * P:(t + 1) * P],
                     k=lambda h, n: kT[32 * (h % 4):32 * (h % 4) + W, h // 4, 0:n],
                     v=lambda h, c: v[:, c, h * W:(h + 1) * W],
                     o=lambda h: o[:, :, h * W:(h + 1) * W], width=W)
        block = stack.enter_context(nc.Block())
        w = g.w["L3_attn_qkv_weights"]

        @block.sync
        def _(sp):
            start_counts(sp, sem)
            sp.dma_start(wk[:], w[:, D:2 * D]).then_inc(loaded, 16)
            sp.dma_start(wv[:], w[:, 2 * D:3 * D]).then_inc(loaded, 16)
            sp.wait_ge(zeroed, 1)
            for c in range(GR):
                sp.dma_start(wq[:, c, :, 0:W], w[:, 32 * c:32 * c + 32].rearrange("p (j d) -> p j d", j=4)).then_inc(loaded, 16)
            for b in range(BATCH):
                sp.wait_ge(kF_ready, b + 1)
                sp.dma_start(kd[b], kF[:, b]).then_inc(kd_stored, 16)
            sp.wait_ge(kd_stored, 16 * BATCH)
            sp.wait_ge(zeroed, 2)
            for b in range(BATCH):
                for h in range(HEADS):
                    p0 = 32 * (h % 4)
                    sp.dma_start(kT_all[p0:p0 + W, b, h // 4].rearrange("c (d m) -> c d m", d=W),
                                 kd[b, h * W:(h + 1) * W].rearrange("d c m -> c d m")).then_inc(kT_loaded, 16)

        @block.gpsimd
        def _(pool):
            nc.gpsimd.memset(wq[:], 0.0).then_inc(zeroed, 1)
            nc.gpsimd.memset(kT_all[:], 0.0).then_inc(zeroed, 1)
            with pool.Fori(0, BATCH) as b:
                pool.wait_ge(v_ready, CREDIT + b)
                nc.gpsimd.tensor_copy(xb[:], g.xnT[:, bass.ds(b * SEQ, SEQ)]).then_inc(xb_ready, 1)
                pool.wait_ge(at.o_ready, CREDIT + (b + 1) * HEADS)
                nc.gpsimd.tensor_copy(g.s[:, bass.ds(b * TILES, TILES), :], o[:]).then_inc(o_stored, 1)

        @block.tensor
        def _(pe):
            pe.wait_ge(loaded, 16 * (2 + GR))
            for b in range(BATCH):
                nc.tensor.matmul(g.ps[:, b], wk[:], g.xnT[:, b * SEQ:(b + 1) * SEQ],
                                 start=True, stop=True).then_inc(kF_product, 1)
            pe.wait_ge(kF_ready, BATCH)
            with pe.Fori(0, BATCH) as b:
                pe.wait_ge(xb_ready, CREDIT + b + 1)
                for c in range(GR):
                    pe.wait_ge(q_copied, CREDIT + b * GR + c - 1)
                    nc.tensor.matmul(g.ps[:, 4 + c % 2], wq[:, c].rearrange("p j d -> p (j d)"), xb[:],
                                     start=True, stop=True).then_inc(q_ready, 1)
                for t in range(TILES):
                    ins = nc.tensor.matmul(g.ps[:, 6, t * P:(t + 1) * P], xb[:, t * P:(t + 1) * P], wv[:],
                                           start=True, stop=True)
                ins.then_inc(v_ready, 1)
                pe.wait_ge(q_copied, CREDIT + (b + 1) * GR)
                pe.wait_ge(v_copied, CREDIT + b + 1)
                pe.wait_ge(kT_ready, CREDIT + b + 1)
                at.tensor(pe, b)
                pe.wait_ge(at.o_ready, CREDIT + (b + 1) * HEADS)

        @block.vector
        def _(dve):
            for b in range(BATCH):
                dve.wait_ge(kF_product, b + 1)
                nc.vector.tensor_copy(kF[:, b], g.ps[:, b].rearrange("p (m c) -> p c m", c=W)).then_inc(kF_ready, 1)
            dve.wait_ge(kT_loaded, 16 * BATCH * HEADS)
            with dve.Fori(0, BATCH) as b:
                dve.wait_ge(at.scores_ready, CREDIT + b * STEPS)
                nc.vector.tensor_copy(kT[:], kT_all[:, bass.ds(b, 1)].rearrange("p a c n -> p (a c) n")).then_inc(kT_ready, 1)
                dve.wait_ge(v_ready, CREDIT + b + 1)
                nc.vector.tensor_copy(v[:].rearrange("p t d -> p (t d)"), g.ps[:, 6]).then_inc(v_copied, 1)
                dve.wait_ge(o_stored, CREDIT + b)
                at.vector(dve, b)

        @block.scalar
        def _(act):
            with act.Fori(0, BATCH) as b:
                for c in range(GR):
                    act.wait_ge(q_ready, CREDIT + b * GR + c + 1)
                    nc.scalar.activation(qT[:, c], g.ps[:, 4 + c % 2], ACT.Copy, scale=W ** -0.5).then_inc(q_copied, 1)
                at.scalar(act, b)


class Mixture:

    def __init__(self, nc, g, tag, experts, chunks, swiglu, biased, routing):
        self.g, self.tag = g, tag
        self.E, self.HC, self.swiglu, self.biased, self.routing = experts, chunks, swiglu, biased, routing
        self.run()

    def run(self):
        g, nc = self.g, self.g.nc
        E, HC, swiglu, biased, routing = self.E, self.HC, self.swiglu, self.biased, self.routing
        HIN = 2 if swiglu else HC
        K = E
        R = EXPERTS
        W = g.w
        L = self.tag[:2].upper()
        with ExitStack() as stack:
            sb, once, sem = scope(nc, stack, self.tag)
            w1 = sb("w1", [P, E, HIN * P])
            w2 = sb("w2", [P, E, HC, D])
            wg = sb("wg", [P, R])
            b1 = sb("b1", [P, E * HIN]) if biased else None
            b2 = sb("b2", [K, D]) if biased else None
            bg = sb("bg", [P, 2, R]) if biased else None
            iota = sb("iota", [P, R])
            xb = sb("xb", [P, SEQ])
            h = sb("h", [P, 2, HC, SEQ])
            sa = sb("sa", [P, 2, SEQ]) if swiglu else None
            acc = sb("acc", [P, TILES, D])
            z = sb("z", [P, TILES, R])
            zm = sb("zm", [P, TILES])
            pr = sb("pr", [P, TILES, R])
            top = sb("top", [P, TILES, 8])
            idx = sb("idx", [P, TILES, 8], U32)
            idxf = sb("idxf", [P, TILES, 8])
            pick = sb("pick", [P, 2, TILES, R])
            rw = sb("rw", [P, TILES, K])
            rwT = sb("rwT", [K, TILES, P]) if biased else None
            loaded = once("loaded")
            dve_step = once("dve_step")
            xb_ready = sem("xb_ready")
            logits_ready = sem("logits_ready")
            z_ready = sem("z_ready")
            probs_ready = sem("probs_ready")
            rw_ready = sem("rw_ready")
            rw_turned = sem("rw_turned")
            rwT_ready = sem("rwT_ready")
            bias_ready = sem("bias_ready")
            hid_ready = sem("hid_ready")
            half_ready = sem("half_ready")
            h_ready = sem("h_ready")
            out_ready = sem("out_ready")
            acc_step = sem("acc_step")
            gate_ready = sem("gate_ready")
            block = stack.enter_context(nc.Block())
            A = E * TILES + (1 if biased else 0)
            NH = HC * E if not swiglu else E
            PER = HIN if not swiglu else 1

            loads = [(w1, W[f"{L}_w1"]), (w2, W[f"{L}_w2"]), (wg, W[f"{L}_wg"]), (iota, g.c["iota"])]
            if biased:
                loads += [(b1, W[f"{L}_b1"]), (b2, W[f"{L}_b2"]), (bg, W[f"{L}_bg"].partition_broadcast(P))]

            @block.sync
            def _(sp):
                start_counts(sp, sem)
                for dst, src in loads[2:] + loads[:2]:
                    sp.dma_start(dst[:], src).then_inc(loaded, 16)

            @block.gpsimd
            def _(pool):
                with pool.Fori(0, BATCH) as b:
                    pool.wait_ge(hid_ready, CREDIT + b * E * HIN)
                    nc.gpsimd.tensor_copy(xb[:], g.xnT[:, bass.ds(b * SEQ, SEQ)]).then_inc(xb_ready, 1)

            def hidden(pe, b, e):
                for c in range(HIN):
                    i = e * HIN + c
                    if swiglu:
                        pe.wait_ge(h_ready, CREDIT + b * NH + e - 1)
                    else:
                        pe.wait_ge(h_ready, CREDIT + b * NH + i - 3)
                    nc.tensor.matmul(g.ps[:, i % 4], w1[:, e, c * P:(c + 1) * P], xb[:],
                                     start=True, stop=True).then_inc(hid_ready, 1)

            def outputs(pe, b, e):
                pe.wait_ge(h_ready, CREDIT + b * NH + (e + 1) * PER)
                pe.wait_ge(acc_step, CREDIT + b * A + (A - E * TILES) + (e - 1) * TILES if e >= 1 else CREDIT + b * A)
                for t in range(TILES):
                    for c in range(HC):
                        ins = nc.tensor.matmul(g.ps[:, 4 + e % 2, t * D:(t + 1) * D], h[:, e % 2, c, t * P:(t + 1) * P],
                                               w2[:, e, c], start=(c == 0), stop=(c == HC - 1))
                ins.then_inc(out_ready, 1)

            @block.tensor
            def _(pe):
                pe.wait_ge(loaded, 16 * len(loads))
                with pe.Fori(0, BATCH) as b:
                    pe.wait_ge(xb_ready, CREDIT + b + 1)
                    for t in range(TILES):
                        ins = nc.tensor.matmul(g.ps[:, 6, t * R:(t + 1) * R], xb[:, t * P:(t + 1) * P], wg[:],
                                               start=True, stop=True)
                    ins.then_inc(logits_ready, 1)
                    hidden(pe, b, 0)
                    for e in range(E):
                        if e + 1 < E:
                            hidden(pe, b, e + 1)
                        if e == 0 and biased:
                            pe.wait_ge(rw_ready, CREDIT + b + 1)
                            for t in range(TILES):
                                ins = nc.tensor.transpose(g.ps[0:K, 7, t * P:(t + 1) * P], rw[:, t], g.ident[:])
                            ins.then_inc(rw_turned, 1)
                            pe.wait_ge(rwT_ready, CREDIT + b + 1)
                            for t in range(TILES):
                                ins = nc.tensor.matmul(g.ps[:, 6, t * D:(t + 1) * D], rwT[:, t], b2[:],
                                                       start=True, stop=True)
                            ins.then_inc(bias_ready, 1)
                        outputs(pe, b, e)
                    pe.wait_ge(acc_step, CREDIT + b * A + A)

            def route(dve, b):
                ch = Chain(dve, dve_step)
                dve.sem_clear(dve_step)
                dve.wait_ge(logits_ready, CREDIT + b + 1)
                if E > R:
                    ch.done(nc.vector.memset(rw[:, :, R:E], 1.0))
                lg = g.ps[:, 6, 0:TILES * R].rearrange("p (t r) -> p t r", t=TILES)
                if biased:
                    ch.done(nc.vector.tensor_tensor(z[:], lg, bg[:, 0].unsqueeze(1).broadcast_to([P, TILES, R]), ALU.add))
                else:
                    ch.done(nc.vector.tensor_copy(z[:], lg))
                ch.join()
                if routing == "sigmoid":
                    nc.vector.tensor_tensor(z[:], z[:], bg[:, 1].unsqueeze(1).broadcast_to([P, TILES, R]),
                                            ALU.add).then_inc(z_ready, 1)
                    dve.wait_ge(probs_ready, CREDIT + b + 1)
                    ch.done(nc.vector.tensor_copy(z[:], pr[:]))
                    ch.join()
                else:
                    ch.done(nc.vector.tensor_reduce(zm[:], z[:], AX_X, ALU.max))
                    ch.join()
                    nc.vector.tensor_tensor(z[:], z[:], zm[:].unsqueeze(2).broadcast_to([P, TILES, R]),
                                            ALU.subtract).then_inc(z_ready, 1)
                    dve.wait_ge(probs_ready, CREDIT + b + 1)
                    ch.done(nc.vector.tensor_reduce(zm[:], pr[:], AX_X, ALU.add))
                    ch.join()
                    ch.done(nc.vector.reciprocal(zm[:], zm[:]))
                    ch.join()
                    ch.done(nc.vector.tensor_tensor(pr[:], pr[:], zm[:].unsqueeze(2).broadcast_to([P, TILES, R]), ALU.mult))
                    ch.join()
                for t in range(TILES):
                    ch.done(nc.vector.max(top[:, t], pr[:, t]))
                ch.join()
                for t in range(TILES):
                    ch.done(nc.vector.max_index(idx[:, t], top[:, t], pr[:, t]))
                ch.join()
                ch.done(nc.vector.tensor_copy(idxf[:], idx[:]))
                if routing == "renormalized":
                    ch.done(nc.vector.tensor_tensor(zm[:], top[:, :, 0], top[:, :, 1], ALU.add))
                    ch.join()
                    ch.done(nc.vector.reciprocal(zm[:], zm[:]))
                    ch.join()
                    ch.done(nc.vector.tensor_tensor(top[:, :, 0:2], top[:, :, 0:2],
                                                    zm[:].unsqueeze(2).broadcast_to([P, TILES, 2]), ALU.mult))
                ch.join()
                for k in range(2):
                    ch.done(nc.vector.tensor_tensor(pick[:, k], iota[:].unsqueeze(1).broadcast_to([P, TILES, R]),
                                                    idxf[:, :, k:k + 1].broadcast_to([P, TILES, R]), ALU.is_equal))
                ch.join()
                for k in range(2):
                    ch.done(nc.vector.tensor_tensor(pick[:, k], pick[:, k],
                                                    top[:, :, k:k + 1].broadcast_to([P, TILES, R]), ALU.mult))
                ch.join()
                nc.vector.tensor_tensor(rw[:, :, 0:R], pick[:, 0], pick[:, 1], ALU.add).then_inc(rw_ready, 1)
                dve.wait_ge(rw_ready, CREDIT + b + 1)
                ch.join()

            def add_up(dve, b, e):
                dve.wait_ge(out_ready, CREDIT + b * E + e + 1)
                if e == 0 and not biased:
                    dve.wait_ge(gate_ready, CREDIT + b)
                for t in range(TILES):
                    ps = g.ps[:, 4 + e % 2, t * D:(t + 1) * D]
                    if e == 0 and not biased:
                        ins = nc.vector.tensor_scalar(acc[:, t], ps, rw[:, t, 0:1], None, ALU.mult)
                    else:
                        dve.wait_ge(acc_step, CREDIT + b * A + (A - E * TILES) + (e * TILES + t - TILES + 1 if e else 0))
                        ins = nc.vector.scalar_tensor_tensor(acc[:, t], ps, rw[:, t, e:e + 1], acc[:, t],
                                                             ALU.mult, ALU.add)
                    ins.then_inc(acc_step, 1)

            @block.vector
            def _(dve):
                dve.wait_ge(loaded, 16 * len(loads))
                with dve.Fori(0, BATCH) as b:
                    route(dve, b)
                    if biased:
                        dve.wait_ge(rw_turned, CREDIT + b + 1)
                        nc.vector.tensor_copy(rwT[:].rearrange("k t p -> k (t p)"), g.ps[0:K, 7]).then_inc(rwT_ready, 1)
                        dve.wait_ge(bias_ready, CREDIT + b + 1)
                        dve.wait_ge(gate_ready, CREDIT + b)
                        nc.vector.tensor_copy(acc[:].rearrange("p t d -> p (t d)"), g.ps[:, 6]).then_inc(acc_step, 1)
                    for e in range(E):
                        if swiglu:
                            dve.wait_ge(half_ready, CREDIT + b * E + e + 1)
                            dve.wait_ge(hid_ready, CREDIT + b * E * HIN + (e + 1) * HIN)
                            dve.wait_ge(out_ready, CREDIT + b * E + e - 1)
                            nc.vector.scalar_tensor_tensor(h[:, e % 2, 0], g.ps[:, (2 * e + 1) % 4],
                                                           b1[:, 2 * e + 1:2 * e + 2], sa[:, e % 2],
                                                           ALU.add, ALU.mult).then_inc(h_ready, 1)
                        if e >= 1:
                            add_up(dve, b, e - 1)
                    add_up(dve, b, E - 1)

            @block.scalar
            def _(act):
                act.wait_ge(loaded, 16 * len(loads))
                with act.Fori(0, BATCH) as b:
                    act.wait_ge(z_ready, CREDIT + b + 1)
                    nc.scalar.activation(pr[:], z[:], ACT.Sigmoid if routing == "sigmoid" else ACT.Exp).then_inc(probs_ready, 1)
                    for e in range(E):
                        for c in range(1 if swiglu else HIN):
                            i = e * HIN + c
                            act.wait_ge(hid_ready, CREDIT + b * E * HIN + i + 1)
                            if swiglu:
                                act.wait_ge(h_ready, CREDIT + b * NH + e - 1)
                                nc.scalar.activation(sa[:, e % 2], g.ps[:, i % 4], ACT.Silu,
                                                     bias=b1[:, i:i + 1]).then_inc(half_ready, 1)
                            else:
                                act.wait_ge(out_ready, CREDIT + b * E + e - 1)
                                bias = b1[:, i:i + 1] if biased else 0.0
                                nc.scalar.activation(h[:, e % 2, c], g.ps[:, i % 4], ACT.Gelu,
                                                     bias=bias).then_inc(h_ready, 1)
                    act.wait_ge(acc_step, CREDIT + b * A + A)
                    nc.scalar.activation(g.gate[:, bass.ds(b * TILES, TILES), :], acc[:], ACT.Silu).then_inc(gate_ready, 1)


def l0_ffn_stage(g):
    Mixture(g.nc, g, "l0f", EXPERTS + 1, 4, False, True, "sigmoid")


def l1_ffn_stage(g):
    Mixture(g.nc, g, "l1f", EXPERTS + 1, 1, True, True, "softmax")


def l3_ffn_stage(g):
    Mixture(g.nc, g, "l3f", EXPERTS, 4, False, False, "renormalized")


def more_constants():
    q, j = np.arange(P)[:, None], np.arange(WINDOW + P)[None] - WINDOW
    band = np.where((j > q) | (j < q - WINDOW), -1e30, 0).astype(np.float32)
    return {"rope": rotary_constants(), "band": band, "pick": np.tile(np.eye(32, dtype=np.float32), (3, 1)), "iota": np.tile(np.arange(EXPERTS, dtype=np.float32), (P, 1))}


def more_layouts(a, out, rows, cols):
    H = a["L0_ffn_W1"].shape[1]
    w1 = np.concatenate([a["L0_ffn_W1"], a["L0_ffn_Ws1"][None]])
    w2 = np.concatenate([a["L0_ffn_W2"], a["L0_ffn_Ws2"][None]])
    out["L0_w1"] = w1.transpose(2, 0, 1)
    out["L0_w2"] = w2.transpose(2, 0, 1).reshape(H // P, P, EXPERTS + 1, D).transpose(1, 2, 0, 3)
    out["L0_wg"] = a["L0_ffn_Wg"].T
    out["L0_bg"] = np.stack([a["L0_ffn_bg"], a["L0_ffn_bias"]])
    out["L0_b1"] = cols(np.concatenate([a["L0_ffn_b1"], a["L0_ffn_bs1"][None]]).reshape(-1))
    out["L0_b2"] = np.concatenate([a["L0_ffn_b2"], a["L0_ffn_bs2"][None]])
    out["L1_w1"] = np.concatenate([a["L1_ffn_rw1"], a["L1_ffn_sw1"]]).transpose(1, 0, 2)
    out["L1_w2"] = np.concatenate([a["L1_ffn_rw2"], a["L1_ffn_sw2"]]).transpose(1, 0, 2)[:, :, None]
    out["L1_wg"] = a["L1_ffn_gate_w"]
    out["L1_bg"] = np.stack([a["L1_ffn_gate_b"], a["L1_ffn_gate_b"]])
    out["L1_b1"] = cols(np.concatenate([a["L1_ffn_rb1"], a["L1_ffn_sb1"]]).reshape(-1))
    out["L1_b2"] = np.concatenate([a["L1_ffn_rb2"], a["L1_ffn_sb2"]])
    F = a["L3_ffn_w1"].shape[2]
    out["L3_w1"] = a["L3_ffn_w1"].transpose(1, 0, 2)
    out["L3_w2"] = a["L3_ffn_w2"].reshape(EXPERTS, F // P, P, D).transpose(2, 0, 1, 3)
    out["L3_wg"] = a["L3_ffn_gate_w"]
    out["L0_attn_Wq"] = a["L0_attn_Wq"]
    out["L0_attn_Wkv"] = a["L0_attn_Wkv"]
    out["L0_attn_Wout"] = rows(a["L0_attn_Wout"])
    for n in ("gamma", "q_scale", "k_scale"):
        out[f"L0_attn_{n}"] = a[f"L0_attn_{n}"][:, None]
    out["L0_attn_null_kv"] = a["L0_attn_null_kv"]
    out["L3_attn_qkv_weights"] = a["L3_attn_qkv_weights"]
    for u in (1, 2):
        m = f"L2_attn_m{u}_"
        for n in ("Win", "Wx", "Wout", "Wconv", "Alog", "Wdt"):
            out[f"L2_m{u}_{n}"] = a[m + n]
        out[f"L2_m{u}_vec"] = np.stack([a[m + "bconv"], a[m + "bdt"], a[m + "Dp"]], 1)
    out["L2_attn_ln"] = np.stack([a["L2_attn_ln_g"], a["L2_attn_ln_b"]], 1)
    for n in ("Wqkv", "q_scale", "k_scale", "W1", "b1", "W2", "b2"):
        out[f"L2_ffn_{n}"] = a[f"L2_ffn_{n}"]
    out["L2_ffn_Wo"] = a["L2_ffn_Wo"].reshape(DEPTH, PAIRS, P, D).transpose(0, 2, 1, 3)
    out["L2_ffn_ln"] = np.stack([a["L2_ffn_ln_g"], a["L2_ffn_ln_b"]], 2).transpose(1, 0, 2)


def rotary_constants():
    f = np.float32
    half = np.arange(0, DH, 2, dtype=f)
    inv_freq = f(1) / f(10000) ** (half / f(DH))
    t = np.arange(SEQ, dtype=f)
    freqs = t[:, None] * inv_freq[None]
    freqs = np.concatenate([freqs, freqs], -1)
    base = (half + f(0.4 * DH)) / f(1.4 * DH)
    power = (t - SEQ // 2) / f(WINDOW // 2)
    scale = base[None] ** power[:, None]
    scale = np.concatenate([scale, scale], -1)
    sign = np.where(np.arange(DH) < DH // 2, -1, 1).astype(f)
    cos, sin = np.cos(freqs), np.sin(freqs) * sign
    q = np.stack([cos * scale, sin * scale]) * f(8)
    k = np.stack([cos / scale, sin / scale])
    return np.stack([q, k]).astype(f).reshape(2, 2, TILES, P, DH).transpose(3, 0, 1, 2, 4)


NMASK = 4
ATTN = (l0_attn_stage, l1_attn_stage, l2_attn_stage, l3_attn_stage)
FFN = (l0_ffn_stage, l1_ffn_stage, l2_ffn_stage, l3_ffn_stage)


def finish_stage(g, gate_tensor, last):
    nc = g.nc
    tag = f"upd{g.serial}"
    g.serial += 1
    with ExitStack() as stack:
        sb, sem, _ = scope(nc, stack, tag)
        prod_done = sem("prod_done")
        x_ready = sem("x_ready")
        stored = sem("stored")
        block = stack.enter_context(nc.Block())

        @block.vector
        def _(dve):
            nc.vector.tensor_tensor(g.s[:], g.s[:], gate_tensor[:], ALU.mult).then_inc(prod_done, 1)
            dve.wait_ge(prod_done, 1)
            nc.vector.tensor_tensor(g.x[:], g.x[:], g.s[:], ALU.add).then_inc(x_ready, 1)

        @block.sync
        def _(sp):
            if last:
                sp.wait_ge(x_ready, 1)
                sp.dma_start(g.out.rearrange("b (t p) d -> p (b t) d", p=P), g.x[:]).then_inc(stored, 16)
                sp.wait_ge(stored, 16)


def four_gated_layers(nc, x_in, weights, consts, out):
    g = Ctx()
    g.nc, g.x_in, g.w, g.c, g.out, g.serial = nc, x_in, weights, consts, out, 0
    with ExitStack() as stack:
        def sb(name, shape, dt=F32):
            return stack.enter_context(nc.sbuf_tensor(name, shape, dt))

        g.x = sb("x", [P, NT, D])
        g.xn = sb("xn", [P, NT, D])
        g.xnT = sb("xnT", [P, BATCH * SEQ])
        g.s = sb("s", [P, NT, D])
        g.gate = sb("gate", [P, NT, D])
        g.ident = sb("ident", [P, P])
        g.identb = sb("identb", [P, P], BF16)
        g.maskf = sb("maskf", [P, NMASK, P])
        g.maskb = sb("maskb", [P, NMASK, P], BF16)
        g.neghalf = sb("neghalf", [P, 64])
        g.ps = stack.enter_context(nc.psum_tensor("ps", [P, 8, 512], F32))
        load_stage(g)
        run_stages(g)


def run_stages(g):
    for k in range(4):
        norm_stage(g, f"n{k}")
        ATTN[k](g)
        FFN[k](g)
        finish_stage(g, g.gate, k == 3)


def constants():
    i = np.arange(P)
    NEG = np.float32(-1e30)
    q, k = i[:, None], i[None, :]
    causal = np.where(k > q, NEG, 0)
    prefix = np.where((k > q) & ~((q < 64) & (k < 64)), NEG, 0)
    band_prev = np.where(k < q, NEG, 0)
    band_own = np.where((k > q) | (k < q - 32), NEG, 0)
    masks = np.stack([causal, prefix, band_prev, band_own], 1).astype(np.float32)
    return {"ident": np.eye(P, dtype=np.float32), "masks": masks, **more_constants()}


def layouts(a):
    def rows(w):
        return w.reshape(-1, P, w.shape[-1]).transpose(1, 0, 2)

    def cols(v):
        return v.reshape(-1, P).T

    HD = HEADS * DH
    out = {}
    for n in ("q", "k", "v"):
        out[f"L1_attn_W{n}"] = a[f"L1_attn_W{n}"].transpose(1, 0, 2).reshape(D, HD)
    out["L1_attn_Wo"] = rows(a["L1_attn_Wo"].reshape(HD, D))
    out["L1_attn_bq"] = cols(a["L1_attn_bq"].reshape(HD))
    out["L1_attn_bk"] = cols(a["L1_attn_bk"].reshape(HD))
    out["L1_attn_bv"] = a["L1_attn_bv"].reshape(HD)
    out["L1_attn_bo"] = a["L1_attn_bo"]
    more_layouts(a, out, rows, cols)
    return out


def kernel(**inputs):
    import concourse.bacc as _bacc
    from concourse.bass_utils import run_bass_kernel_spmd as _run

    nc = _bacc.Bacc("TRN2", target_bir_lowering=False, num_devices=1)
    arrays = {}

    def dram(name, a):
        a = np.ascontiguousarray(a)
        arrays[name] = a
        return nc.dram_tensor(name, a.shape, mybir.dt.from_np(a.dtype), kind="ExternalInput").ap()

    x = dram("x_dram", inputs["L0_attn_x"])
    weights = {n: dram(f"{n}_dram", a) for n, a in layouts({k: np.asarray(v) for k, v in inputs.items()}).items()}
    consts = {n: dram(f"{n}_const", a) for n, a in constants().items()}
    out = nc.dram_tensor("out_dram", (BATCH, SEQ, D), F32, kind="ExternalOutput").ap()
    four_gated_layers(nc, x, weights, consts, out)
    r = _run(nc, [arrays], core_ids=[0])
    return r.results[0]["out_dram"]
```

```python
import numpy as np

import concourse.bass as bass
from concourse import mybir
from contextlib import ExitStack

ALU = mybir.AluOpType
ACT = mybir.ActivationFunctionType
F32 = mybir.dt.float32
BF16 = mybir.dt.bfloat16
U32 = mybir.dt.uint32
AX_X = mybir.AxisListType.X

P = 128
BATCH, SEQ, D = 4, 512, 128
TILES = SEQ // P
NT = BATCH * TILES
HEADS, DH = 16, 64
PAIRS = HEADS // 2
LN_EPS = 1e-5
EXPERTS = 8
STEPS = HEADS * TILES
CREDIT = 4


def head_tile(n):
    return n // TILES, n % TILES


class Ctx:
    pass


def scope(nc, stack, tag):
    made = []

    def end():
        nc.clear_and_free_semaphores(made)
        nc.all_engine_barrier()

    stack.callback(end)

    def sb(name, shape, dt=F32):
        return stack.enter_context(nc.sbuf_tensor(f"{tag}_{name}", shape, dt))

    def once(name):
        made.append(nc.alloc_semaphore(f"{tag}_{name}"))
        return made[-1]

    def counted(name):
        counted.made.append(once(name))
        return counted.made[-1]

    counted.made = []
    return sb, once, counted


def start_counts(eng, counted):
    for s in counted.made:
        eng.sem_inc(s, CREDIT)


class Chain:

    def __init__(self, eng, semaphore):
        self.eng, self.sem, self.n = eng, semaphore, 0

    def done(self, ins):
        self.n += 1
        ins.then_inc(self.sem, 1)

    def join(self):
        self.eng.wait_ge(self.sem, self.n)

    def restart(self):
        self.join()
        self.eng.sem_clear(self.sem)
        self.n = 0


def load_stage(g):
    nc = g.nc
    with ExitStack() as stack:
        sb, sem, _ = scope(nc, stack, "load")
        landed = sem("landed")
        block = stack.enter_context(nc.Block())

        @block.sync
        def _(sp):
            sp.dma_start(g.x[:], g.x_in.rearrange("b (t p) d -> p (b t) d", p=P)).then_inc(landed, 16)
            sp.dma_start(g.ident[:], g.c["ident"]).then_inc(landed, 16)
            sp.dma_start(g.maskf[:], g.c["masks"]).then_inc(landed, 16)
            sp.wait_ge(landed, 48)

        @block.vector
        def _(dve):
            dve.memset(g.neghalf[:], -0.5)
            dve.wait_ge(landed, 48)
            nc.vector.tensor_copy(g.identb[:], g.ident[:])
            nc.vector.tensor_copy(g.maskb[:], g.maskf[:])


def norm_stage(g, tag):
    nc = g.nc
    with ExitStack() as stack:
        sb, sem, _ = scope(nc, stack, tag)
        stats = sb("stats", [P, NT, 6])
        mv = sb("mv", [P, NT, 2])
        rstd = sb("rstd", [P, NT])
        stats_done = sem("stats_done")
        mean_done = sem("mean_done")
        var_ready = sem("var_ready")
        rstd_ready = sem("rstd_ready")
        xn_ready = sem("xn_ready")
        turned = sem("turned")
        copied = sem("copied")
        block = stack.enter_context(nc.Block())

        @block.vector
        def _(dve):
            for n in range(NT):
                nc.vector.bn_stats(stats[:, n], g.x[:, n]).then_inc(stats_done, 1)
            for n in range(NT):
                dve.wait_ge(stats_done, n + 1)
                nc.vector.bn_aggr(mv[:, n], stats[:, n]).then_inc(mean_done, 1)
            dve.wait_ge(mean_done, NT)
            nc.vector.tensor_scalar(mv[:, :, 1], mv[:, :, 1], LN_EPS, None, ALU.add).then_inc(var_ready, 1)
            dve.wait_ge(rstd_ready, 1)
            for n in range(NT):
                nc.vector.tensor_scalar(g.xn[:, n], g.x[:, n], mv[:, n, 0:1], rstd[:, n:n + 1],
                                        ALU.subtract, ALU.mult).then_inc(xn_ready, 1)

        @block.gpsimd
        def _(pool):
            pool.wait_ge(var_ready, 1)
            nc.gpsimd.tensor_tensor(rstd[:], mv[:, :, 1], g.neghalf[:, 0:NT], ALU.pow).then_inc(rstd_ready, 1)

        @block.tensor
        def _(pe):
            for b in range(BATCH):
                if b >= 2:
                    pe.wait_ge(copied, b - 1)
                for t in range(TILES):
                    n = b * TILES + t
                    pe.wait_ge(xn_ready, n + 1)
                    ins = nc.tensor.transpose(g.ps[:, b % 2, t * P:(t + 1) * P], g.xn[:, n], g.ident[:])
                ins.then_inc(turned, 1)

        @block.scalar
        def _(act):
            for b in range(BATCH):
                act.wait_ge(turned, b + 1)
                nc.scalar.copy(g.xnT[:, b * SEQ:(b + 1) * SEQ], g.ps[:, b % 2]).then_inc(copied, 1)


class Softmax:

    def __init__(self, g, sb, sem, q, k, v, o, width, nulls=None, v_null=None):
        self.g, self.nc = g, g.nc
        self.q, self.k, self.v, self.o, self.width = q, k, v, o, width
        self.nulls, self.v_null = nulls, v_null
        self.extra = 0 if nulls is None else 2
        self.p = sb("p", [P, 2, SEQ + self.extra])
        self.pT = sb("pT", [P, 2, SEQ])
        self.pTn = sb("pTn", [2, 2, P]) if self.extra else None
        self.negmax = sb("negmax", [P, STEPS])
        self.rowsum = sb("rowsum", [P, STEPS])
        self.rinv = sb("rinv", [P, STEPS])
        self.scores_ready = sem("scores_ready")
        self.negmax_ready = sem("negmax_ready")
        self.probs_ready = sem("probs_ready")
        self.turned = sem("turned")
        self.copied_dve = sem("copied_dve")
        self.copied_act = sem("copied_act")
        self.null_copied = sem("null_copied")
        self.pv_done = sem("pv_done")
        self.rinv_ready = sem("rinv_ready")
        self.o_ready = sem("o_ready")

    def copied(self, b, n):
        h, t = head_tile(n)
        if t < 2:
            return self.copied_dve, CREDIT + b * 2 * HEADS + 2 * h + t + 1
        return self.copied_act, CREDIT + b * 2 * HEADS + 2 * h + t - 1

    def pe_scores(self, pe, b, n):
        nc, g = self.nc, self.g
        h, t = head_tile(n)
        keys = (t + 1) * P
        s = g.ps[:, 2 * (n % 2):2 * (n % 2) + 2].rearrange("p a c -> p (a c)")
        pe.wait_ge(self.probs_ready, CREDIT + b * STEPS + n - 1)
        if self.extra:
            pe.wait_ge(self.null_copied, CREDIT + b * STEPS + n - 1)
        nc.tensor.matmul(s[:, 0:keys], self.q(h, t), self.k(h, keys), start=True, stop=False)
        ins = nc.tensor.matmul(s[:, keys - P:keys], g.identb[:],
                               g.maskb[:, 1 if (self.extra and t == 0) else 0], start=False, stop=True)
        if self.extra:
            ins = nc.tensor.matmul(s[:, keys:keys + 2], self.q(h, t), self.nulls(h), start=True, stop=True)
        ins.then_inc(self.scores_ready, 1)

    def pe_turn(self, pe, b, n):
        nc, g = self.nc, self.g
        h, t = head_tile(n)
        pe.wait_ge(self.probs_ready, CREDIT + b * STEPS + n + 1)
        if n >= 2:
            pe.wait_ge(*self.copied(b, n - 2))
        for c in range(t + 1):
            ins = nc.tensor.transpose(g.ps[:, 4 + n % 2, c * P:(c + 1) * P],
                                      self.p[:, n % 2, c * P:(c + 1) * P], g.ident[:])
        if self.extra:
            ins = nc.tensor.transpose(g.ps[0:2, 2 * (n % 2) + 1, 256:256 + P],
                                      self.p[:, n % 2, (t + 1) * P:(t + 1) * P + 2], g.ident[:])
        ins.then_inc(self.turned, 1)

    def pe_pv(self, pe, b, n):
        nc, g = self.nc, self.g
        h, t = head_tile(n)
        pe.wait_ge(*self.copied(b, n))
        if self.extra:
            pe.wait_ge(self.null_copied, CREDIT + b * STEPS + n + 1)
        if t == 0:
            pe.wait_ge(self.o_ready, CREDIT + b * HEADS + h - 1)
        out = g.ps[:, 6 + h % 2, t * self.width:(t + 1) * self.width]
        for c in range(t + 1):
            ins = nc.tensor.matmul(out, self.pT[:, n % 2, c * P:(c + 1) * P], self.v(h, c),
                                   start=(c == 0), stop=(c == t and not self.extra))
        if self.extra:
            ins = nc.tensor.matmul(out, self.pTn[:, n % 2], self.v_null(h), start=False, stop=True)
        ins.then_inc(self.pv_done, 1)

    def tensor(self, pe, b):
        self.pe_scores(pe, b, 0)
        for n in range(STEPS):
            if n + 1 < STEPS:
                self.pe_scores(pe, b, n + 1)
            self.pe_turn(pe, b, n)
            if n >= 1:
                self.pe_pv(pe, b, n - 1)
        self.pe_pv(pe, b, STEPS - 1)

    def copy_turned(self, eng, copy, b, n, signal):
        t = n % TILES
        eng.wait_ge(self.turned, CREDIT + b * STEPS + n + 1)
        eng.wait_ge(self.pv_done, CREDIT + b * STEPS + n - 1)
        copy(self.pT[:, n % 2, 0:(t + 1) * P], self.g.ps[:, 4 + n % 2, 0:(t + 1) * P]).then_inc(signal, 1)

    def dve_out(self, dve, b, h):
        nc, g = self.nc, self.g
        cols = slice(h * TILES, (h + 1) * TILES)
        dve.wait_ge(self.probs_ready, CREDIT + b * STEPS + (h + 1) * TILES)
        nc.vector.reciprocal(self.rinv[:, cols], self.rowsum[:, cols]).then_inc(self.rinv_ready, 1)
        dve.wait_ge(self.pv_done, CREDIT + b * STEPS + (h + 1) * TILES)
        dve.wait_ge(self.rinv_ready, CREDIT + b * HEADS + h + 1)
        ps = g.ps[:, 6 + h % 2, 0:TILES * self.width].rearrange("p (t w) -> p t w", t=TILES)
        nc.vector.tensor_tensor(self.o(h), ps, self.rinv[:, cols].unsqueeze(2).broadcast_to([P, TILES, self.width]),
                                ALU.mult).then_inc(self.o_ready, 1)

    def vector(self, dve, b):
        nc, g = self.nc, self.g
        for n in range(STEPS + 2):
            if n < STEPS:
                t = n % TILES
                s = g.ps[:, 2 * (n % 2):2 * (n % 2) + 2].rearrange("p a c -> p (a c)")
                dve.wait_ge(self.scores_ready, CREDIT + b * STEPS + n + 1)
                nc.vector.tensor_reduce(self.negmax[:, n:n + 1], s[:, 0:(t + 1) * P + self.extra], AX_X, ALU.max,
                                        negate=True).then_inc(self.negmax_ready, 1)
            if 1 <= n <= STEPS and (n - 1) % TILES < 2:
                self.copy_turned(dve, nc.vector.tensor_copy, b, n - 1, self.copied_dve)
            if n >= TILES and n % TILES == 1:
                self.dve_out(dve, b, n // TILES - 1)

    def scalar(self, act, b):
        nc, g = self.nc, self.g
        for n in range(STEPS + 1):
            if n < STEPS:
                t = n % TILES
                keys = (t + 1) * P + self.extra
                s = g.ps[:, 2 * (n % 2):2 * (n % 2) + 2].rearrange("p a c -> p (a c)")
                act.wait_ge(self.negmax_ready, CREDIT + b * STEPS + n + 1)
                if n >= 2:
                    act.wait_ge(self.turned, CREDIT + b * STEPS + n - 1)
                nc.scalar.activation(self.p[:, n % 2, 0:keys], s[:, 0:keys], ACT.Exp,
                                     bias=self.negmax[:, n:n + 1],
                                     accum_out=self.rowsum[:, n:n + 1]).then_inc(self.probs_ready, 1)
            if n >= 1:
                if self.extra:
                    act.wait_ge(self.turned, CREDIT + b * STEPS + n)
                    act.wait_ge(self.pv_done, CREDIT + b * STEPS + n - 2)
                    nc.scalar.copy(self.pTn[:, (n - 1) % 2],
                                   g.ps[0:2, 2 * ((n - 1) % 2) + 1, 256:256 + P]).then_inc(self.null_copied, 1)
                if (n - 1) % TILES >= 2:
                    self.copy_turned(act, nc.scalar.copy, b, n - 1, self.copied_act)


class OutProduct:

    def __init__(self, g, sb, sem, o, wo):
        self.g, self.nc, self.o, self.wo = g, g.nc, o, wo
        self.oT = sb("oT", [P, PAIRS, P])
        self.oT_turned = sem("oT_turned")
        self.oT_copied = sem("oT_copied")
        self.s_ready = sem("s_ready")
        self.s_copied = sem("s_copied") 

    def tensor(self, pe, b, wo=None):
        nc, g = self.nc, self.g
        wo = wo or (lambda c: self.wo[:, c])
        for t in range(TILES):
            pe.wait_ge(self.oT_copied, CREDIT + b * 2 * TILES + 2 * t)
            for c in range(PAIRS):
                ins = nc.tensor.transpose(g.ps[:, 4 + c // 4, (c % 4) * P:(c % 4 + 1) * P],
                                          self.o[:, t, c * P:(c + 1) * P], g.ident[:])
                if c % 4 == 3:
                    ins.then_inc(self.oT_turned, 1)
            pe.wait_ge(self.oT_copied, CREDIT + b * 2 * TILES + 2 * t + 2)
            pe.wait_ge(self.s_copied, CREDIT + b * TILES + t - 1)
            for c in range(PAIRS):
                ins = nc.tensor.matmul(g.ps[:, t % 2, 0:D], self.oT[:, c], wo(c),
                                       start=(c == 0), stop=(c == PAIRS - 1))
            ins.then_inc(self.s_ready, 1)
        pe.wait_ge(self.s_copied, CREDIT + (b + 1) * TILES )

    def scalar(self, act, b):
        for i in range(2 * TILES):
            act.wait_ge(self.oT_turned, CREDIT + b * 2 * TILES + i + 1)
            act.wait_ge(self.s_ready, CREDIT + b * TILES + i // 2)
            self.nc.scalar.copy(self.oT[:, 4 * (i % 2):4 * (i % 2) + 4].rearrange("p c n -> p (c n)"),
                                self.g.ps[:, 4 + i % 2]).then_inc(self.oT_copied, 1)


def l0_attn_stage(g):
    nc = g.nc
    HD = HEADS * DH
    SCALE = 8.0
    with ExitStack() as stack:
        sb, once, sem = scope(nc, stack, "l0a")
        wq = sb("wq", [P, HD])
        wkv = sb("wkv", [P, 2 * DH])
        wo = sb("wo", [P, PAIRS, D])
        gamma = sb("gamma", [P, 1])
        qks = sb("qks", [P, 3])
        nk = sb("nk", [2, 2, DH])
        nsq = sb("nsq", [2, DH])
        nss = sb("nss", [2, 1])
        nrk = sb("nrk", [2, 1])
        nkT = sb("nkT", [P, 2])
        v_null = sb("v_null", [2, DH])
        stats = sb("stats", [P, NT, 6])
        mv = sb("mv", [P, NT, 2])
        rstd = sb("rstd", [P, NT])
        xg = g.gate
        xgT = sb("xgT", [P, NT, D])
        xb = sb("xb", [P, SEQ])
        qb = sb("qb", [P, SEQ])
        kraw = sb("kraw", [P, TILES, DH])
        ksq = sb("ksq", [P, TILES, DH])
        kd = sb("kd", [P, TILES, 2, DH])
        kT = sb("kT", [P, SEQ])
        v = sb("v", [P, TILES, DH])
        sq = sb("sq", [P, 2, 512])
        qn = sb("qn", [P, 2, HD])
        ss = sb("ss", [P, TILES + 1, HEADS])
        rn = sb("rn", [P, TILES + 1, HEADS])
        qT = sb("qT", [P, PAIRS, SEQ])
        o = sb("o", [P, TILES, HD])
        loaded = once("loaded")
        dve_step = once("dve_step")
        pre = once("pre")
        nss_ready = once("nss_ready")
        nrk_ready = once("nrk_ready")
        nk_turned = once("nk_turned")
        nkT_ready = once("nkT_ready")
        var_ready = once("var_ready")
        rstd_ready = once("rstd_ready")
        xg_ready = once("xg_ready")
        xg_turned = once("xg_turned")
        xgT_ready = once("xgT_ready")
        xb_ready = sem("xb_ready")
        kv_ready = sem("kv_ready")
        ss_ready = sem("ss_ready")
        rn_ready = sem("rn_ready")
        kd_ready = sem("kd_ready")
        k_turned = sem("k_turned")
        kT_ready = sem("kT_ready")
        q_ready = sem("q_ready")
        sq_ready = sem("sq_ready")
        sq_summed = sem("sq_summed")
        q_normed = sem("q_normed")
        q_turned = sem("q_turned")
        q_copied = sem("q_copied")
        op = OutProduct(g, sb, sem, o, wo)
        at = Softmax(g, sb, sem,
                     q=lambda h, t: qT[64 * (h % 2):64 * (h % 2) + 64, h // 2, t * P:(t + 1) * P],
                     k=lambda h, n: kT[64 * (h % 2):64 * (h % 2) + 64, 0:n],
                     v=lambda h, c: v[:, c], o=lambda h: o[:, :, h * DH:(h + 1) * DH], width=DH,
                     nulls=lambda h: nkT[64 * (h % 2):64 * (h % 2) + 64, :], v_null=lambda h: v_null[:])
        block = stack.enter_context(nc.Block())
        LOADED = 16 * 11
        Q = 2 * TILES

        @block.sync
        def _(sp):
            start_counts(sp, sem)
            w = g.w
            for dst, src in ((nk[:, 0], w["L0_attn_null_kv"][0]), (nk[:, 1], w["L0_attn_null_kv"][0]),
                             (v_null[:], w["L0_attn_null_kv"][1]), (gamma[:], w["L0_attn_gamma"]),
                             (wkv[:], w["L0_attn_Wkv"]), (wq[:], w["L0_attn_Wq"]), (wo[:], w["L0_attn_Wout"])):
                sp.dma_start(dst, src).then_inc(loaded, 16)
            for i, n in enumerate(("L0_attn_q_scale", "L0_attn_k_scale")):
                for half in range(2):
                    sp.dma_start(qks[half * DH:half * DH + DH, i:i + 1], w[n]).then_inc(loaded, 16)

        @block.vector
        def _(dve):
            ch = Chain(dve, pre)
            for n in range(NT):
                ch.done(nc.vector.bn_stats(stats[:, n], g.xn[:, n]))
            ch.join()
            for n in range(NT):
                ch.done(nc.vector.bn_aggr(mv[:, n], stats[:, n]))
            ch.join()
            nc.vector.tensor_scalar(mv[:, :, 1], mv[:, :, 1], LN_EPS, None, ALU.add).then_inc(var_ready, 1)
            dve.wait_ge(loaded, LOADED)
            ch.done(nc.vector.tensor_tensor(nsq[:], nk[:, 0], nk[:, 0], ALU.mult))
            ch.done(nc.vector.tensor_scalar(qks[:, 2:3], qks[:, 0:1], qks[:, 1:2], SCALE, ALU.mult, ALU.mult))
            ch.join()
            ch.done(nc.vector.tensor_reduce(nss[:], nsq[:], AX_X, ALU.add))
            ch.join()
            nc.vector.tensor_scalar(nss[:], nss[:], 1e-24, None, ALU.max).then_inc(nss_ready, 1)
            dve.wait_ge(nrk_ready, 1)
            ch.done(nc.vector.tensor_scalar(nk[:], nk[:], nrk[:], None, ALU.mult))
            dve.wait_ge(rstd_ready, 1)
            for n in range(NT):
                nc.vector.tensor_scalar(xg[:, n], g.xn[:, n], mv[:, n, 0:1], rstd[:, n:n + 1],
                                        ALU.subtract, ALU.mult).then_inc(xg_ready, 1)
            dve.wait_ge(nk_turned, 1)
            nc.vector.tensor_scalar(nkT[:], g.ps[:, 7, 0:2], qks[:, 2:3], None, ALU.mult).then_inc(nkT_ready, 1)
            assert ch.n == NK_STEPS, ch.n
            with dve.Fori(0, BATCH) as b:
                ch = Chain(dve, dve_step)
                dve.sem_clear(dve_step)
                dve.wait_ge(kv_ready, CREDIT + b + 1)
                kv = g.ps[:, 6].rearrange("p (t c) -> p t c", t=TILES)
                ch.done(nc.vector.tensor_copy(kraw[:], kv[:, :, 0:DH]))
                ch.done(nc.vector.tensor_copy(v[:], kv[:, :, DH:2 * DH]))
                ch.join()
                ch.done(nc.vector.tensor_tensor(ksq[:], kraw[:], kraw[:], ALU.mult))
                ch.join()
                ch.done(nc.vector.tensor_reduce(ss[:, 0, 0:TILES], ksq[:], AX_X, ALU.add))
                ch.join()
                nc.vector.tensor_scalar(ss[:, 0, 0:TILES], ss[:, 0, 0:TILES], 1e-24, None, ALU.max).then_inc(ss_ready, 1)

                def sum_squares(t):
                    for i in (2 * t, 2 * t + 1):
                        dve.wait_ge(sq_ready, CREDIT + b * Q + i + 1)
                        nc.vector.tensor_reduce(ss[:, 1 + t, 8 * (i % 2):8 * (i % 2) + 8],
                                                sq[:, i % 2].rearrange("p (h d) -> p h d", d=DH), AX_X,
                                                ALU.add).then_inc(sq_summed, 1)
                    dve.wait_ge(sq_summed, CREDIT + b * Q + 2 * t + 2)
                    nc.vector.tensor_scalar(ss[:, 1 + t], ss[:, 1 + t], 1e-24, None, ALU.max).then_inc(ss_ready, 1)

                def normalize(t):
                    dve.wait_ge(rn_ready, CREDIT + b * (TILES + 1) + t + 2)
                    dve.wait_ge(q_turned, CREDIT + b * Q + 2 * t - 2)
                    for i in (2 * t, 2 * t + 1):
                        hs = slice(8 * (i % 2), 8 * (i % 2) + 8)
                        nc.vector.tensor_tensor(
                            qn[:, t % 2, 512 * (i % 2):512 * (i % 2) + 512].rearrange("p (h d) -> p h d", d=DH),
                            g.ps[:, i % 4].rearrange("p (h d) -> p h d", d=DH),
                            rn[:, 1 + t, hs].unsqueeze(2).broadcast_to([P, 8, DH]), ALU.mult).then_inc(q_normed, 1)

                sum_squares(0)
                dve.wait_ge(rn_ready, CREDIT + b * (TILES + 1) + 1)
                for half in range(2):
                    nc.vector.tensor_tensor(kd[:, :, half], kraw[:],
                                            rn[:, 0, 0:TILES].unsqueeze(2).broadcast_to([P, TILES, DH]),
                                            ALU.mult).then_inc(kd_ready, 1)
                for t in range(TILES):
                    if t + 1 < TILES:
                        sum_squares(t + 1)
                    normalize(t)
                at.vector(dve, b)
                for t in range(TILES):
                    dve.wait_ge(op.s_ready, CREDIT + b * TILES + t + 1)
                    nc.vector.tensor_copy(g.s[:, bass.ds(b * TILES + t, 1), :].rearrange("p a d -> p (a d)"),
                                          g.ps[:, t % 2, 0:D]).then_inc(op.s_copied, 1)
                ch.join()

        @block.gpsimd
        def _(pool):
            pool.wait_ge(var_ready, 1)
            nc.gpsimd.tensor_tensor(rstd[:], mv[:, :, 1], g.neghalf[:, 0:NT], ALU.pow).then_inc(rstd_ready, 1)
            pool.wait_ge(nss_ready, 1)
            nc.gpsimd.tensor_tensor(nrk[:], nss[:], g.neghalf[0:2, 0:1], ALU.pow).then_inc(nrk_ready, 1)
            pool.wait_ge(xgT_ready, BATCH)
            with pool.Fori(0, BATCH) as b:
                pool.wait_ge(q_ready, CREDIT + b * Q)
                nc.gpsimd.tensor_copy(xb[:], g.xnT[:, bass.ds(b * SEQ, SEQ)]).then_inc(xb_ready, 1)
                nc.gpsimd.tensor_copy(qb[:], xgT[:].rearrange("p t d -> p (t d)")[:, bass.ds(b * SEQ, SEQ)])\
                    .then_inc(xb_ready, 1)
                for j in range(TILES + 1):
                    n = TILES if j == 0 else HEADS
                    pool.wait_ge(ss_ready, CREDIT + b * (TILES + 1) + j + 1)
                    nc.gpsimd.tensor_tensor(rn[:, j, 0:n], ss[:, j, 0:n], g.neghalf[:, 0:n], ALU.pow).then_inc(rn_ready, 1)

        @block.tensor
        def _(pe):
            pe.wait_ge(loaded, LOADED)
            pe.wait_ge(pre, NK_STEPS)
            nc.tensor.transpose(g.ps[:, 7, 0:2], nk[:].rearrange("k a d -> k (a d)"), g.ident[0:2, 0:2]).then_inc(nk_turned, 1)
            for b in range(BATCH):
                if b >= 2:
                    pe.wait_ge(xgT_ready, b - 1)
                pe.wait_ge(xg_ready, (b + 1) * TILES)
                for t in range(TILES):
                    ins = nc.tensor.transpose(g.ps[:, b % 2, t * P:(t + 1) * P], xg[:, b * TILES + t], g.ident[:])
                ins.then_inc(xg_turned, 1)
            pe.wait_ge(xgT_ready, BATCH)
            pe.wait_ge(nkT_ready, 1)

            def query_product(b, t):
                for i in (2 * t, 2 * t + 1):
                    pe.wait_ge(q_normed, CREDIT + b * Q + i - 3)
                    nc.tensor.matmul(g.ps[:, i % 4], qb[:, t * P:(t + 1) * P], wq[:, 512 * (i % 2):512 * (i % 2) + 512],
                                     start=True, stop=True).then_inc(q_ready, 1)

            with pe.Fori(0, BATCH) as b:
                pe.wait_ge(xb_ready, CREDIT + 2 * b + 2)
                for t in range(TILES):
                    ins = nc.tensor.matmul(g.ps[:, 6, t * P:(t + 1) * P], xb[:, t * P:(t + 1) * P], wkv[:],
                                           start=True, stop=True)
                ins.then_inc(kv_ready, 1)
                query_product(b, 0)
                query_product(b, 1)
                pe.wait_ge(kd_ready, CREDIT + 2 * b + 2)
                for t in range(TILES):
                    ins = nc.tensor.transpose(g.ps[:, 7, t * P:(t + 1) * P], kd[:, t].rearrange("p a d -> p (a d)"), g.ident[:])
                ins.then_inc(k_turned, 1)
                for t in range(TILES):
                    for half in range(2):
                        i = 2 * t + half
                        pe.wait_ge(q_normed, CREDIT + b * Q + i + 1)
                        pe.wait_ge(q_copied, CREDIT + b * Q + i - 1)
                        for c in range(4):
                            ins = nc.tensor.transpose(g.ps[:, 4 + half, c * P:(c + 1) * P],
                                                      qn[:, t % 2, (4 * half + c) * P:(4 * half + c + 1) * P], g.ident[:])
                        ins.then_inc(q_turned, 1)
                    if t + 2 < TILES:
                        query_product(b, t + 2)
                pe.wait_ge(q_copied, CREDIT + b * Q + Q)
                pe.wait_ge(kT_ready, CREDIT + b + 1)
                at.tensor(pe, b)
                pe.wait_ge(at.o_ready, CREDIT + (b + 1) * HEADS)
                op.tensor(pe, b)

        @block.scalar
        def _(act):
            act.wait_ge(loaded, LOADED)
            for b in range(BATCH):
                act.wait_ge(xg_turned, b + 1)
                nc.scalar.activation(xgT[:].rearrange("p t d -> p (t d)")[:, b * SEQ:(b + 1) * SEQ], g.ps[:, b % 2],
                                     ACT.Copy, scale=gamma[:]).then_inc(xgT_ready, 1)
            with act.Fori(0, BATCH) as b:
                def copy_queries(t):
                    for half in range(2):
                        act.wait_ge(q_turned, CREDIT + b * Q + 2 * t + half + 1)
                        nc.scalar.copy(qT[:, 4 * half:4 * half + 4, t * P:(t + 1) * P],
                                       g.ps[:, 4 + half].rearrange("p (c n) -> p c n", c=4)).then_inc(q_copied, 1)

                for t in range(TILES):
                    for i in (2 * t, 2 * t + 1):
                        act.wait_ge(q_ready, CREDIT + b * Q + i + 1)
                        act.wait_ge(sq_summed, CREDIT + b * Q + i - 1)
                        nc.scalar.activation(sq[:, i % 2], g.ps[:, i % 4], ACT.Square).then_inc(sq_ready, 1)
                    if t == 1:
                        act.wait_ge(k_turned, CREDIT + b + 1)
                        nc.scalar.activation(kT[:], g.ps[:, 7], ACT.Copy, scale=qks[:, 2:3]).then_inc(kT_ready, 1)
                    if t >= 1:
                        copy_queries(t - 1)
                copy_queries(TILES - 1)
                at.scalar(act, b)
                op.scalar(act, b)


NK_STEPS = 2 * NT + 4


def l1_attn_stage(g):
    nc = g.nc
    HD = HEADS * DH
    with ExitStack() as stack:
        sb, once, sem = scope(nc, stack, "l1a")
        wq, wk, wv = (sb(n, [P, HD]) for n in ("wq", "wk", "wv"))
        wo = sb("wo", [P, PAIRS, D])
        bq, bk = (sb(n, [P, PAIRS]) for n in ("bq", "bk"))
        bv = sb("bv", [P, HD])
        bo = sb("bo", [P, D])
        xb = sb("xb", [P, SEQ])
        qT = sb("qT", [P, PAIRS, SEQ])
        kT = sb("kT", [P, PAIRS, SEQ])
        v = sb("v", [P, TILES, HD])
        o = sb("o", [P, TILES, HD])
        loaded = once("loaded")
        bq_scaled = once("bq_scaled")
        xb_ready = sem("xb_ready")
        proj_ready = sem("proj_ready")
        proj_copied = sem("proj_copied")
        v_ready = sem("v_ready")
        v_copied = sem("v_copied")
        op = OutProduct(g, sb, sem, o, wo)
        at = Softmax(g, sb, sem,
                     q=lambda h, t: qT[64 * (h % 2):64 * (h % 2) + 64, h // 2, t * P:(t + 1) * P],
                     k=lambda h, n: kT[64 * (h % 2):64 * (h % 2) + 64, h // 2, 0:n],
                     v=lambda h, c: v[:, c, h * DH:(h + 1) * DH],
                     o=lambda h: o[:, :, h * DH:(h + 1) * DH], width=DH)
        block = stack.enter_context(nc.Block())

        @block.sync
        def _(sp):
            start_counts(sp, sem)
            for dst, src in ((wq, "L1_attn_Wq"), (wk, "L1_attn_Wk"), (wv, "L1_attn_Wv"), (wo, "L1_attn_Wo"),
                             (bq, "L1_attn_bq"), (bk, "L1_attn_bk")):
                sp.dma_start(dst[:], g.w[src]).then_inc(loaded, 16)
            sp.dma_start(bv[:], g.w["L1_attn_bv"].partition_broadcast(P)).then_inc(loaded, 16)
            sp.dma_start(bo[:], g.w["L1_attn_bo"].partition_broadcast(P)).then_inc(loaded, 16)

        LOADED = 16 * 8

        @block.gpsimd
        def _(pool):
            with pool.Fori(0, BATCH) as b:
                pool.wait_ge(v_ready, CREDIT + b * 2 * TILES)
                nc.gpsimd.tensor_copy(xb[:], g.xnT[:, bass.ds(b * SEQ, SEQ)]).then_inc(xb_ready, 1)

        @block.tensor
        def _(pe):
            pe.wait_ge(loaded, LOADED)
            with pe.Fori(0, BATCH) as b:
                pe.wait_ge(xb_ready, CREDIT + b + 1)
                for i in range(2 * PAIRS):
                    w, c = (wq, wk)[i % 2], i // 2
                    pe.wait_ge(proj_copied, CREDIT + b * 2 * PAIRS + i - 1)
                    nc.tensor.matmul(g.ps[:, i % 2], w[:, c * P:(c + 1) * P], xb[:],
                                     start=True, stop=True).then_inc(proj_ready, 1)
                for i in range(2 * TILES):
                    t, half = i // 2, i % 2
                    pe.wait_ge(v_copied, CREDIT + b * 2 * TILES + i - 1)
                    nc.tensor.matmul(g.ps[:, 2 + i % 2], xb[:, t * P:(t + 1) * P], wv[:, half * 512:half * 512 + 512],
                                     start=True, stop=True).then_inc(v_ready, 1)
                pe.wait_ge(proj_copied, CREDIT + (b + 1) * 2 * PAIRS )
                pe.wait_ge(v_copied, CREDIT + (b + 1) * 2 * TILES)
                at.tensor(pe, b)
                pe.wait_ge(at.o_ready, CREDIT + (b + 1) * HEADS )
                op.tensor(pe, b)

        @block.vector
        def _(dve):
            dve.wait_ge(loaded, LOADED)
            nc.vector.tensor_scalar(bq[:], bq[:], DH ** -0.5, None, ALU.mult).then_inc(bq_scaled, 1)
            with dve.Fori(0, BATCH) as b:
                for i in range(2 * TILES):
                    t, half = i // 2, i % 2
                    dve.wait_ge(v_ready, CREDIT + b * 2 * TILES + i + 1)
                    cols = slice(half * 512, half * 512 + 512)
                    nc.vector.tensor_tensor(v[:, t, cols], g.ps[:, 2 + i % 2], bv[:, cols], ALU.add).then_inc(v_copied, 1)
                at.vector(dve, b)
                for t in range(TILES):
                    dve.wait_ge(op.s_ready, CREDIT + b * TILES + t + 1)
                    nc.vector.tensor_tensor(g.s[:, bass.ds(b * TILES + t, 1), :].rearrange("p a d -> p (a d)"),
                                            g.ps[:, t % 2, 0:D], bo[:], ALU.add).then_inc(op.s_copied, 1)

        @block.scalar
        def _(act):
            act.wait_ge(bq_scaled, 1)
            with act.Fori(0, BATCH) as b:
                for i in range(2 * PAIRS):
                    c = i // 2
                    dst, bias, scale = ((qT, bq, DH ** -0.5), (kT, bk, 1.0))[i % 2]
                    act.wait_ge(proj_ready, CREDIT + b * 2 * PAIRS + i + 1)
                    nc.scalar.activation(dst[:, c], g.ps[:, i % 2], ACT.Identity, bias=bias[:, c:c + 1],
                                         scale=scale).then_inc(proj_copied, 1)
                at.scalar(act, b)
                op.scalar(act, b)


STATES, TAPS, DT_RANK, HALF = 16, 4, 4, D // 2


def l2_attn_stage(g):
    nc = g.nc
    PAD = TAPS - 1
    with ExitStack() as stack:
        sb, once, sem = scope(nc, stack, "l2a")
        par = {n: sb(n, [P, 2, c]) for n, c in (("win", 2 * P), ("wx", DT_RANK + 2 * STATES), ("wout", HALF),
                                                ("wconv", TAPS), ("alog", STATES), ("vec", 3))}
        wdt = sb("wdt", [DT_RANK, 2, P])
        A = sb("A", [P, 2, STATES])
        lnp = sb("lnp", [P, 2])
        pick = sb("pick", [96, 2 * STATES])
        sel = sb("sel", [96, 2 * STATES, P], BF16)
        stats = sb("stats", [P, NT, 6])
        mv = sb("mv", [P, NT, 2])
        rstd = sb("rstd", [P, NT])
        hn = g.gate
        hT = sb("hT", [P, BATCH * SEQ])
        xp = sb("xp", [P, SEQ + 2 * PAD])
        cv = sb("cv", [P, TAPS, SEQ])
        xc = sb("xc", [P, SEQ])
        zs = sb("zs", [P, SEQ])
        dt4 = sb("dt4", [DT_RANK, SEQ])
        sp_a = sb("sp_a", [P, SEQ])
        sp_e = sb("sp_e", [P, SEQ])
        sp_l = sb("sp_l", [P, SEQ])
        sp_m = sb("sp_m", [P, SEQ])
        dt = sb("dt", [P, SEQ])
        dtx = sb("dtx", [P, SEQ])
        rest = sb("rest", [2 * STATES, 2, SEQ])
        part = sb("part", [2 * STATES, 3, SEQ], BF16)
        split = sb("split", [96, SEQ], BF16)
        dA = sb("dA", [P, 2, SEQ])
        dBx = sb("dBx", [P, 2, SEQ])
        hs = sb("hs", [P, 2, SEQ])
        hc = sb("hc", [P, 2, SEQ])
        yg = sb("yg", [P, SEQ])
        y = sb("y", [P, SEQ])
        res = sb("res", [P, TILES, D])
        loaded = once("loaded")
        pre = once("pre")
        var_ready = once("var_ready")
        rstd_ready = once("rstd_ready")
        hn_ready = once("hn_ready")
        h_turned = once("h_turned")
        hT_ready = once("hT_ready")
        A_ready = once("A_ready")
        dve_step = once("dve_step")
        act_step = once("act_step")
        in_ready = sem("in_ready")
        xp_ready = sem("xp_ready")
        zs_ready = sem("zs_ready")
        conv_ready = sem("conv_ready")
        xc_ready = sem("xc_ready")
        dbc_ready = sem("dbc_ready")
        dt4_ready = sem("dt4_ready")
        dt_product = sem("dt_product")
        soft_ready = sem("soft_ready")
        dt_ready = sem("dt_ready")
        split_ready = sem("split_ready")
        bc_ready = sem("bc_ready")
        dA_ready = sem("dA_ready")
        dBx_ready = sem("dBx_ready")
        hs_ready = sem("hs_ready")
        hc_ready = sem("hc_ready")
        y_added = sem("y_added")
        y_ready = sem("y_ready")
        out_ready = sem("out_ready")
        res_ready = sem("res_ready")
        s_ready = sem("s_ready")
        block = stack.enter_context(nc.Block())
        names = ("Win", "Wx", "Wout", "Wconv", "Alog", "vec", "Wdt")
        LOADED = 16 * (2 * len(names) + 2)
        N = STATES

        def at(b, u, per, k):
            return CREDIT + u * per + k + b * 2 * per

        @block.sync
        def _(sp):
            start_counts(sp, sem)
            for u in range(2):
                for n in names:
                    dst = wdt[:, u] if n == "Wdt" else par[n.lower()][:, u]
                    sp.dma_start(dst, g.w[f"L2_m{u + 1}_{n}"]).then_inc(loaded, 16)
            sp.dma_start(lnp[:], g.w["L2_attn_ln"]).then_inc(loaded, 16)
            sp.dma_start(pick[:], g.c["pick"]).then_inc(loaded, 16)

        @block.gpsimd
        def _(pool):
            pool.wait_ge(var_ready, 1)
            nc.gpsimd.tensor_tensor(rstd[:], mv[:, :, 1], g.neghalf[:, 0:NT], ALU.pow).then_inc(rstd_ready, 1)

        @block.tensor
        def _(pe):
            for b in range(BATCH):
                if b >= 2:
                    pe.wait_ge(hT_ready, b - 1)
                pe.wait_ge(hn_ready, (b + 1) * TILES)
                for t in range(TILES):
                    ins = nc.tensor.transpose(g.ps[:, b % 2, t * P:(t + 1) * P], hn[:, b * TILES + t], g.ident[:])
                ins.then_inc(h_turned, 1)
            pe.wait_ge(hT_ready, BATCH)
            pe.wait_ge(loaded, LOADED)
            pe.wait_ge(pre, MAMBA_PRE)
            with pe.Fori(0, BATCH) as b:
                for u in range(2):
                    pe.wait_ge(out_ready, at(b, u, 1, 0))
                    for c in range(2):
                        ins = nc.tensor.matmul(g.ps[:, c], par["win"][:, u, c * P:(c + 1) * P],
                                               hT[:, bass.ds(b * SEQ, SEQ)], start=True, stop=True)
                    ins.then_inc(in_ready, 1)
                    pe.wait_ge(xc_ready, at(b, u, 1, 1))
                    pe.wait_ge(zs_ready, at(b, u, 1, 1))
                    nc.tensor.matmul(g.ps[0:DT_RANK, 2], par["wx"][:, u, 0:DT_RANK], xc[:], start=True, stop=True)
                    nc.tensor.matmul(g.ps[0:2 * N, 3], par["wx"][:, u, DT_RANK:], xc[:],
                                     start=True, stop=True).then_inc(dbc_ready, 1)
                    pe.wait_ge(dt4_ready, at(b, u, 1, 1))
                    nc.tensor.matmul(g.ps[:, 4], wdt[:, u], dt4[:], start=True, stop=True).then_inc(dt_product, 1)
                    pe.wait_ge(split_ready, at(b, u, 1, 1))

                    def spread(n):
                        pe.wait_ge(hc_ready, at(b, u, N, n - 1))
                        nc.tensor.matmul(g.ps[:, n % 2], sel[:, n], split[:], start=True, stop=True)
                        nc.tensor.matmul(g.ps[:, 2 + n % 2], sel[:, N + n], split[:],
                                         start=True, stop=True).then_inc(bc_ready, 1)

                    spread(0)
                    for n in range(N):
                        if n + 1 < N:
                            spread(n + 1)
                        pe.wait_ge(hc_ready, at(b, u, N, n + 1))
                        nc.tensor.matmul(g.ps[:, 5], g.ident[:], hc[:, n % 2], start=(n == 0),
                                         stop=(n == N - 1)).then_inc(y_added, 1)
                    pe.wait_ge(y_ready, at(b, u, 1, 1))
                    if u == 0:
                        pe.wait_ge(res_ready, CREDIT + b)
                    for t in range(TILES):
                        c0 = t * D + u * HALF
                        ins = nc.tensor.matmul(g.ps[:, 6, c0:c0 + HALF], y[:, t * P:(t + 1) * P], par["wout"][:, u],
                                               start=True, stop=True)
                    ins.then_inc(out_ready, 1)

        @block.vector
        def _(dve):
            ch = Chain(dve, pre)
            for n in range(NT):
                ch.done(nc.vector.bn_stats(stats[:, n], g.xn[:, n]))
            ch.join()
            for n in range(NT):
                ch.done(nc.vector.bn_aggr(mv[:, n], stats[:, n]))
            ch.join()
            nc.vector.tensor_scalar(mv[:, :, 1], mv[:, :, 1], LN_EPS, None, ALU.add).then_inc(var_ready, 1)
            ch.done(nc.vector.memset(xp[:], 0.0))
            dve.wait_ge(loaded, LOADED)
            ch.done(nc.vector.tensor_copy(sel[:], pick[:].unsqueeze(2).broadcast_to([96, 2 * N, P])))
            dve.wait_ge(A_ready, 1)
            ch.done(nc.vector.tensor_scalar(A[:], A[:], -1.0, None, ALU.mult))
            dve.wait_ge(rstd_ready, 1)
            for n in range(NT):
                nc.vector.tensor_scalar(hn[:, n], g.xn[:, n], mv[:, n, 0:1], rstd[:, n:n + 1],
                                        ALU.subtract, ALU.mult).then_inc(hn_ready, 1)
            ch.join()
            assert ch.n == MAMBA_PRE
            with dve.Fori(0, BATCH) as b:
                for u in range(2):
                    ch = Chain(dve, dve_step)
                    dve.sem_clear(dve_step)
                    dve.wait_ge(xp_ready, at(b, u, 1, 1))
                    for k in range(TAPS):
                        k0 = 2 * PAD - k if u else k
                        w = par["wconv"][:, u, k:k + 1]
                        if k == 0:
                            ch.done(nc.vector.tensor_scalar(cv[:, 0], xp[:, k0:k0 + SEQ], w, None, ALU.mult))
                        else:
                            ch.join()
                            ins = nc.vector.scalar_tensor_tensor(cv[:, k], xp[:, k0:k0 + SEQ], w, cv[:, k - 1],
                                                                 ALU.mult, ALU.add)
                            if k < TAPS - 1:
                                ch.done(ins)
                    ins.then_inc(conv_ready, 1)
                    dve.wait_ge(dbc_ready, at(b, u, 1, 1))
                    rows = g.ps[0:2 * N, 3]
                    ch.done(nc.vector.tensor_copy(part[:, 0], rows))
                    ch.join()
                    ch.done(nc.vector.tensor_tensor(rest[:, 0], rows, part[:, 0], ALU.subtract))
                    ch.join()
                    ch.done(nc.vector.tensor_copy(part[:, 1], rest[:, 0]))
                    ch.join()
                    ch.done(nc.vector.tensor_tensor(rest[:, 1], rest[:, 0], part[:, 1], ALU.subtract))
                    ch.join()
                    ch.done(nc.vector.tensor_copy(split[64:96], rest[:, 1]))
                    ch.done(nc.vector.tensor_copy(split[32:64], part[:, 1]))
                    ch.join()
                    nc.vector.tensor_copy(split[0:32], part[:, 0]).then_inc(split_ready, 1)
                    dve.wait_ge(dt_product, at(b, u, 1, 1))
                    dve.wait_ge(soft_ready, at(b, u, 1, 1))
                    ch.done(nc.vector.tensor_scalar(sp_m[:], g.ps[:, 4], par["vec"][:, u, 1:2], 0.0, ALU.add, ALU.max))
                    ch.join()
                    nc.vector.tensor_tensor(dt[:], sp_m[:], sp_l[:], ALU.add).then_inc(dt_ready, 1)
                    dve.wait_ge(dt_ready, at(b, u, 1, 1))
                    ch.done(nc.vector.tensor_tensor(dtx[:], dt[:], xc[:], ALU.mult))
                    ch.join()
                    way = slice(None, None, -1) if u else slice(None)
                    for n in range(N):
                        dve.wait_ge(bc_ready, at(b, u, N, n + 1))
                        nc.vector.tensor_tensor(dBx[:, n % 2], g.ps[:, n % 2], dtx[:], ALU.mult).then_inc(dBx_ready, 1)
                        dve.wait_ge(dBx_ready, at(b, u, N, n + 1))
                        dve.wait_ge(dA_ready, at(b, u, N, n + 1))
                        nc.vector.tensor_tensor_scan(hs[:, n % 2, way], dA[:, n % 2, way], dBx[:, n % 2, way], 0.0,
                                                     ALU.mult, ALU.add).then_inc(hs_ready, 1)
                        dve.wait_ge(hs_ready, at(b, u, N, n + 1))
                        dve.wait_ge(y_added, at(b, u, N, n - 1))
                        nc.vector.tensor_tensor(hc[:, n % 2], g.ps[:, 2 + n % 2], hs[:, n % 2], ALU.mult).then_inc(hc_ready, 1)
                    dve.wait_ge(y_added, at(b, u, N, N))
                    ch.done(nc.vector.scalar_tensor_tensor(yg[:], xc[:], par["vec"][:, u, 2:3], g.ps[:, 5],
                                                           ALU.mult, ALU.add))
                    ch.join()
                    dve.wait_ge(out_ready, at(b, u, 1, 0))
                    nc.vector.tensor_tensor(y[:, way], yg[:], zs[:], ALU.mult).then_inc(y_ready, 1)
                dve.wait_ge(out_ready, at(b, 1, 1, 1))
                dve.wait_ge(s_ready, CREDIT + b)
                nc.vector.tensor_tensor(res[:], g.ps[:, 6].rearrange("p (t d) -> p t d", t=TILES),
                                        g.xn[:, bass.ds(b * TILES, TILES), :], ALU.add).then_inc(res_ready, 1)

        @block.scalar
        def _(act):
            act.wait_ge(loaded, LOADED)
            nc.scalar.activation(A[:], par["alog"][:], ACT.Exp).then_inc(A_ready, 1)
            for b in range(BATCH):
                act.wait_ge(h_turned, b + 1)
                nc.scalar.activation(hT[:, b * SEQ:(b + 1) * SEQ], g.ps[:, b % 2], ACT.Identity,
                                     bias=lnp[:, 1:2], scale=lnp[:, 0:1]).then_inc(hT_ready, 1)
            act.wait_ge(pre, MAMBA_PRE)
            with act.Fori(0, BATCH) as b:
                for u in range(2):
                    ch = Chain(act, act_step)
                    act.sem_clear(act_step)
                    act.wait_ge(in_ready, at(b, u, 1, 1))
                    nc.scalar.copy(xp[:, PAD:PAD + SEQ], g.ps[:, 0]).then_inc(xp_ready, 1)
                    act.wait_ge(y_ready, at(b, u, 1, 0))
                    nc.scalar.activation(zs[:], g.ps[:, 1], ACT.Silu).then_inc(zs_ready, 1)
                    act.wait_ge(conv_ready, at(b, u, 1, 1))
                    nc.scalar.activation(xc[:], cv[:, TAPS - 1], ACT.Silu, bias=par["vec"][:, u, 0:1]).then_inc(xc_ready, 1)
                    act.wait_ge(dbc_ready, at(b, u, 1, 1))
                    nc.scalar.copy(dt4[:], g.ps[0:DT_RANK, 2]).then_inc(dt4_ready, 1)
                    act.wait_ge(dt_product, at(b, u, 1, 1))
                    ch.done(nc.scalar.activation(sp_a[:], g.ps[:, 4], ACT.Abs, bias=par["vec"][:, u, 1:2]))
                    ch.join()
                    ch.done(nc.scalar.activation(sp_e[:], sp_a[:], ACT.Exp, scale=-1.0))
                    ch.join()
                    nc.scalar.activation(sp_l[:], sp_e[:], ACT.Ln, bias=1.0).then_inc(soft_ready, 1)
                    act.wait_ge(dt_ready, at(b, u, 1, 1))
                    for n in range(N):
                        act.wait_ge(hs_ready, at(b, u, N, n - 1))
                        nc.scalar.activation(dA[:, n % 2], dt[:], ACT.Exp, scale=A[:, u, n:n + 1]).then_inc(dA_ready, 1)
                act.wait_ge(res_ready, CREDIT + b + 1)
                nc.scalar.activation(g.s[:, bass.ds(b * TILES, TILES), :], res[:], ACT.Gelu).then_inc(s_ready, 1)


MAMBA_PRE = 2 * NT + 3


DEPTH, WINDOW, DI = 6, 32, int(D * 4 * 2 / 3)


def l2_ffn_stage(g):
    nc = g.nc
    HD = HEADS * DH
    QB = 64
    KW = WINDOW + QB
    QBS = P // QB
    QUAD = 4
    QUADS = PAIRS // QUAD
    PER = QBS * QUADS
    STEPS2 = TILES * PER
    CH = [(0, P), (P, P), (2 * P, DI - 2 * P)]
    NLOAD = 12
    ITERATIONS = DEPTH * BATCH
    LOG_BATCH = BATCH.bit_length() - 1
    NONE = (None, None)
    assert BATCH == 1 << LOG_BATCH
    with ExitStack() as stack:
        sb, once, sem = scope(nc, stack, "l2f")
        wqkv = sb("wqkv", [P, 2, 3 * HD])
        wo = sb("wo", [P, 2, PAIRS, D])
        w1 = sb("w1", [P, 2, 2 * DI])
        w2 = sb("w2", [P, 2, 3, D])
        b1 = sb("b1", [P, 2, 2 * DI])
        b2 = sb("b2", [P, 2, D])
        qks = sb("qks", [P, 2, 2, DH])
        lnp = sb("lnp", [P, DEPTH + 1, 2])
        lnd = sb("lnd", [P, 2])
        rope = sb("rope", [P, 2, 2, TILES, DH])
        rot = sb("rot", [P, 2, 2, TILES, DH])
        band_f = sb("band_f", [P, 2, KW])
        band = sb("band", [P, 2, KW], BF16)
        step_down = sb("step_down", [P, 2, P])
        yb = sb("yb", [P, TILES, D])
        xsT = sb("xsT", [P, WINDOW + SEQ + 1])
        nrm = g.xnT[:].rearrange("p (k c) -> p k c", k=2)
        swp = g.xn[:].rearrange("p t d -> p (t d)").rearrange("p (k c) -> p k c", k=2)
        cosd = sb("cosd", [P, 2, HD])
        qz = sb("qz", [P, PAIRS, 2, QBS, 2, QB])
        kT = sb("kT", [P, PAIRS, WINDOW + SEQ])
        vw = sb("vw", [KW, 2 * QBS, HD])
        p = sb("p", [P, 2, QUAD, KW])
        pT = sb("pT", [KW, 2, QUAD, P])
        oT = sb("oT", [P, PAIRS, 2, P])
        ss = sb("ss", [P, 2, HEADS])
        rn = sb("rn", [P, 2, HEADS])
        negmax = sb("negmax", [P, STEPS2 * QUAD])
        rowsum = sb("rowsum", [P, STEPS2 * QUAD])
        rinv = sb("rinv", [P, STEPS2 * QUAD])
        stats = sb("stats", [P, 2, 6])
        mv = sb("mv", [P, 2])
        rstd = sb("rstd", [P, 1])
        xn2 = sb("xn2", [P, D])
        xnT2 = sb("xnT2", [P, P])
        ha = sb("ha", [P, DI])
        hg = sb("hg", [P, DI])
        hh = sb("hh", [P, DI])
        hT = sb("hT", [P, 3, P])
        yt = sb("yt", [P, D])
        const_loaded = once("const_loaded")
        loaded = once("loaded")
        y_started = once("y_started")
        band_ready = once("band_ready")
        pad_ready = once("pad_ready")
        dve_step = once("dve_step")
        act_step = once("act_step")
        rot_ready = sem("rot_ready")
        yb_ready = sem("yb_ready")
        lnd_ready = sem("lnd_ready")
        y_turned = sem("y_turned")
        xs_ready = sem("xs_ready")
        projected = sem("projected")
        sq_ready = sem("sq_ready")
        ss_ready = sem("ss_ready")
        rn_ready = sem("rn_ready")
        nrm_ready = sem("nrm_ready")
        cos_ready = sem("cos_ready")
        rotated = sem("rotated")
        qk_turned = sem("qk_turned")
        q_copied = sem("q_copied")
        k_copied = sem("k_copied")
        v_copied = sem("v_copied")
        scores_ready = sem("scores_ready")
        negmax_ready = sem("negmax_ready")
        probs_ready = sem("probs_ready")
        rinv_ready = sem("rinv_ready")
        scaled = sem("scaled")
        turned = sem("turned")
        pT_copied = sem("pT_copied")
        pv_done = sem("pv_done")
        oT_copied = sem("oT_copied")
        mixed = sem("mixed")
        y_mixed = sem("y_mixed")
        shifted = sem("shifted")
        moments = sem("moments")
        rstd_ready = sem("rstd_ready")
        xn2_ready = sem("xn2_ready")
        xn2_turned = sem("xn2_turned")
        xnT2_ready = sem("xnT2_ready")
        hid_ready = sem("hid_ready")
        hg_ready = sem("hg_ready")
        ha_ready = sem("ha_ready")
        gelu_ready = sem("gelu_ready")
        hh_ready = sem("hh_ready")
        hh_turned = sem("hh_turned")
        hT_ready = sem("hT_ready")
        ff_ready = sem("ff_ready")
        yt_ready = sem("yt_ready")
        y_ready = sem("y_ready")
        y_final = once("y_final")

        def at(it, per, k):
            return CREDIT + k + it * per

        def weight_slot(it):
            return (it >> LOG_BATCH) & 1

        def slots(it, first=False, last=False):
            for t in range(TILES):
                ahead = (it, t + 1) if t + 1 < TILES else NONE if last else (it + 1, 0)
                behind = (it, t - 1) if t else NONE if first else (it - 1, TILES - 1)
                yield ahead, (it, t), behind

        def all_iterations(eng, slot, end=lambda: None):
            slot((0, 0), NONE, NONE)
            for stages in slots(0, first=True):
                slot(*stages)
            end()
            with eng.Fori(1, ITERATIONS - 1) as it:
                for stages in slots(it):
                    slot(*stages)
                end()
            for stages in slots(ITERATIONS - 1, last=True):
                slot(*stages)
            slot(NONE, NONE, (ITERATIONS - 1, TILES - 1))
            end()

        def banks(b0, n):
            return g.ps[:, b0:b0 + n].rearrange("p a c -> p (a c)")

        def step_of(n):
            return n // PER, n % PER // QUADS, n % QUADS

        block = stack.enter_context(nc.Block())

        @block.sync
        def _(sp):
            start_counts(sp, sem)
            sp.dma_start(rope[:], g.c["rope"]).then_inc(const_loaded, 16)
            sp.dma_start(band_f[:], g.c["band"]).then_inc(const_loaded, 16)
            sp.dma_start(step_down[:], g.c["step_down"]).then_inc(const_loaded, 16)
            sp.dma_start(lnp[:, 0:DEPTH], g.w["L2_ffn_ln"]).then_inc(const_loaded, 16)
            for d in range(DEPTH):
                s = d % 2
                if d >= 1:
                    sp.wait_ge(loaded, 16 * NLOAD * d)
                if d >= 2:
                    sp.wait_ge(y_ready, CREDIT + (d - 1) * BATCH * TILES)
                for i, n in enumerate(("q_scale", "k_scale")):
                    sp.dma_start(qks[:, s, i], g.w[f"L2_ffn_{n}"][d].partition_broadcast(P)).then_inc(loaded, 16)
                for c in range(3):
                    sp.dma_start(wqkv[:, s, c * HD:(c + 1) * HD],
                                 g.w["L2_ffn_Wqkv"][d, :, c * HD:(c + 1) * HD]).then_inc(loaded, 16)
                sp.dma_start(wo[:, s], g.w["L2_ffn_Wo"][d]).then_inc(loaded, 16)
                sp.dma_start(w1[:, s], g.w["L2_ffn_W1"][d]).then_inc(loaded, 16)
                for c, (r0, rows) in enumerate(CH):
                    sp.dma_start(w2[0:rows, s, c], g.w["L2_ffn_W2"][d, r0:r0 + rows]).then_inc(loaded, 16)
                sp.dma_start(b1[:, s], g.w["L2_ffn_b1"][d].partition_broadcast(P)).then_inc(loaded, 16)
                sp.dma_start(b2[:, s], g.w["L2_ffn_b2"][d].partition_broadcast(P)).then_inc(loaded, 16)

        @block.gpsimd
        def _(pool):
            def inverse_norms(it, t, k):
                if t is not None:
                    pool.wait_ge(ss_ready, at(it, 2 * TILES, 2 * t + k + 1))
                    nc.gpsimd.tensor_tensor(rn[:, k], ss[:, k], g.neghalf[:, 0:HEADS], ALU.pow).then_inc(rn_ready, 1)

            def cosines(it, t, k):
                if t is not None:
                    pool.wait_ge(rot_ready, at(it, 6, 6))
                    pool.wait_ge(nrm_ready, at(it, 2 * TILES, 2 * t + k + 1))
                    nc.gpsimd.tensor_tensor(
                        cosd[:, k].rearrange("p (h d) -> p h d", d=DH), nrm[:, k].rearrange("p (h d) -> p h d", d=DH),
                        rot[:, k, 0, t].unsqueeze(1).broadcast_to([P, HEADS, DH]), ALU.mult).then_inc(cos_ready, 1)

            def scaled_rotary(it, t):
                if t == 0:
                    pool.wait_ge(loaded, (it >> LOG_BATCH) * (16 * NLOAD) + 16 * NLOAD)
                    pool.wait_ge(rotated, at(it, 2 * TILES, 0))
                    for k in range(2):
                        sc = qks[:, bass.ds(weight_slot(it), 1), k].broadcast_to([P, TILES, DH])
                        nc.gpsimd.tensor_tensor(rot[:, k, 0], rope[:, k, 0], sc, ALU.mult).then_inc(rot_ready, 1)
                        for to, frm in ((0, 32), (32, 0)):
                            sc = qks[:, bass.ds(weight_slot(it), 1), k, frm:frm + 32].broadcast_to([P, TILES, 32])
                            nc.gpsimd.tensor_tensor(rot[:, k, 1, :, to:to + 32], rope[:, k, 1, :, to:to + 32],
                                                    sc, ALU.mult).then_inc(rot_ready, 1)

            def inverse_deviation(it, t):
                if t is not None:
                    pool.wait_ge(moments, at(it, TILES, t + 1))
                    nc.gpsimd.tensor_tensor(rstd[:], mv[:, 1:2], g.neghalf[:, 0:1], ALU.pow).then_inc(rstd_ready, 1)

            def slot(ahead, now, behind):
                inverse_deviation(*behind)
                inverse_norms(*ahead, 0)
                inverse_norms(*ahead, 1)
                scaled_rotary(*ahead)
                cosines(*ahead, 0)
                cosines(*ahead, 1)

            pool.wait_ge(const_loaded, 64)
            all_iterations(pool, slot)

        @block.tensor
        def _(pe):
            pe.wait_ge(band_ready, 1)

            def turn_y(it, t):
                if t is not None:
                    pe.wait_ge(yb_ready, at(it, TILES, t + 1))
                    pe.wait_ge(yt_ready, at(it, TILES, t - 2))
                    nc.tensor.transpose(g.ps[:, 7, 0:P], yb[:, t], g.ident[:]).then_inc(y_turned, 1)

            def project(it, t, k):
                if t is None:
                    return
                if k == 0:
                    if t == 0:
                        pe.wait_ge(loaded, (it >> LOG_BATCH) * (16 * NLOAD) + 16 * NLOAD)
                    pe.wait_ge(xs_ready, at(it, 2 * TILES, 2 * t + 2))
                    pe.wait_ge(q_copied, at(it, 2 * TILES, 2 * t))
                elif k == 1:
                    pe.wait_ge(k_copied, at(it, TILES, t))
                else:
                    pe.wait_ge(nrm_ready, at(it, 2 * TILES, 2 * t + k - 1))
                if k < 2:
                    x, rows, c0 = xsT[:, WINDOW + t * P:WINDOW + (t + 1) * P], P, k * HD
                else:
                    w = QBS * t + k - 2
                    x, rows, c0 = xsT[:, w * QB:w * QB + KW], KW, 2 * HD
                for hf in range(2):
                    ins = nc.tensor.matmul(g.ps[0:rows, 2 * (k % 2) + hf], x,
                                           wqkv[:, bass.ds(weight_slot(it), 1), c0 + hf * 512:c0 + (hf + 1) * 512]
                                           .rearrange("p a c -> p (a c)"), start=True, stop=True)
                ins.then_inc(projected, 1)

            def turn_qk(it, t, k):
                if t is None:
                    return
                pe.wait_ge(rotated, at(it, 2 * TILES, 2 * t + k + 1))
                pe.wait_ge(v_copied, at(it, 2 * TILES, 2 * t + k + 1))
                for c in range(PAIRS):
                    ins = nc.tensor.transpose(g.ps[:, 2 * k + c // 4, (c % 4) * P:(c % 4 + 1) * P],
                                              cosd[:, k, c * P:(c + 1) * P], g.ident[:])
                ins.then_inc(qk_turned, 1)

            def scores(it, t, i):
                if t is None:
                    return
                n = PER * t + i
                _, j, quad = step_of(n)
                if i == 0:
                    pe.wait_ge(q_copied, at(it, 2 * TILES, 2 * t + 2))
                    pe.wait_ge(k_copied, at(it, TILES, t + 1))
                pe.wait_ge(probs_ready, at(it, STEPS2, n))
                out = g.ps[:, 4, 0:QUAD * KW]
                w = QBS * t + j
                nc.tensor.matmul(out, g.identb[:], band[:, 1 if w else 0].unsqueeze(1).broadcast_to([P, QUAD, KW]),
                                 start=True, stop=False)
                for c in range(QUAD):
                    pair = quad * QUAD + c
                    ins = nc.tensor.matmul(out[:, c * KW:(c + 1) * KW],
                                           qz[:, pair, t % 2, j].rearrange("p h q -> p (h q)"),
                                           kT[:, pair, w * QB:w * QB + KW], start=False, stop=(c == QUAD - 1))
                ins.then_inc(scores_ready, 1)

            def turn(it, t, i):
                if t is None:
                    return
                n = PER * t + i
                pe.wait_ge(scaled, at(it, STEPS2, n + 1))
                pe.wait_ge(pT_copied, at(it, STEPS2, n))
                for c in range(QUAD):
                    ins = nc.tensor.transpose(g.ps[0:KW, 5, c * P:(c + 1) * P], p[:, n % 2, c], g.ident[:])
                ins.then_inc(turned, 1)

            def pv(it, t, i):
                if t is None:
                    return
                n = PER * t + i
                _, j, quad = step_of(n)
                if i == 0:
                    pe.wait_ge(v_copied, at(it, 2 * TILES, 2 * t + 2))
                    pe.wait_ge(y_mixed, at(it, TILES, t))
                pe.wait_ge(pT_copied, at(it, STEPS2, n + 1))
                pe.wait_ge(oT_copied, at(it, 2 * STEPS2, 2 * n))
                for c in range(QUAD):
                    pair = quad * QUAD + c
                    ins = nc.tensor.matmul(g.ps[:, 6, c * P:(c + 1) * P],
                                           vw[:, (QBS * t + j) % (2 * QBS), pair * P:(pair + 1) * P],
                                           pT[:, n % 2, c], start=True, stop=True)
                ins.then_inc(pv_done, 1)

            def mix(it, t):
                if t is None:
                    return
                pe.wait_ge(oT_copied, at(it, 2 * STEPS2, 2 * PER * (t + 1)))
                for c in range(PAIRS):
                    ins = nc.tensor.matmul(g.ps[:, 6, 0:D], oT[:, c, t % 2],
                                           wo[:, bass.ds(weight_slot(it), 1), c].rearrange("p a c -> p (a c)"),
                                           start=(c == 0), stop=(c == PAIRS - 1))
                ins.then_inc(mixed, 1)

            def shift(it, t):
                if t is None:
                    return
                pe.wait_ge(y_mixed, at(it, TILES, t + 1))
                last = isinstance(it, int) and it == ITERATIONS - 1
                pe.wait_ge(xs_ready, at(it, 2 * TILES, 2 * min(t + 3, TILES if last else t + 3)))
                ins = nc.tensor.matmul(g.ps[:, 7, 0:D // 2], step_down[:, 0], yb[:, t, D // 2:D],
                                       start=True, stop=(t == 0))
                if t:
                    ins = nc.tensor.matmul(g.ps[:, 7, 0:D // 2], step_down[:, 1], yb[:, t - 1, D // 2:D],
                                           start=False, stop=True)
                ins.then_inc(shifted, 1)

            def turn_xn2(it, t):
                if t is None:
                    return
                pe.wait_ge(xn2_ready, at(it, 2 * TILES, 2 * t + 2))
                nc.tensor.transpose(g.ps[:, 7, 0:P], xn2[:], g.ident[:]).then_inc(xn2_turned, 1)

            def hidden(it, t, hf):
                if t is None:
                    return
                if hf:
                    pe.wait_ge(xnT2_ready, at(it, TILES, t + 1))
                else:
                    pe.wait_ge(hg_ready, at(it, TILES, t + 1))
                nc.tensor.matmul(g.ps[:, 7, 0:DI], xnT2[:],
                                 w1[:, bass.ds(weight_slot(it), 1), hf * DI:(hf + 1) * DI].rearrange("p a c -> p (a c)"),
                                 start=True, stop=True).then_inc(hid_ready, 1)

            def turn_hidden(it, t):
                if t is None:
                    return
                pe.wait_ge(hh_ready, at(it, TILES, t + 1))
                for c, (r0, rows) in enumerate(CH):
                    ins = nc.tensor.transpose(g.ps[0:rows, 7, c * P:(c + 1) * P], hh[:, r0:r0 + rows], g.ident[:])
                ins.then_inc(hh_turned, 1)

            def feed(it, t):
                if t is None:
                    return
                pe.wait_ge(hT_ready, at(it, 2 * TILES, 2 * t + 2))
                for c, (r0, rows) in enumerate(CH):
                    ins = nc.tensor.matmul(g.ps[:, 7, 0:D], hT[0:rows, c],
                                           w2[0:rows, bass.ds(weight_slot(it), 1), c].rearrange("p a c -> p (a c)"),
                                           start=(c == 0), stop=(c == 2))
                ins.then_inc(ff_ready, 1)

            def slot(ahead, now, behind):
                scores(*now, 0)
                turn_y(*ahead)
                shift(*behind)
                project(*ahead, 0)
                scores(*now, 1)
                turn(*now, 0)
                turn_xn2(*behind)
                project(*ahead, 1)
                scores(*now, 2)
                turn(*now, 1)
                pv(*now, 0)
                hidden(*behind, 1)
                project(*ahead, 2)
                scores(*now, 3)
                turn(*now, 2)
                pv(*now, 1)
                hidden(*behind, 0)
                project(*ahead, 3)
                turn(*now, 3)
                pv(*now, 2)
                turn_hidden(*behind)
                turn_qk(*ahead, 0)
                pv(*now, 3)
                feed(*behind)
                turn_qk(*ahead, 1)
                mix(*now)

            all_iterations(pe, slot)

        @block.vector
        def _(dve):
            nc.vector.tensor_copy(g.gate[:], g.xn[:]).then_inc(y_started, 1)
            nc.vector.memset(xsT[:], 0.0)
            nc.vector.memset(qz[:], 0.0)
            nc.vector.memset(kT[:], 0.0).then_inc(pad_ready, 1)
            dve.wait_ge(const_loaded, 64)
            nc.vector.tensor_copy(band[:], band_f[:]).then_inc(band_ready, 1)
            dve.wait_ge(y_started, 1)
            dve.wait_ge(pad_ready, 1)
            SW = ((0, 32), (32, 0))

            def heads(x):
                return x.rearrange("p (h d) -> p h d", d=DH)

            def fetch(it, t):
                if t is None:
                    return
                dve.wait_ge(y_ready, at(it, TILES, t - 2))
                nc.vector.tensor_copy(yb[:, t], g.gate[:, bass.ds((it & (BATCH - 1)) * TILES + t, 1), :]
                                      .rearrange("p a d -> p (a d)")).then_inc(yb_ready, 1)

            def affine_of(it, t):
                if t == 0:
                    dve.wait_ge(xnT2_ready, at(it, TILES, 0))
                    nc.vector.tensor_copy(lnd[:], lnp[:, bass.ds(it >> LOG_BATCH, 1)]
                                          .rearrange("p a c -> p (a c)")).then_inc(lnd_ready, 1)

            def norms(ch, it, t, k):
                if t is None:
                    return
                dve.wait_ge(sq_ready, at(it, 2 * TILES, 2 * t + k + 1))
                ch.done(nc.vector.tensor_reduce(ss[:, k], heads(cosd[:, k]), AX_X, ALU.add))
                ch.join()
                nc.vector.tensor_scalar(ss[:, k], ss[:, k], 1e-24, None, ALU.max).then_inc(ss_ready, 1)

            def normalize(it, t, k):
                if t is None:
                    return
                dve.wait_ge(rn_ready, at(it, 2 * TILES, 2 * t + k + 1))
                nc.vector.tensor_tensor(heads(nrm[:, k]), heads(banks(2 * k, 2)),
                                        rn[:, k].unsqueeze(2).broadcast_to([P, HEADS, DH]), ALU.mult).then_inc(nrm_ready, 1)

            def swap(ch, it, t, k):
                if t is None:
                    return
                dve.wait_ge(rot_ready, at(it, 6, 6))
                dve.wait_ge(nrm_ready, at(it, 2 * TILES, 2 * t + k + 1))
                for to, frm in SW:
                    ch.done(nc.vector.tensor_tensor(
                        heads(swp[:, k])[:, :, to:to + 32], heads(nrm[:, k])[:, :, frm:frm + 32],
                        rot[:, k, 1, t, to:to + 32].unsqueeze(1).broadcast_to([P, HEADS, 32]), ALU.mult))

            def rotate(ch, it, t, k):
                if t is None:
                    return
                ch.join()
                dve.wait_ge(cos_ready, at(it, 2 * TILES, 2 * t + k + 1))
                nc.vector.tensor_tensor(cosd[:, k], cosd[:, k], swp[:, k], ALU.add).then_inc(rotated, 1)

            def maxima(it, t, i):
                if t is None:
                    return
                n = PER * t + i
                dve.wait_ge(scores_ready, at(it, STEPS2, n + 1))
                nc.vector.tensor_reduce(negmax[:, QUAD * n:QUAD * (n + 1)],
                                        g.ps[:, 4, 0:QUAD * KW].rearrange("p (c k) -> p c k", k=KW),
                                        AX_X, ALU.max, negate=True).then_inc(negmax_ready, 1)

            def scale(it, t, i):
                if t is None:
                    return
                n = PER * t + i
                dve.wait_ge(probs_ready, at(it, STEPS2, n + 1))
                nc.vector.reciprocal(rinv[:, QUAD * n:QUAD * (n + 1)],
                                     rowsum[:, QUAD * n:QUAD * (n + 1)]).then_inc(rinv_ready, 1)
                dve.wait_ge(rinv_ready, at(it, STEPS2, n + 1))
                nc.vector.tensor_tensor(
                    p[:, n % 2], p[:, n % 2],
                    rinv[:, QUAD * n:QUAD * (n + 1)].unsqueeze(2).broadcast_to([P, QUAD, KW]), ALU.mult).then_inc(scaled, 1)

            def copy_probs(it, t, i):
                if t is None:
                    return
                n = PER * t + i
                dve.wait_ge(turned, at(it, STEPS2, n + 1))
                dve.wait_ge(pv_done, at(it, STEPS2, n - 1))
                nc.vector.tensor_copy(pT[:, n % 2].rearrange("p c q -> p (c q)"), g.ps[0:KW, 5]).then_inc(pT_copied, 1)

            def moments_of(ch, it, t):
                if t is None:
                    return
                dve.wait_ge(y_mixed, at(it, TILES, t + 1))
                ch.done(nc.vector.bn_stats(stats[:, 0], yb[:, t, 0:D // 2]))
                dve.wait_ge(shifted, at(it, TILES, t + 1))
                ch.done(nc.vector.bn_stats(stats[:, 1], g.ps[:, 7, 0:D // 2]))
                ch.join()
                ch.done(nc.vector.bn_aggr(mv[:], stats[:]))
                ch.join()
                nc.vector.tensor_scalar(mv[:, 1:2], mv[:, 1:2], LN_EPS, None, ALU.add).then_inc(moments, 1)

            def normalize_shifted(it, t):
                if t is None:
                    return
                dve.wait_ge(rstd_ready, at(it, TILES, t + 1))
                nc.vector.tensor_scalar(xn2[:, 0:D // 2], yb[:, t, 0:D // 2], mv[:, 0:1], rstd[:],
                                        ALU.subtract, ALU.mult).then_inc(xn2_ready, 1)
                nc.vector.tensor_scalar(xn2[:, D // 2:D], g.ps[:, 7, 0:D // 2], mv[:, 0:1], rstd[:],
                                        ALU.subtract, ALU.mult).then_inc(xn2_ready, 1)

            def bias_hidden(it, t, hf):
                if t is None:
                    return
                dve.wait_ge(hid_ready, at(it, 2 * TILES, 2 * t + 2 - hf))
                nc.vector.tensor_tensor((ha, hg)[hf][:], g.ps[:, 7, 0:DI],
                                        b1[:, bass.ds(weight_slot(it), 1), hf * DI:(hf + 1) * DI].rearrange("p a c -> p (a c)"),
                                        ALU.add).then_inc((ha_ready, hg_ready)[hf], 1)

            def gate_hidden(it, t):
                if t is None:
                    return
                dve.wait_ge(ha_ready, at(it, TILES, t + 1))
                dve.wait_ge(gelu_ready, at(it, TILES, t + 1))
                nc.vector.tensor_tensor(hh[:], ha[:], hg[:], ALU.mult).then_inc(hh_ready, 1)

            def feed_out(it, t):
                if t is None:
                    return
                dve.wait_ge(ff_ready, at(it, TILES, t + 1))
                nc.vector.tensor_tensor(yt[:], g.ps[:, 7, 0:D], yb[:, t], ALU.add).then_inc(yt_ready, 1)
                dve.wait_ge(yt_ready, at(it, TILES, t + 1))
                nc.vector.tensor_tensor(g.gate[:, bass.ds((it & (BATCH - 1)) * TILES + t, 1), :].rearrange("p a d -> p (a d)"),
                                        yt[:], b2[:, bass.ds(weight_slot(it), 1), :].rearrange("p a d -> p (a d)"),
                                        ALU.add).then_inc(y_ready, 1)

            def mix_out(it, t):
                if t is None:
                    return
                dve.wait_ge(mixed, at(it, TILES, t + 1))
                nc.vector.tensor_tensor(yb[:, t], yb[:, t], g.ps[:, 6, 0:D], ALU.add).then_inc(y_mixed, 1)

            def slot(ahead, now, behind):
                fetch(*ahead)
                affine_of(*behind)
                maxima(*now, 0)
                moments_of(ch, *behind)
                scale(*now, 0)
                normalize_shifted(*behind)
                norms(ch, *ahead, 0)
                maxima(*now, 1)
                copy_probs(*now, 0)
                scale(*now, 1)
                norms(ch, *ahead, 1)
                maxima(*now, 2)
                copy_probs(*now, 1)
                normalize(*ahead, 0)
                scale(*now, 2)
                bias_hidden(*behind, 1)
                swap(ch, *ahead, 0)
                maxima(*now, 3)
                copy_probs(*now, 2)
                normalize(*ahead, 1)
                scale(*now, 3)
                bias_hidden(*behind, 0)
                rotate(ch, *ahead, 0)
                gate_hidden(*behind)
                swap(ch, *ahead, 1)
                copy_probs(*now, 3)
                rotate(ch, *ahead, 1)
                feed_out(*behind)
                mix_out(*now)

            ch = Chain(dve, dve_step)
            all_iterations(dve, slot, ch.restart)
            dve.wait_ge(y_ready, CREDIT + DEPTH * BATCH * TILES)

        @block.scalar
        def _(act):
            act.wait_ge(pad_ready, 1)

            def shift_copies(it, t):
                if t is not None:
                    act.wait_ge(y_turned, at(it, TILES, t + 1))
                    c0 = WINDOW + t * P
                    nc.scalar.copy(xsT[0:64, c0:c0 + P], g.ps[0:64, 7, 0:P]).then_inc(xs_ready, 1)
                    nc.scalar.copy(xsT[64:P, c0 + 1:c0 + P + 1], g.ps[64:P, 7, 0:P]).then_inc(xs_ready, 1)

            def squares(it, t, k):
                if t is not None:
                    act.wait_ge(projected, at(it, 4 * TILES, 4 * t + k + 1))
                    nc.scalar.activation(cosd[:, k], banks(2 * k, 2), ACT.Square).then_inc(sq_ready, 1)

            def copy_values(it, t, j):
                if t is not None:
                    act.wait_ge(projected, at(it, 4 * TILES, 4 * t + j + 3))
                    nc.scalar.copy(vw[:, (QBS * t + j) % (2 * QBS)], banks(2 * j, 2)[0:KW]).then_inc(v_copied, 1)

            def copy_q(it, t):
                if t is not None:
                    act.wait_ge(qk_turned, at(it, 2 * TILES, 2 * t + 1))
                    for hf in range(2):
                        rows = slice(hf * DH, (hf + 1) * DH)
                        for c in range(0, PAIRS, 4):
                            ins = nc.scalar.copy(qz[rows, c:c + 4, t % 2, :, hf],
                                                 g.ps[rows, c // 4].rearrange("p (c j q) -> p c j q", c=4, q=QB))
                        ins.then_inc(q_copied, 1)

            def copy_k(it, t):
                if t is not None:
                    act.wait_ge(qk_turned, at(it, 2 * TILES, 2 * t + 2))
                    nc.scalar.copy(kT[:, :, WINDOW + t * P:WINDOW + (t + 1) * P],
                                   banks(2, 2).rearrange("p (c q) -> p c q", c=PAIRS)).then_inc(k_copied, 1)

            def exps(ch, it, t, i):
                if t is None:
                    return
                n = PER * t + i
                act.wait_ge(negmax_ready, at(it, STEPS2, n + 1))
                act.wait_ge(turned, at(it, STEPS2, n - 1))
                for c in range(QUAD):
                    col = QUAD * n + c
                    ins = nc.scalar.activation(p[:, n % 2, c], g.ps[:, 4, c * KW:(c + 1) * KW], ACT.Exp,
                                               bias=negmax[:, col:col + 1], accum_out=rowsum[:, col:col + 1])
                    if c < QUAD - 1:
                        ch.done(ins)
                ins.then_inc(probs_ready, 1)

            def copy_outputs(it, t, i):
                if t is None:
                    return
                n = PER * t + i
                _, j, quad = step_of(n)
                act.wait_ge(pv_done, at(it, STEPS2, n + 1))
                for hf in range(2):
                    rows = slice(hf * DH, (hf + 1) * DH)
                    nc.scalar.copy(oT[rows, quad * QUAD:(quad + 1) * QUAD, t % 2, j * QB:(j + 1) * QB],
                                   g.ps[rows, 6].rearrange("p (c h q) -> p c h q", h=2, q=QB)[:, :, hf]).then_inc(oT_copied, 1)

            def affine(it, t):
                if t is not None:
                    act.wait_ge(lnd_ready, at(it, 1, 1))
                    act.wait_ge(xn2_turned, at(it, TILES, t + 1))
                    nc.scalar.activation(xnT2[:], g.ps[:, 7, 0:P], ACT.Identity, bias=lnd[:, 1:2],
                                         scale=lnd[:, 0:1]).then_inc(xnT2_ready, 1)

            def gelu(it, t):
                if t is not None:
                    act.wait_ge(hg_ready, at(it, TILES, t + 1))
                    nc.scalar.activation(hg[:], hg[:], ACT.Gelu).then_inc(gelu_ready, 1)

            def copy_hidden(it, t):
                if t is not None:
                    act.wait_ge(hh_turned, at(it, TILES, t + 1))
                    nc.scalar.copy(hT[:, 0:2], g.ps[:, 7, 0:2 * P].rearrange("p (c n) -> p c n", c=2)).then_inc(hT_ready, 1)
                    nc.scalar.copy(hT[0:CH[2][1], 2], g.ps[0:CH[2][1], 7, 2 * P:3 * P]).then_inc(hT_ready, 1)

            def slot(ahead, now, behind):
                shift_copies(*ahead)
                exps(ch, *now, 0)
                squares(*ahead, 0)
                exps(ch, *now, 1)
                affine(*behind)
                squares(*ahead, 1)
                exps(ch, *now, 2)
                copy_outputs(*now, 0)
                exps(ch, *now, 3)
                copy_outputs(*now, 1)
                gelu(*behind)
                copy_values(*ahead, 0)
                copy_values(*ahead, 1)
                copy_outputs(*now, 2)
                copy_hidden(*behind)
                copy_q(*ahead)
                copy_outputs(*now, 3)
                copy_k(*ahead)

            ch = Chain(act, act_step)
            all_iterations(act, slot, ch.restart)
            act.wait_ge(y_ready, CREDIT + DEPTH * BATCH * TILES)
            nc.scalar.activation(g.gate[:], g.gate[:], ACT.Silu).then_inc(y_final, 1)


def l3_attn_stage(g):
    nc = g.nc
    W = D // HEADS
    GR = HEADS // 4
    M = SEQ // W
    with ExitStack() as stack:
        sb, once, sem = scope(nc, stack, "l3a")
        wq = sb("wq", [P, GR, 4, 32])
        wk = sb("wk", [P, D])
        wv = sb("wv", [P, D])
        kF = sb("kF", [P, BATCH, W, M])
        kT_all = sb("kT_all", [P, BATCH, GR, SEQ])
        xb = sb("xb", [P, SEQ])
        qT = sb("qT", [P, GR, SEQ])
        kT = sb("kT", [P, GR, SEQ])
        v = sb("v", [P, TILES, D])
        o = sb("o", [P, TILES, D])
        kd = nc.dram_tensor("k_turn", (BATCH, P, W, M), F32).ap()
        loaded = once("loaded")
        zeroed = once("zeroed")
        kF_product = once("kF_product")
        kF_ready = once("kF_ready")
        kd_stored = once("kd_stored")
        kT_loaded = once("kT_loaded")
        xb_ready = sem("xb_ready")
        kT_ready = sem("kT_ready")
        q_ready = sem("q_ready")
        q_copied = sem("q_copied")
        v_ready = sem("v_ready")
        v_copied = sem("v_copied")
        o_stored = sem("o_stored")
        at = Softmax(g, sb, sem,
                     q=lambda h, t: qT[32 * (h % 4):32 * (h % 4) + W, h // 4, t * P:(t + 1) * P],
                     k=lambda h, n: kT[32 * (h % 4):32 * (h % 4) + W, h // 4, 0:n],
                     v=lambda h, c: v[:, c, h * W:(h + 1) * W],
                     o=lambda h: o[:, :, h * W:(h + 1) * W], width=W)
        block = stack.enter_context(nc.Block())
        w = g.w["L3_attn_qkv_weights"]

        @block.sync
        def _(sp):
            start_counts(sp, sem)
            sp.dma_start(wk[:], w[:, D:2 * D]).then_inc(loaded, 16)
            sp.dma_start(wv[:], w[:, 2 * D:3 * D]).then_inc(loaded, 16)
            sp.wait_ge(zeroed, 1)
            for c in range(GR):
                sp.dma_start(wq[:, c, :, 0:W], w[:, 32 * c:32 * c + 32].rearrange("p (j d) -> p j d", j=4)).then_inc(loaded, 16)
            for b in range(BATCH):
                sp.wait_ge(kF_ready, b + 1)
                sp.dma_start(kd[b], kF[:, b]).then_inc(kd_stored, 16)
            sp.wait_ge(kd_stored, 16 * BATCH)
            sp.wait_ge(zeroed, 2)
            for b in range(BATCH):
                for h in range(HEADS):
                    p0 = 32 * (h % 4)
                    sp.dma_start(kT_all[p0:p0 + W, b, h // 4].rearrange("c (d m) -> c d m", d=W),
                                 kd[b, h * W:(h + 1) * W].rearrange("d c m -> c d m")).then_inc(kT_loaded, 16)

        @block.gpsimd
        def _(pool):
            nc.gpsimd.memset(wq[:], 0.0).then_inc(zeroed, 1)
            nc.gpsimd.memset(kT_all[:], 0.0).then_inc(zeroed, 1)
            with pool.Fori(0, BATCH) as b:
                pool.wait_ge(v_ready, CREDIT + b)
                nc.gpsimd.tensor_copy(xb[:], g.xnT[:, bass.ds(b * SEQ, SEQ)]).then_inc(xb_ready, 1)
                pool.wait_ge(at.o_ready, CREDIT + (b + 1) * HEADS)
                nc.gpsimd.tensor_copy(g.s[:, bass.ds(b * TILES, TILES), :], o[:]).then_inc(o_stored, 1)

        @block.tensor
        def _(pe):
            pe.wait_ge(loaded, 16 * (2 + GR))
            for b in range(BATCH):
                nc.tensor.matmul(g.ps[:, b], wk[:], g.xnT[:, b * SEQ:(b + 1) * SEQ],
                                 start=True, stop=True).then_inc(kF_product, 1)
            pe.wait_ge(kF_ready, BATCH)
            with pe.Fori(0, BATCH) as b:
                pe.wait_ge(xb_ready, CREDIT + b + 1)
                for c in range(GR):
                    pe.wait_ge(q_copied, CREDIT + b * GR + c - 1)
                    nc.tensor.matmul(g.ps[:, 4 + c % 2], wq[:, c].rearrange("p j d -> p (j d)"), xb[:],
                                     start=True, stop=True).then_inc(q_ready, 1)
                for t in range(TILES):
                    ins = nc.tensor.matmul(g.ps[:, 6, t * P:(t + 1) * P], xb[:, t * P:(t + 1) * P], wv[:],
                                           start=True, stop=True)
                ins.then_inc(v_ready, 1)
                pe.wait_ge(q_copied, CREDIT + (b + 1) * GR)
                pe.wait_ge(v_copied, CREDIT + b + 1)
                pe.wait_ge(kT_ready, CREDIT + b + 1)
                at.tensor(pe, b)
                pe.wait_ge(at.o_ready, CREDIT + (b + 1) * HEADS)

        @block.vector
        def _(dve):
            for b in range(BATCH):
                dve.wait_ge(kF_product, b + 1)
                nc.vector.tensor_copy(kF[:, b], g.ps[:, b].rearrange("p (m c) -> p c m", c=W)).then_inc(kF_ready, 1)
            dve.wait_ge(kT_loaded, 16 * BATCH * HEADS)
            with dve.Fori(0, BATCH) as b:
                dve.wait_ge(at.scores_ready, CREDIT + b * STEPS)
                nc.vector.tensor_copy(kT[:], kT_all[:, bass.ds(b, 1)].rearrange("p a c n -> p (a c) n")).then_inc(kT_ready, 1)
                dve.wait_ge(v_ready, CREDIT + b + 1)
                nc.vector.tensor_copy(v[:].rearrange("p t d -> p (t d)"), g.ps[:, 6]).then_inc(v_copied, 1)
                dve.wait_ge(o_stored, CREDIT + b)
                at.vector(dve, b)

        @block.scalar
        def _(act):
            with act.Fori(0, BATCH) as b:
                for c in range(GR):
                    act.wait_ge(q_ready, CREDIT + b * GR + c + 1)
                    nc.scalar.activation(qT[:, c], g.ps[:, 4 + c % 2], ACT.Copy, scale=W ** -0.5).then_inc(q_copied, 1)
                at.scalar(act, b)


class Mixture:

    def __init__(self, nc, g, tag, experts, chunks, swiglu, biased, routing):
        self.g, self.tag = g, tag
        self.E, self.HC, self.swiglu, self.biased, self.routing = experts, chunks, swiglu, biased, routing
        self.run()

    def run(self):
        g, nc = self.g, self.g.nc
        E, HC, swiglu, biased, routing = self.E, self.HC, self.swiglu, self.biased, self.routing
        HIN = 2 if swiglu else HC
        K = E
        R = EXPERTS
        W = g.w
        L = self.tag[:2].upper()
        with ExitStack() as stack:
            sb, once, sem = scope(nc, stack, self.tag)
            w1 = sb("w1", [P, E, HIN * P])
            w2 = sb("w2", [P, E, HC, D])
            wg = sb("wg", [P, R])
            b1 = sb("b1", [P, E * HIN]) if biased else None
            b2 = sb("b2", [K, D]) if biased else None
            bg = sb("bg", [P, 2, R]) if biased else None
            iota = sb("iota", [P, R])
            xb = sb("xb", [P, SEQ])
            h = sb("h", [P, 2, HC, SEQ])
            sa = sb("sa", [P, 2, SEQ]) if swiglu else None
            acc = sb("acc", [P, TILES, D])
            z = sb("z", [P, TILES, R])
            zm = sb("zm", [P, TILES])
            pr = sb("pr", [P, TILES, R])
            top = sb("top", [P, TILES, 8])
            idx = sb("idx", [P, TILES, 8], U32)
            idxf = sb("idxf", [P, TILES, 8])
            pick = sb("pick", [P, 2, TILES, R])
            rw = sb("rw", [P, TILES, K])
            rwT = sb("rwT", [K, TILES, P]) if biased else None
            loaded = once("loaded")
            dve_step = once("dve_step")
            xb_ready = sem("xb_ready")
            logits_ready = sem("logits_ready")
            z_ready = sem("z_ready")
            probs_ready = sem("probs_ready")
            rw_ready = sem("rw_ready")
            rw_turned = sem("rw_turned")
            rwT_ready = sem("rwT_ready")
            bias_ready = sem("bias_ready")
            hid_ready = sem("hid_ready")
            half_ready = sem("half_ready")
            h_ready = sem("h_ready")
            out_ready = sem("out_ready")
            acc_step = sem("acc_step")
            gate_ready = sem("gate_ready")
            block = stack.enter_context(nc.Block())
            A = E * TILES + (1 if biased else 0)
            NH = HC * E if not swiglu else E
            PER = HIN if not swiglu else 1

            loads = [(w1, W[f"{L}_w1"]), (w2, W[f"{L}_w2"]), (wg, W[f"{L}_wg"]), (iota, g.c["iota"])]
            if biased:
                loads += [(b1, W[f"{L}_b1"]), (b2, W[f"{L}_b2"]), (bg, W[f"{L}_bg"].partition_broadcast(P))]

            @block.sync
            def _(sp):
                start_counts(sp, sem)
                for dst, src in loads[2:] + loads[:2]:
                    sp.dma_start(dst[:], src).then_inc(loaded, 16)

            @block.gpsimd
            def _(pool):
                with pool.Fori(0, BATCH) as b:
                    pool.wait_ge(hid_ready, CREDIT + b * E * HIN)
                    nc.gpsimd.tensor_copy(xb[:], g.xnT[:, bass.ds(b * SEQ, SEQ)]).then_inc(xb_ready, 1)

            def hidden(pe, b, e):
                for c in range(HIN):
                    i = e * HIN + c
                    if swiglu:
                        pe.wait_ge(h_ready, CREDIT + b * NH + e - 1)
                    else:
                        pe.wait_ge(h_ready, CREDIT + b * NH + i - 3)
                    nc.tensor.matmul(g.ps[:, i % 4], w1[:, e, c * P:(c + 1) * P], xb[:],
                                     start=True, stop=True).then_inc(hid_ready, 1)

            def outputs(pe, b, e):
                pe.wait_ge(h_ready, CREDIT + b * NH + (e + 1) * PER)
                pe.wait_ge(acc_step, CREDIT + b * A + (A - E * TILES) + (e - 1) * TILES if e >= 1 else CREDIT + b * A)
                for t in range(TILES):
                    for c in range(HC):
                        ins = nc.tensor.matmul(g.ps[:, 4 + e % 2, t * D:(t + 1) * D], h[:, e % 2, c, t * P:(t + 1) * P],
                                               w2[:, e, c], start=(c == 0), stop=(c == HC - 1))
                ins.then_inc(out_ready, 1)

            @block.tensor
            def _(pe):
                pe.wait_ge(loaded, 16 * len(loads))
                with pe.Fori(0, BATCH) as b:
                    pe.wait_ge(xb_ready, CREDIT + b + 1)
                    for t in range(TILES):
                        ins = nc.tensor.matmul(g.ps[:, 6, t * R:(t + 1) * R], xb[:, t * P:(t + 1) * P], wg[:],
                                               start=True, stop=True)
                    ins.then_inc(logits_ready, 1)
                    hidden(pe, b, 0)
                    for e in range(E):
                        if e + 1 < E:
                            hidden(pe, b, e + 1)
                        if e == 0 and biased:
                            pe.wait_ge(rw_ready, CREDIT + b + 1)
                            for t in range(TILES):
                                ins = nc.tensor.transpose(g.ps[0:K, 7, t * P:(t + 1) * P], rw[:, t], g.ident[:])
                            ins.then_inc(rw_turned, 1)
                            pe.wait_ge(rwT_ready, CREDIT + b + 1)
                            for t in range(TILES):
                                ins = nc.tensor.matmul(g.ps[:, 6, t * D:(t + 1) * D], rwT[:, t], b2[:],
                                                       start=True, stop=True)
                            ins.then_inc(bias_ready, 1)
                        outputs(pe, b, e)
                    pe.wait_ge(acc_step, CREDIT + b * A + A)

            def route(dve, b):
                ch = Chain(dve, dve_step)
                dve.sem_clear(dve_step)
                dve.wait_ge(logits_ready, CREDIT + b + 1)
                if E > R:
                    ch.done(nc.vector.memset(rw[:, :, R:E], 1.0))
                lg = g.ps[:, 6, 0:TILES * R].rearrange("p (t r) -> p t r", t=TILES)
                if biased:
                    ch.done(nc.vector.tensor_tensor(z[:], lg, bg[:, 0].unsqueeze(1).broadcast_to([P, TILES, R]), ALU.add))
                else:
                    ch.done(nc.vector.tensor_copy(z[:], lg))
                ch.join()
                if routing == "sigmoid":
                    nc.vector.tensor_tensor(z[:], z[:], bg[:, 1].unsqueeze(1).broadcast_to([P, TILES, R]),
                                            ALU.add).then_inc(z_ready, 1)
                    dve.wait_ge(probs_ready, CREDIT + b + 1)
                    ch.done(nc.vector.tensor_copy(z[:], pr[:]))
                    ch.join()
                else:
                    ch.done(nc.vector.tensor_reduce(zm[:], z[:], AX_X, ALU.max))
                    ch.join()
                    nc.vector.tensor_tensor(z[:], z[:], zm[:].unsqueeze(2).broadcast_to([P, TILES, R]),
                                            ALU.subtract).then_inc(z_ready, 1)
                    dve.wait_ge(probs_ready, CREDIT + b + 1)
                    ch.done(nc.vector.tensor_reduce(zm[:], pr[:], AX_X, ALU.add))
                    ch.join()
                    ch.done(nc.vector.reciprocal(zm[:], zm[:]))
                    ch.join()
                    ch.done(nc.vector.tensor_tensor(pr[:], pr[:], zm[:].unsqueeze(2).broadcast_to([P, TILES, R]), ALU.mult))
                    ch.join()
                for t in range(TILES):
                    ch.done(nc.vector.max(top[:, t], pr[:, t]))
                ch.join()
                for t in range(TILES):
                    ch.done(nc.vector.max_index(idx[:, t], top[:, t], pr[:, t]))
                ch.join()
                ch.done(nc.vector.tensor_copy(idxf[:], idx[:]))
                if routing == "renormalized":
                    ch.done(nc.vector.tensor_tensor(zm[:], top[:, :, 0], top[:, :, 1], ALU.add))
                    ch.join()
                    ch.done(nc.vector.reciprocal(zm[:], zm[:]))
                    ch.join()
                    ch.done(nc.vector.tensor_tensor(top[:, :, 0:2], top[:, :, 0:2],
                                                    zm[:].unsqueeze(2).broadcast_to([P, TILES, 2]), ALU.mult))
                ch.join()
                for k in range(2):
                    ch.done(nc.vector.tensor_tensor(pick[:, k], iota[:].unsqueeze(1).broadcast_to([P, TILES, R]),
                                                    idxf[:, :, k:k + 1].broadcast_to([P, TILES, R]), ALU.is_equal))
                ch.join()
                for k in range(2):
                    ch.done(nc.vector.tensor_tensor(pick[:, k], pick[:, k],
                                                    top[:, :, k:k + 1].broadcast_to([P, TILES, R]), ALU.mult))
                ch.join()
                nc.vector.tensor_tensor(rw[:, :, 0:R], pick[:, 0], pick[:, 1], ALU.add).then_inc(rw_ready, 1)
                dve.wait_ge(rw_ready, CREDIT + b + 1)
                ch.join()

            def add_up(dve, b, e):
                dve.wait_ge(out_ready, CREDIT + b * E + e + 1)
                if e == 0 and not biased:
                    dve.wait_ge(gate_ready, CREDIT + b)
                for t in range(TILES):
                    ps = g.ps[:, 4 + e % 2, t * D:(t + 1) * D]
                    if e == 0 and not biased:
                        ins = nc.vector.tensor_scalar(acc[:, t], ps, rw[:, t, 0:1], None, ALU.mult)
                    else:
                        dve.wait_ge(acc_step, CREDIT + b * A + (A - E * TILES) + (e * TILES + t - TILES + 1 if e else 0))
                        ins = nc.vector.scalar_tensor_tensor(acc[:, t], ps, rw[:, t, e:e + 1], acc[:, t],
                                                             ALU.mult, ALU.add)
                    ins.then_inc(acc_step, 1)

            @block.vector
            def _(dve):
                dve.wait_ge(loaded, 16 * len(loads))
                with dve.Fori(0, BATCH) as b:
                    route(dve, b)
                    if biased:
                        dve.wait_ge(rw_turned, CREDIT + b + 1)
                        nc.vector.tensor_copy(rwT[:].rearrange("k t p -> k (t p)"), g.ps[0:K, 7]).then_inc(rwT_ready, 1)
                        dve.wait_ge(bias_ready, CREDIT + b + 1)
                        dve.wait_ge(gate_ready, CREDIT + b)
                        nc.vector.tensor_copy(acc[:].rearrange("p t d -> p (t d)"), g.ps[:, 6]).then_inc(acc_step, 1)
                    for e in range(E):
                        if swiglu:
                            dve.wait_ge(half_ready, CREDIT + b * E + e + 1)
                            dve.wait_ge(hid_ready, CREDIT + b * E * HIN + (e + 1) * HIN)
                            dve.wait_ge(out_ready, CREDIT + b * E + e - 1)
                            nc.vector.scalar_tensor_tensor(h[:, e % 2, 0], g.ps[:, (2 * e + 1) % 4],
                                                           b1[:, 2 * e + 1:2 * e + 2], sa[:, e % 2],
                                                           ALU.add, ALU.mult).then_inc(h_ready, 1)
                        if e >= 1:
                            add_up(dve, b, e - 1)
                    add_up(dve, b, E - 1)

            @block.scalar
            def _(act):
                act.wait_ge(loaded, 16 * len(loads))
                with act.Fori(0, BATCH) as b:
                    act.wait_ge(z_ready, CREDIT + b + 1)
                    nc.scalar.activation(pr[:], z[:], ACT.Sigmoid if routing == "sigmoid" else ACT.Exp).then_inc(probs_ready, 1)
                    for e in range(E):
                        for c in range(1 if swiglu else HIN):
                            i = e * HIN + c
                            act.wait_ge(hid_ready, CREDIT + b * E * HIN + i + 1)
                            if swiglu:
                                act.wait_ge(h_ready, CREDIT + b * NH + e - 1)
                                nc.scalar.activation(sa[:, e % 2], g.ps[:, i % 4], ACT.Silu,
                                                     bias=b1[:, i:i + 1]).then_inc(half_ready, 1)
                            else:
                                act.wait_ge(out_ready, CREDIT + b * E + e - 1)
                                bias = b1[:, i:i + 1] if biased else 0.0
                                nc.scalar.activation(h[:, e % 2, c], g.ps[:, i % 4], ACT.Gelu,
                                                     bias=bias).then_inc(h_ready, 1)
                    act.wait_ge(acc_step, CREDIT + b * A + A)
                    nc.scalar.activation(g.gate[:, bass.ds(b * TILES, TILES), :], acc[:], ACT.Silu).then_inc(gate_ready, 1)


def l0_ffn_stage(g):
    Mixture(g.nc, g, "l0f", EXPERTS + 1, 4, False, True, "sigmoid")


def l1_ffn_stage(g):
    Mixture(g.nc, g, "l1f", EXPERTS + 1, 1, True, True, "softmax")


def l3_ffn_stage(g):
    Mixture(g.nc, g, "l3f", EXPERTS, 4, False, False, "renormalized")


def more_constants():
    q, j = np.arange(P)[:, None] % 64, np.arange(WINDOW + 64)[None] - WINDOW
    outside = (j > q) | (j < q - WINDOW)
    band = np.where(np.stack([outside | (j < 0), outside], 1), -1e30, 0).astype(np.float32)
    step_down = np.zeros((P, 2, P), np.float32)
    step_down[:, 0] = np.eye(P, k=1)
    step_down[P - 1, 1, 0] = 1
    return {"rope": rotary_constants(), "band": band, "step_down": step_down, "pick": np.tile(np.eye(32, dtype=np.float32), (3, 1)), "iota": np.tile(np.arange(EXPERTS, dtype=np.float32), (P, 1))}


def more_layouts(a, out, rows, cols):
    H = a["L0_ffn_W1"].shape[1]
    w1 = np.concatenate([a["L0_ffn_W1"], a["L0_ffn_Ws1"][None]])
    w2 = np.concatenate([a["L0_ffn_W2"], a["L0_ffn_Ws2"][None]])
    out["L0_w1"] = w1.transpose(2, 0, 1)
    out["L0_w2"] = w2.transpose(2, 0, 1).reshape(H // P, P, EXPERTS + 1, D).transpose(1, 2, 0, 3)
    out["L0_wg"] = a["L0_ffn_Wg"].T
    out["L0_bg"] = np.stack([a["L0_ffn_bg"], a["L0_ffn_bias"]])
    out["L0_b1"] = cols(np.concatenate([a["L0_ffn_b1"], a["L0_ffn_bs1"][None]]).reshape(-1))
    out["L0_b2"] = np.concatenate([a["L0_ffn_b2"], a["L0_ffn_bs2"][None]])
    out["L1_w1"] = np.concatenate([a["L1_ffn_rw1"], a["L1_ffn_sw1"]]).transpose(1, 0, 2)
    out["L1_w2"] = np.concatenate([a["L1_ffn_rw2"], a["L1_ffn_sw2"]]).transpose(1, 0, 2)[:, :, None]
    out["L1_wg"] = a["L1_ffn_gate_w"]
    out["L1_bg"] = np.stack([a["L1_ffn_gate_b"], a["L1_ffn_gate_b"]])
    out["L1_b1"] = cols(np.concatenate([a["L1_ffn_rb1"], a["L1_ffn_sb1"]]).reshape(-1))
    out["L1_b2"] = np.concatenate([a["L1_ffn_rb2"], a["L1_ffn_sb2"]])
    F = a["L3_ffn_w1"].shape[2]
    out["L3_w1"] = a["L3_ffn_w1"].transpose(1, 0, 2)
    out["L3_w2"] = a["L3_ffn_w2"].reshape(EXPERTS, F // P, P, D).transpose(2, 0, 1, 3)
    out["L3_wg"] = a["L3_ffn_gate_w"]
    out["L0_attn_Wq"] = a["L0_attn_Wq"]
    out["L0_attn_Wkv"] = a["L0_attn_Wkv"]
    out["L0_attn_Wout"] = rows(a["L0_attn_Wout"])
    for n in ("gamma", "q_scale", "k_scale"):
        out[f"L0_attn_{n}"] = a[f"L0_attn_{n}"][:, None]
    out["L0_attn_null_kv"] = a["L0_attn_null_kv"]
    out["L3_attn_qkv_weights"] = a["L3_attn_qkv_weights"]
    for u in (1, 2):
        m = f"L2_attn_m{u}_"
        for n in ("Win", "Wx", "Wout", "Wconv", "Alog", "Wdt"):
            out[f"L2_m{u}_{n}"] = a[m + n]
        out[f"L2_m{u}_vec"] = np.stack([a[m + "bconv"], a[m + "bdt"], a[m + "Dp"]], 1)
    out["L2_attn_ln"] = np.stack([a["L2_attn_ln_g"], a["L2_attn_ln_b"]], 1)
    for n in ("Wqkv", "q_scale", "k_scale", "W1", "b1", "W2", "b2"):
        out[f"L2_ffn_{n}"] = a[f"L2_ffn_{n}"]
    out["L2_ffn_Wo"] = a["L2_ffn_Wo"].reshape(DEPTH, PAIRS, P, D).transpose(0, 2, 1, 3)
    out["L2_ffn_ln"] = np.stack([a["L2_ffn_ln_g"], a["L2_ffn_ln_b"]], 2).transpose(1, 0, 2)


def rotary_constants():
    f = np.float32
    half = np.arange(0, DH, 2, dtype=f)
    inv_freq = f(1) / f(10000) ** (half / f(DH))
    t = np.arange(SEQ, dtype=f)
    freqs = t[:, None] * inv_freq[None]
    freqs = np.concatenate([freqs, freqs], -1)
    base = (half + f(0.4 * DH)) / f(1.4 * DH)
    power = (t - SEQ // 2) / f(WINDOW // 2)
    scale = base[None] ** power[:, None]
    scale = np.concatenate([scale, scale], -1)
    sign = np.where(np.arange(DH) < DH // 2, -1, 1).astype(f)
    cos, sin = np.cos(freqs), np.sin(freqs) * sign
    q = np.stack([cos * scale, sin * scale]) * f(8)
    k = np.stack([cos / scale, sin / scale])
    return np.stack([q, k]).astype(f).reshape(2, 2, TILES, P, DH).transpose(3, 0, 1, 2, 4)


NMASK = 4
ATTN = (l0_attn_stage, l1_attn_stage, l2_attn_stage, l3_attn_stage)
FFN = (l0_ffn_stage, l1_ffn_stage, l2_ffn_stage, l3_ffn_stage)


def finish_stage(g, gate_tensor, last):
    nc = g.nc
    tag = f"upd{g.serial}"
    g.serial += 1
    with ExitStack() as stack:
        sb, sem, _ = scope(nc, stack, tag)
        prod_done = sem("prod_done")
        x_ready = sem("x_ready")
        stored = sem("stored")
        block = stack.enter_context(nc.Block())

        @block.vector
        def _(dve):
            nc.vector.tensor_tensor(g.s[:], g.s[:], gate_tensor[:], ALU.mult).then_inc(prod_done, 1)
            dve.wait_ge(prod_done, 1)
            nc.vector.tensor_tensor(g.x[:], g.x[:], g.s[:], ALU.add).then_inc(x_ready, 1)

        @block.sync
        def _(sp):
            if last:
                sp.wait_ge(x_ready, 1)
                sp.dma_start(g.out.rearrange("b (t p) d -> p (b t) d", p=P), g.x[:]).then_inc(stored, 16)
                sp.wait_ge(stored, 16)


def four_gated_layers(nc, x_in, weights, consts, out):
    g = Ctx()
    g.nc, g.x_in, g.w, g.c, g.out, g.serial = nc, x_in, weights, consts, out, 0
    with ExitStack() as stack:
        def sb(name, shape, dt=F32):
            return stack.enter_context(nc.sbuf_tensor(name, shape, dt))

        g.x = sb("x", [P, NT, D])
        g.xn = sb("xn", [P, NT, D])
        g.xnT = sb("xnT", [P, BATCH * SEQ])
        g.s = sb("s", [P, NT, D])
        g.gate = sb("gate", [P, NT, D])
        g.ident = sb("ident", [P, P])
        g.identb = sb("identb", [P, P], BF16)
        g.maskf = sb("maskf", [P, NMASK, P])
        g.maskb = sb("maskb", [P, NMASK, P], BF16)
        g.neghalf = sb("neghalf", [P, 64])
        g.ps = stack.enter_context(nc.psum_tensor("ps", [P, 8, 512], F32))
        load_stage(g)
        run_stages(g)


def run_stages(g):
    for k in range(4):
        norm_stage(g, f"n{k}")
        ATTN[k](g)
        FFN[k](g)
        finish_stage(g, g.gate, k == 3)


def constants():
    i = np.arange(P)
    NEG = np.float32(-1e30)
    q, k = i[:, None], i[None, :]
    causal = np.where(k > q, NEG, 0)
    prefix = np.where((k > q) & ~((q < 64) & (k < 64)), NEG, 0)
    band_prev = np.where(k < q, NEG, 0)
    band_own = np.where((k > q) | (k < q - 32), NEG, 0)
    masks = np.stack([causal, prefix, band_prev, band_own], 1).astype(np.float32)
    return {"ident": np.eye(P, dtype=np.float32), "masks": masks, **more_constants()}


def layouts(a):
    def rows(w):
        return w.reshape(-1, P, w.shape[-1]).transpose(1, 0, 2)

    def cols(v):
        return v.reshape(-1, P).T

    HD = HEADS * DH
    out = {}
    for n in ("q", "k", "v"):
        out[f"L1_attn_W{n}"] = a[f"L1_attn_W{n}"].transpose(1, 0, 2).reshape(D, HD)
    out["L1_attn_Wo"] = rows(a["L1_attn_Wo"].reshape(HD, D))
    out["L1_attn_bq"] = cols(a["L1_attn_bq"].reshape(HD))
    out["L1_attn_bk"] = cols(a["L1_attn_bk"].reshape(HD))
    out["L1_attn_bv"] = a["L1_attn_bv"].reshape(HD)
    out["L1_attn_bo"] = a["L1_attn_bo"]
    more_layouts(a, out, rows, cols)
    return out


def kernel(**inputs):
    import concourse.bacc as _bacc
    from concourse.bass_utils import run_bass_kernel_spmd as _run

    nc = _bacc.Bacc("TRN2", target_bir_lowering=False, num_devices=1)
    arrays = {}

    def dram(name, a):
        a = np.ascontiguousarray(a)
        arrays[name] = a
        return nc.dram_tensor(name, a.shape, mybir.dt.from_np(a.dtype), kind="ExternalInput").ap()

    x = dram("x_dram", inputs["L0_attn_x"])
    weights = {n: dram(f"{n}_dram", a) for n, a in layouts({k: np.asarray(v) for k, v in inputs.items()}).items()}
    consts = {n: dram(f"{n}_const", a) for n, a in constants().items()}
    out = nc.dram_tensor("out_dram", (BATCH, SEQ, D), F32, kind="ExternalOutput").ap()
    four_gated_layers(nc, x, weights, consts, out)
    r = _run(nc, [arrays], core_ids=[0])
    return r.results[0]["out_dram"]
```

```python
import numpy as np

import concourse.bass as bass
from concourse import mybir
from contextlib import ExitStack

ALU = mybir.AluOpType
ACT = mybir.ActivationFunctionType
F32 = mybir.dt.float32
BF16 = mybir.dt.bfloat16
U32 = mybir.dt.uint32
AX_X = mybir.AxisListType.X

P = 128
BATCH, SEQ, D = 4, 512, 128
TILES = SEQ // P
NT = BATCH * TILES
HEADS, DH = 16, 64
PAIRS = HEADS // 2
LN_EPS = 1e-5
EXPERTS = 8
CREDIT = 4


class Ctx:
    pass


def scope(nc, stack, tag):
    made = []

    def end():
        nc.clear_and_free_semaphores(made)
        nc.all_engine_barrier()

    stack.callback(end)

    def sb(name, shape, dt=F32):
        return stack.enter_context(nc.sbuf_tensor(f"{tag}_{name}", shape, dt))

    def once(name):
        made.append(nc.alloc_semaphore(f"{tag}_{name}"))
        return made[-1]

    def counted(name):
        counted.made.append(once(name))
        return counted.made[-1]

    counted.made = []
    return sb, once, counted


def start_counts(eng, counted):
    for s in counted.made:
        eng.sem_inc(s, CREDIT)


class Chain:

    def __init__(self, eng, semaphore):
        self.eng, self.sem, self.n = eng, semaphore, 0

    def done(self, ins):
        self.n += 1
        ins.then_inc(self.sem, 1)

    def join(self):
        self.eng.wait_ge(self.sem, self.n)

    def restart(self):
        self.join()
        self.eng.sem_clear(self.sem)
        self.n = 0


def load_stage(g):
    nc = g.nc
    with ExitStack() as stack:
        sb, sem, _ = scope(nc, stack, "load")
        masks = sb("masks", [P, 72])
        landed = sem("landed")
        block = stack.enter_context(nc.Block())

        @block.sync
        def _(sp):
            sp.dma_start(g.x[:], g.x_in.rearrange("b (t p) d -> p (b t) d", p=P)).then_inc(landed, 16)
            sp.dma_start(g.ident[:], g.c["ident"]).then_inc(landed, 16)
            sp.dma_start(masks[:, 0:64], g.c["causal64"]).then_inc(landed, 16)
            sp.dma_start(masks[:, 64:72], g.c["causal8"]).then_inc(landed, 16)
            sp.wait_ge(landed, 64)

        @block.vector
        def _(dve):
            dve.memset(g.neghalf[:], -0.5)
            dve.wait_ge(landed, 64)
            nc.vector.tensor_copy(g.identb[:], g.ident[:])
            nc.vector.tensor_copy(g.causal64[:], masks[:, 0:64])
            nc.vector.tensor_copy(g.causal8[:], masks[:, 64:72])


def norm_stage(g, tag):
    nc = g.nc
    with ExitStack() as stack:
        sb, sem, _ = scope(nc, stack, tag)
        stats = sb("stats", [P, NT, 6])
        mv = sb("mv", [P, NT, 2])
        rstd = sb("rstd", [P, NT])
        stats_done = sem("stats_done")
        mean_done = sem("mean_done")
        var_ready = sem("var_ready")
        rstd_ready = sem("rstd_ready")
        xn_ready = sem("xn_ready")
        turned = sem("turned")
        copied = sem("copied")
        block = stack.enter_context(nc.Block())

        @block.vector
        def _(dve):
            for n in range(NT):
                nc.vector.bn_stats(stats[:, n], g.x[:, n]).then_inc(stats_done, 1)
            for n in range(NT):
                dve.wait_ge(stats_done, n + 1)
                nc.vector.bn_aggr(mv[:, n], stats[:, n]).then_inc(mean_done, 1)
            dve.wait_ge(mean_done, NT)
            nc.vector.tensor_scalar(mv[:, :, 1], mv[:, :, 1], LN_EPS, None, ALU.add).then_inc(var_ready, 1)
            dve.wait_ge(rstd_ready, 1)
            for n in range(NT):
                nc.vector.tensor_scalar(g.xn[:, n], g.x[:, n], mv[:, n, 0:1], rstd[:, n:n + 1],
                                        ALU.subtract, ALU.mult).then_inc(xn_ready, 1)

        @block.gpsimd
        def _(pool):
            pool.wait_ge(var_ready, 1)
            nc.gpsimd.tensor_tensor(rstd[:], mv[:, :, 1], g.neghalf[:, 0:NT], ALU.pow).then_inc(rstd_ready, 1)

        @block.tensor
        def _(pe):
            for b in range(BATCH):
                if b >= 2:
                    pe.wait_ge(copied, b - 1)
                for t in range(TILES):
                    n = b * TILES + t
                    pe.wait_ge(xn_ready, n + 1)
                    ins = nc.tensor.transpose(g.ps[:, b % 2, t * P:(t + 1) * P], g.xn[:, n], g.ident[:])
                ins.then_inc(turned, 1)

        @block.scalar
        def _(act):
            for b in range(BATCH):
                act.wait_ge(turned, b + 1)
                nc.scalar.copy(g.xnT[:, b * SEQ:(b + 1) * SEQ], g.ps[:, b % 2]).then_inc(copied, 1)


class Softmax:

    def __init__(self, g, sb, sem, steps, keys, q, k, v, mask, collect, copier):
        self.g, self.nc, self.steps = g, g.nc, steps
        self.keys = keys
        self.q, self.k, self.v = q, k, v
        self.mask = mask
        self.collect = collect
        self.copier = copier
        most = max(keys(n) for n in range(steps))
        self.p = sb("p", [P, 3, most])
        self.pT = sb("pT", [P, 2, (most + P - 1) // P * P])
        self.negmax = sb("negmax", [P, steps])
        self.rowsum = sb("rowsum", [P, steps])
        self.rinv = sb("rinv", [P, steps])
        self.scores_ready = sem("scores_ready")
        self.negmax_ready = sem("negmax_ready")
        self.probs_ready = sem("probs_ready")
        self.rinv_ready = sem("rinv_ready")
        self.scaled = sem("scaled")
        self.turned = sem("turned")
        self.copied = sem("copied")
        self.pv_done = sem("pv_done")
        self.collected = sem("collected")

    def at(self, b, k):
        return CREDIT + b * self.steps + k

    def banks(self, first):
        return self.g.ps[:, first:first + 2].rearrange("p a c -> p (a c)")

    def chunks(self, n):
        nk = self.keys(n)
        return [(c, c * P, min(P, nk - c * P)) for c in range((nk + P - 1) // P)]

    def pe_scores(self, pe, b, n):
        if n >= self.steps:
            return
        nc, nk, mask = self.nc, self.keys(n), self.mask(n)
        s = self.banks(n % 3)
        pe.wait_ge(self.probs_ready, self.at(b, max(n - (1 if nk > 512 else 2), 0)))
        for c0 in range(0, nk, 512):
            c1 = min(c0 + 512, nk)
            ins = nc.tensor.matmul(s[:, c0:c1], self.q(n), self.k(n, c0, c1), start=True, stop=mask is None)
        if mask is not None:
            m0 = nk - mask.shape[-1]
            for c0, c1 in ((m0, min(nk, 512)), (max(m0, 512), nk)):
                if c0 < c1:
                    ins = nc.tensor.matmul(s[:, c0:c1], self.g.identb[:], mask[:, c0 - m0:c1 - m0],
                                           start=False, stop=True)
        ins.then_inc(self.scores_ready, 1)

    def pe_turn(self, pe, b, n):
        pe.wait_ge(self.scaled, self.at(b, n + 1))
        pe.wait_ge(self.copied, self.at(b, n - 1))
        out = self.banks(3 + n % 2)
        for c, c0, rows in self.chunks(n):
            if 32 < rows <= 64:
                rows = P
            ins = self.nc.tensor.transpose(out[0:rows, c * P:(c + 1) * P], self.p[:, n % 3, c0:c0 + rows],
                                           self.g.ident[:])
        ins.then_inc(self.turned, 1)

    def pe_pv(self, pe, b, n):
        if n < 0:
            return
        pe.wait_ge(self.copied, self.at(b, n + 1))
        pe.wait_ge(self.collected, self.at(b, n - 1))
        chunks = self.chunks(n)
        for c, c0, rows in chunks:
            ins = self.nc.tensor.matmul(self.g.ps[:, 6 + n % 2, 0:P], self.v(n, c, rows),
                                        self.pT[0:rows, n % 2, c * P:(c + 1) * P],
                                        start=(c == 0), stop=(c == len(chunks) - 1))
        ins.then_inc(self.pv_done, 1)

    def tensor(self, pe, b):
        self.pe_scores(pe, b, 0)
        self.pe_scores(pe, b, 1)
        for n in range(self.steps):
            self.pe_scores(pe, b, n + 2)
            self.pe_turn(pe, b, n)
            self.pe_pv(pe, b, n - 1)
        self.pe_pv(pe, b, self.steps - 1)

    def maximum(self, dve, b, n):
        if n < self.steps:
            dve.wait_ge(self.scores_ready, self.at(b, n + 1))
            self.nc.vector.tensor_reduce(self.negmax[:, n:n + 1], self.banks(n % 3)[:, 0:self.keys(n)], AX_X, ALU.max,
                                         negate=True).then_inc(self.negmax_ready, 1)

    def inverse_sum(self, dve, b, n):
        if n < self.steps:
            dve.wait_ge(self.probs_ready, self.at(b, n + 1))
            self.nc.vector.reciprocal(self.rinv[:, n:n + 1], self.rowsum[:, n:n + 1]).then_inc(self.rinv_ready, 1)

    def copy_turned(self, eng, copy, b, n):
        eng.wait_ge(self.turned, self.at(b, n + 1))
        eng.wait_ge(self.pv_done, self.at(b, n - 1))
        bank, nk = self.banks(3 + n % 2), self.keys(n)
        full, rows = nk // P * P, nk % P
        if full:
            ins = copy(self.pT[:, n % 2, 0:full], bank[:, 0:full])
        if rows:
            ins = copy(self.pT[0:rows, n % 2, full:full + P], bank[0:rows, full:full + P])
        ins.then_inc(self.copied, 1)

    def vector(self, dve, b):
        self.maximum(dve, b, 0)
        self.maximum(dve, b, 1)
        self.inverse_sum(dve, b, 0)
        for n in range(self.steps + 1):
            self.inverse_sum(dve, b, n + 1)
            self.maximum(dve, b, n + 2)
            if n < self.steps and self.copier == "dve":
                self.copy_turned(dve, self.nc.vector.tensor_copy, b, n)
            if n >= 1 and self.copier == "act":
                self.collect(dve, b, n - 1)

    def probabilities(self, act, b, n):
        if n < self.steps:
            nk = self.keys(n)
            act.wait_ge(self.negmax_ready, self.at(b, n + 1))
            act.wait_ge(self.turned, self.at(b, max(n - 2, 0)))
            self.nc.scalar.activation(self.p[:, n % 3, 0:nk], self.banks(n % 3)[:, 0:nk], ACT.Exp,
                                      bias=self.negmax[:, n:n + 1],
                                      accum_out=self.rowsum[:, n:n + 1]).then_inc(self.probs_ready, 1)

    def scalar(self, act, b):
        self.probabilities(act, b, 0)
        self.probabilities(act, b, 1)
        for n in range(self.steps + 1):
            self.probabilities(act, b, n + 2)
            if n < self.steps and self.copier == "act":
                self.copy_turned(act, self.nc.scalar.copy, b, n)
            if n >= 1 and self.copier == "dve":
                self.collect(act, b, n - 1)

    def pool(self, pool, b):
        for n in range(self.steps):
            nk = self.keys(n)
            pool.wait_ge(self.rinv_ready, self.at(b, n + 1))
            self.nc.gpsimd.tensor_tensor(self.p[:, n % 3, 0:nk], self.p[:, n % 3, 0:nk],
                                         self.rinv[:, n:n + 1].broadcast_to([P, nk]), ALU.mult).then_inc(self.scaled, 1)


class OutProduct:

    def __init__(self, g, sb, sem, oT, wo):
        self.g, self.nc, self.oT, self.wo = g, g.nc, oT, wo
        self.s_ready = sem("s_ready")
        self.s_copied = sem("s_copied")

    def tensor(self, pe, b):
        nc, g = self.nc, self.g
        for t in range(TILES):
            pe.wait_ge(self.s_copied, CREDIT + b * TILES + t - 1)
            for c in range(PAIRS):
                ins = nc.tensor.matmul(g.ps[:, t % 2, 0:D], self.oT[:, c, t * P:(t + 1) * P], self.wo[:, c],
                                       start=(c == 0), stop=(c == PAIRS - 1))
            ins.then_inc(self.s_ready, 1)
        pe.wait_ge(self.s_copied, CREDIT + (b + 1) * TILES)


def l0_attn_stage(g):
    nc = g.nc
    HD = HEADS * DH
    SCALE = 8.0
    NULLS, PREFIX = 2, 64
    QB = P // HEADS
    KC = TILES + 1
    with ExitStack() as stack:
        sb, once, sem = scope(nc, stack, "l0a")
        wq = sb("wq", [P, HD])
        wkv = sb("wkv", [P, 2 * DH])
        wo = sb("wo", [P, PAIRS, D])
        gamma = sb("gamma", [P, 1])
        qks = sb("qks", [P, 3])
        null_kv = sb("null_kv", [NULLS, 2 * DH])
        stats = sb("stats", [P, NT, 6])
        mv = sb("mv", [P, NT, 2])
        rstd = sb("rstd", [P, NT])
        xg = g.gate
        xgT = sb("xgT", [P, NT, D])
        xb = sb("xb", [P, KC * P])
        qb = sb("qb", [P, SEQ])
        kraw = sb("kraw", [P, KC, DH])
        ksq = sb("ksq", [P, KC, DH])
        kd = sb("kd", [P, KC, 2, DH])
        kT = sb("kT", [P, KC * P])
        v = sb("v", [P, KC, 2, DH])
        sq = sb("sq", [P, 2, 512])
        qn = sb("qn", [P, 2, HD])
        ss = sb("ss", [P, TILES + 1, HEADS])
        rn = sb("rn", [P, TILES + 1, HEADS])
        qz = sb("qz", [P, SEQ // QB, HEADS, QB])
        oT = sb("oT", [P, PAIRS, SEQ])
        loaded = once("loaded")
        dve_step = once("dve_step")
        pre = once("pre")
        zeroed = once("zeroed")
        var_ready = once("var_ready")
        rstd_ready = once("rstd_ready")
        xg_ready = once("xg_ready")
        xg_turned = once("xg_turned")
        xgT_ready = once("xgT_ready")
        xb_ready = sem("xb_ready")
        kv_ready = sem("kv_ready")
        ss_ready = sem("ss_ready")
        rn_ready = sem("rn_ready")
        kd_ready = sem("kd_ready")
        k_turned = sem("k_turned")
        kT_ready = sem("kT_ready")
        q_ready = sem("q_ready")
        sq_ready = sem("sq_ready")
        sq_summed = sem("sq_summed")
        q_normed = sem("q_normed")
        q_turned = sem("q_turned")
        q_copied = sem("q_copied")
        op = OutProduct(g, sb, sem, oT, wo)

        def collect(act, b, n):
            if n == 0:
                act.wait_ge(op.s_ready, CREDIT + b * TILES)
            act.wait_ge(at.pv_done, at.at(b, n + 1))
            for hf in range(2):
                rows = slice(hf * DH, (hf + 1) * DH)
                ins = nc.scalar.copy(oT[rows, :, n * QB:(n + 1) * QB],
                                     g.ps[rows, 6 + n % 2, 0:P].rearrange("p (c h q) -> p c h q", h=2, q=QB)[:, :, hf])
            ins.then_inc(at.collected, 1)

        free = PREFIX // QB
        at = Softmax(g, sb, sem, steps=SEQ // QB, keys=lambda n: NULLS + max(QB * (n + 1), PREFIX),
                     q=lambda n: qz[:, n].rearrange("p h q -> p (h q)"), k=lambda n, c0, c1: kT[:, c0:c1],
                     v=lambda n, c, rows: v[0:rows, c].rearrange("p a d -> p (a d)"),
                     mask=lambda n: None if n < free else g.causal8[:], collect=collect, copier="dve")
        block = stack.enter_context(nc.Block())
        LOADED = 16 * 10
        Q = 2 * TILES

        @block.sync
        def _(sp):
            start_counts(sp, sem)
            w = g.w
            for dst, src in ((null_kv[:, 0:DH], w["L0_attn_null_kv"][0]),
                             (null_kv[:, DH:2 * DH], w["L0_attn_null_kv"][1]), (gamma[:], w["L0_attn_gamma"]),
                             (wkv[:], w["L0_attn_Wkv"]), (wq[:], w["L0_attn_Wq"]), (wo[:], w["L0_attn_Wout"])):
                sp.dma_start(dst, src).then_inc(loaded, 16)
            for i, n in enumerate(("L0_attn_q_scale", "L0_attn_k_scale")):
                for half in range(2):
                    sp.dma_start(qks[half * DH:half * DH + DH, i:i + 1], w[n]).then_inc(loaded, 16)

        @block.vector
        def _(dve):
            ch = Chain(dve, pre)
            for n in range(NT):
                ch.done(nc.vector.bn_stats(stats[:, n], g.xn[:, n]))
            ch.join()
            for n in range(NT):
                ch.done(nc.vector.bn_aggr(mv[:, n], stats[:, n]))
            ch.join()
            nc.vector.tensor_scalar(mv[:, :, 1], mv[:, :, 1], LN_EPS, None, ALU.add).then_inc(var_ready, 1)
            dve.wait_ge(loaded, LOADED)
            ch.done(nc.vector.tensor_scalar(qks[:, 2:3], qks[:, 0:1], qks[:, 1:2], SCALE, ALU.mult, ALU.mult))
            nc.vector.memset(at.p[:], 0.0)
            nc.vector.memset(qz[:], 0.0)
            nc.vector.memset(xb[:], 0.0).then_inc(zeroed, 1)
            dve.wait_ge(rstd_ready, 1)
            for n in range(NT):
                nc.vector.tensor_scalar(xg[:, n], g.xn[:, n], mv[:, n, 0:1], rstd[:, n:n + 1],
                                        ALU.subtract, ALU.mult).then_inc(xg_ready, 1)
            assert ch.n == NK_STEPS, ch.n
            with dve.Fori(0, BATCH) as b:
                ch = Chain(dve, dve_step)
                dve.sem_clear(dve_step)
                dve.wait_ge(kv_ready, CREDIT + b + 1)
                kv = at.banks(6)[:, 0:KC * P].rearrange("p (t c) -> p t c", t=KC)
                ch.done(nc.vector.tensor_copy(kraw[:], kv[:, :, 0:DH]))
                for half in range(2):
                    ch.done(nc.vector.tensor_copy(v[:, :, half], kv[:, :, DH:2 * DH]))
                ch.join()
                ch.done(nc.vector.tensor_tensor(ksq[:], kraw[:], kraw[:], ALU.mult))
                ch.join()
                ch.done(nc.vector.tensor_reduce(ss[:, 0, 0:KC], ksq[:], AX_X, ALU.add))
                ch.join()
                nc.vector.tensor_scalar(ss[:, 0, 0:KC], ss[:, 0, 0:KC], 1e-24, None, ALU.max).then_inc(ss_ready, 1)

                def sum_squares(t):
                    for i in (2 * t, 2 * t + 1):
                        dve.wait_ge(sq_ready, CREDIT + b * Q + i + 1)
                        nc.vector.tensor_reduce(ss[:, 1 + t, 8 * (i % 2):8 * (i % 2) + 8],
                                                sq[:, i % 2].rearrange("p (h d) -> p h d", d=DH), AX_X,
                                                ALU.add).then_inc(sq_summed, 1)
                    dve.wait_ge(sq_summed, CREDIT + b * Q + 2 * t + 2)
                    nc.vector.tensor_scalar(ss[:, 1 + t], ss[:, 1 + t], 1e-24, None, ALU.max).then_inc(ss_ready, 1)

                def normalize(t):
                    dve.wait_ge(rn_ready, CREDIT + b * (TILES + 1) + t + 2)
                    dve.wait_ge(q_turned, CREDIT + b * Q + 2 * t - 2)
                    for i in (2 * t, 2 * t + 1):
                        hs = slice(8 * (i % 2), 8 * (i % 2) + 8)
                        nc.vector.tensor_tensor(
                            qn[:, t % 2, 512 * (i % 2):512 * (i % 2) + 512].rearrange("p (h d) -> p h d", d=DH),
                            g.ps[:, i % 4].rearrange("p (h d) -> p h d", d=DH),
                            rn[:, 1 + t, hs].unsqueeze(2).broadcast_to([P, 8, DH]), ALU.mult).then_inc(q_normed, 1)

                sum_squares(0)
                dve.wait_ge(rn_ready, CREDIT + b * (TILES + 1) + 1)
                for half in range(2):
                    nc.vector.tensor_tensor(kd[:, :, half], kraw[:],
                                            rn[:, 0, 0:KC].unsqueeze(2).broadcast_to([P, KC, DH]),
                                            ALU.mult).then_inc(kd_ready, 1)
                for t in range(TILES):
                    if t + 1 < TILES:
                        sum_squares(t + 1)
                    normalize(t)
                at.vector(dve, b)
                for t in range(TILES):
                    dve.wait_ge(op.s_ready, CREDIT + b * TILES + t + 1)
                    nc.vector.tensor_copy(g.s[:, bass.ds(b * TILES + t, 1), :].rearrange("p a d -> p (a d)"),
                                          g.ps[:, t % 2, 0:D]).then_inc(op.s_copied, 1)
                ch.join()

        @block.gpsimd
        def _(pool):
            pool.wait_ge(var_ready, 1)
            nc.gpsimd.tensor_tensor(rstd[:], mv[:, :, 1], g.neghalf[:, 0:NT], ALU.pow).then_inc(rstd_ready, 1)
            pool.wait_ge(zeroed, 1)
            pool.wait_ge(xgT_ready, BATCH)
            with pool.Fori(0, BATCH) as b:
                pool.wait_ge(q_ready, CREDIT + b * Q)
                nc.gpsimd.tensor_copy(xb[:, NULLS:NULLS + SEQ], g.xnT[:, bass.ds(b * SEQ, SEQ)]).then_inc(xb_ready, 1)
                nc.gpsimd.tensor_copy(qb[:], xgT[:].rearrange("p t d -> p (t d)")[:, bass.ds(b * SEQ, SEQ)])\
                    .then_inc(xb_ready, 1)
                for j in range(TILES + 1):
                    n = KC if j == 0 else HEADS
                    pool.wait_ge(ss_ready, CREDIT + b * (TILES + 1) + j + 1)
                    nc.gpsimd.tensor_tensor(rn[:, j, 0:n], ss[:, j, 0:n], g.neghalf[:, 0:n], ALU.pow).then_inc(rn_ready, 1)
                at.pool(pool, b)

        @block.tensor
        def _(pe):
            pe.wait_ge(loaded, LOADED)
            pe.wait_ge(pre, NK_STEPS)
            for b in range(BATCH):
                if b >= 2:
                    pe.wait_ge(xgT_ready, b - 1)
                pe.wait_ge(xg_ready, (b + 1) * TILES)
                for t in range(TILES):
                    ins = nc.tensor.transpose(g.ps[:, b % 2, t * P:(t + 1) * P], xg[:, b * TILES + t], g.ident[:])
                ins.then_inc(xg_turned, 1)
            pe.wait_ge(xgT_ready, BATCH)

            def query_product(b, t):
                for i in (2 * t, 2 * t + 1):
                    pe.wait_ge(q_normed, CREDIT + b * Q + i - 3)
                    nc.tensor.matmul(g.ps[:, i % 4], qb[:, t * P:(t + 1) * P], wq[:, 512 * (i % 2):512 * (i % 2) + 512],
                                     start=True, stop=True).then_inc(q_ready, 1)

            with pe.Fori(0, BATCH) as b:
                pe.wait_ge(xb_ready, CREDIT + 2 * b + 2)
                for t in range(KC):
                    ins = nc.tensor.matmul(at.banks(6)[:, t * P:(t + 1) * P], xb[:, t * P:(t + 1) * P], wkv[:],
                                           start=True, stop=(t > 0))
                    if t == 0:
                        nc.tensor.matmul(g.ps[:, 6, 0:P], g.ident[0:NULLS, :], null_kv[:], start=False, stop=True)
                ins.then_inc(kv_ready, 1)
                query_product(b, 0)
                query_product(b, 1)
                pe.wait_ge(kd_ready, CREDIT + 2 * b + 2)
                for t in range(KC):
                    ins = nc.tensor.transpose(at.banks(6)[:, t * P:(t + 1) * P], kd[:, t].rearrange("p a d -> p (a d)"), g.ident[:])
                ins.then_inc(k_turned, 1)
                for t in range(TILES):
                    for half in range(2):
                        i = 2 * t + half
                        pe.wait_ge(q_normed, CREDIT + b * Q + i + 1)
                        pe.wait_ge(q_copied, CREDIT + b * Q + i - 1)
                        for c in range(4):
                            ins = nc.tensor.transpose(g.ps[:, 4 + half, c * P:(c + 1) * P],
                                                      qn[:, t % 2, (4 * half + c) * P:(4 * half + c + 1) * P], g.ident[:])
                        ins.then_inc(q_turned, 1)
                    if t + 2 < TILES:
                        query_product(b, t + 2)
                pe.wait_ge(q_copied, CREDIT + b * Q + Q)
                pe.wait_ge(kT_ready, CREDIT + b + 1)
                at.tensor(pe, b)
                pe.wait_ge(at.collected, at.at(b + 1, 0))
                op.tensor(pe, b)

        @block.scalar
        def _(act):
            act.wait_ge(loaded, LOADED)
            act.wait_ge(zeroed, 1)
            for b in range(BATCH):
                act.wait_ge(xg_turned, b + 1)
                nc.scalar.activation(xgT[:].rearrange("p t d -> p (t d)")[:, b * SEQ:(b + 1) * SEQ], g.ps[:, b % 2],
                                     ACT.Copy, scale=gamma[:]).then_inc(xgT_ready, 1)
            with act.Fori(0, BATCH) as b:
                def copy_queries(t):
                    for half in range(2):
                        act.wait_ge(q_turned, CREDIT + b * Q + 2 * t + half + 1)
                        steps = slice(t * P // QB, (t + 1) * P // QB)
                        for hf in range(2):
                            rows = slice(hf * DH, (hf + 1) * DH)
                            dst = qz[rows, steps, 8 * half:8 * half + 8].rearrange("p i (c h) q -> p h c i q", h=2)[:, hf]
                            ins = nc.scalar.copy(dst, g.ps[rows, 4 + half].rearrange("p (c i q) -> p c i q", c=4, q=QB))
                        ins.then_inc(q_copied, 1)

                for t in range(TILES):
                    for i in (2 * t, 2 * t + 1):
                        act.wait_ge(q_ready, CREDIT + b * Q + i + 1)
                        act.wait_ge(sq_summed, CREDIT + b * Q + i - 1)
                        nc.scalar.activation(sq[:, i % 2], g.ps[:, i % 4], ACT.Square).then_inc(sq_ready, 1)
                    if t == 1:
                        act.wait_ge(k_turned, CREDIT + b + 1)
                        nc.scalar.activation(kT[:], at.banks(6)[:, 0:KC * P], ACT.Copy, scale=qks[:, 2:3]).then_inc(kT_ready, 1)
                    if t >= 1:
                        copy_queries(t - 1)
                copy_queries(TILES - 1)
                at.scalar(act, b)


NK_STEPS = 2 * NT + 1


def l1_attn_stage(g):
    nc = g.nc
    HD = HEADS * DH
    QB = 64
    BLOCKS = SEQ // QB
    with ExitStack() as stack:
        sb, once, sem = scope(nc, stack, "l1a")
        wq, wk, wv = (sb(n, [P, HD]) for n in ("wq", "wk", "wv"))
        wo = sb("wo", [P, PAIRS, D])
        bq, bk = (sb(n, [P, PAIRS]) for n in ("bq", "bk"))
        bv = sb("bv", [P, HD])
        bo = sb("bo", [P, D])
        xb = sb("xb", [P, SEQ])
        qz = sb("qz", [P, PAIRS, SEQ // QB, 2, QB])
        kT = sb("kT", [P, PAIRS, SEQ])
        v = sb("v", [P, TILES, HD])
        oT = sb("oT", [P, PAIRS, SEQ])
        loaded = once("loaded")
        bq_scaled = once("bq_scaled")
        zeroed = once("zeroed")
        xb_ready = sem("xb_ready")
        proj_ready = sem("proj_ready")
        proj_copied = sem("proj_copied")
        v_ready = sem("v_ready")
        v_copied = sem("v_copied")
        op = OutProduct(g, sb, sem, oT, wo)

        def collect(act, b, n):
            c, i = n // BLOCKS, n % BLOCKS
            if n == 0:
                act.wait_ge(op.s_ready, CREDIT + b * TILES)
            act.wait_ge(at.pv_done, at.at(b, n + 1))
            for hf in range(2):
                rows = slice(hf * DH, (hf + 1) * DH)
                ins = nc.scalar.copy(oT[rows, c, i * QB:(i + 1) * QB], g.ps[rows, 6 + n % 2, hf * QB:(hf + 1) * QB])
            ins.then_inc(at.collected, 1)

        at = Softmax(g, sb, sem, steps=PAIRS * BLOCKS, keys=lambda n: QB * (n % BLOCKS + 1),
                     q=lambda n: qz[:, n // BLOCKS, n % BLOCKS].rearrange("p h q -> p (h q)"),
                     k=lambda n, c0, c1: kT[:, n // BLOCKS, c0:c1],
                     v=lambda n, c, rows: v[0:rows, c, n // BLOCKS * P:(n // BLOCKS + 1) * P],
                     mask=lambda n: g.causal64[:], collect=collect, copier="dve")
        block = stack.enter_context(nc.Block())

        @block.sync
        def _(sp):
            start_counts(sp, sem)
            for dst, src in ((wq, "L1_attn_Wq"), (wk, "L1_attn_Wk"), (wv, "L1_attn_Wv"), (wo, "L1_attn_Wo"),
                             (bq, "L1_attn_bq"), (bk, "L1_attn_bk")):
                sp.dma_start(dst[:], g.w[src]).then_inc(loaded, 16)
            sp.dma_start(bv[:], g.w["L1_attn_bv"].partition_broadcast(P)).then_inc(loaded, 16)
            sp.dma_start(bo[:], g.w["L1_attn_bo"].partition_broadcast(P)).then_inc(loaded, 16)

        LOADED = 16 * 8

        @block.gpsimd
        def _(pool):
            with pool.Fori(0, BATCH) as b:
                pool.wait_ge(v_ready, CREDIT + b * 2 * TILES)
                nc.gpsimd.tensor_copy(xb[:], g.xnT[:, bass.ds(b * SEQ, SEQ)]).then_inc(xb_ready, 1)
                at.pool(pool, b)

        @block.tensor
        def _(pe):
            pe.wait_ge(loaded, LOADED)
            with pe.Fori(0, BATCH) as b:
                pe.wait_ge(xb_ready, CREDIT + b + 1)
                for i in range(2 * PAIRS):
                    w, c = (wq, wk)[i % 2], i // 2
                    pe.wait_ge(proj_copied, CREDIT + b * 2 * PAIRS + i - 1)
                    nc.tensor.matmul(g.ps[:, i % 2], w[:, c * P:(c + 1) * P], xb[:],
                                     start=True, stop=True).then_inc(proj_ready, 1)
                for i in range(2 * TILES):
                    t, half = i // 2, i % 2
                    pe.wait_ge(v_copied, CREDIT + b * 2 * TILES + i - 1)
                    nc.tensor.matmul(g.ps[:, 2 + i % 2], xb[:, t * P:(t + 1) * P], wv[:, half * 512:half * 512 + 512],
                                     start=True, stop=True).then_inc(v_ready, 1)
                pe.wait_ge(proj_copied, CREDIT + (b + 1) * 2 * PAIRS )
                pe.wait_ge(v_copied, CREDIT + (b + 1) * 2 * TILES)
                at.tensor(pe, b)
                pe.wait_ge(at.collected, at.at(b + 1, 0))
                op.tensor(pe, b)

        @block.vector
        def _(dve):
            dve.wait_ge(loaded, LOADED)
            nc.vector.tensor_scalar(bq[:], bq[:], DH ** -0.5, None, ALU.mult).then_inc(bq_scaled, 1)
            nc.vector.memset(at.p[:], 0.0)
            nc.vector.memset(qz[:], 0.0).then_inc(zeroed, 1)
            with dve.Fori(0, BATCH) as b:
                for i in range(2 * TILES):
                    t, half = i // 2, i % 2
                    dve.wait_ge(v_ready, CREDIT + b * 2 * TILES + i + 1)
                    cols = slice(half * 512, half * 512 + 512)
                    nc.vector.tensor_tensor(v[:, t, cols], g.ps[:, 2 + i % 2], bv[:, cols], ALU.add).then_inc(v_copied, 1)
                at.vector(dve, b)
                for t in range(TILES):
                    dve.wait_ge(op.s_ready, CREDIT + b * TILES + t + 1)
                    nc.vector.tensor_tensor(g.s[:, bass.ds(b * TILES + t, 1), :].rearrange("p a d -> p (a d)"),
                                            g.ps[:, t % 2, 0:D], bo[:], ALU.add).then_inc(op.s_copied, 1)

        @block.scalar
        def _(act):
            act.wait_ge(bq_scaled, 1)
            act.wait_ge(zeroed, 1)
            with act.Fori(0, BATCH) as b:
                for i in range(2 * PAIRS):
                    c = i // 2
                    act.wait_ge(proj_ready, CREDIT + b * 2 * PAIRS + i + 1)
                    if i % 2:
                        ins = nc.scalar.activation(kT[:, c], g.ps[:, i % 2], ACT.Identity, bias=bk[:, c:c + 1])
                    else:
                        for hf in range(2):
                            rows = slice(hf * DH, (hf + 1) * DH)
                            ins = nc.scalar.activation(qz[rows, c, :, hf], g.ps[rows, i % 2].rearrange("p (i q) -> p i q", q=QB),
                                                       ACT.Identity, bias=bq[rows, c:c + 1], scale=DH ** -0.5)
                    ins.then_inc(proj_copied, 1)
                at.scalar(act, b)


STATES, TAPS, DT_RANK, HALF = 16, 4, 4, D // 2


def l2_attn_stage(g):
    nc = g.nc
    PAD = TAPS - 1
    with ExitStack() as stack:
        sb, once, sem = scope(nc, stack, "l2a")
        par = {n: sb(n, [P, 2, c]) for n, c in (("win", 2 * P), ("wx", DT_RANK + 2 * STATES), ("wout", HALF),
                                                ("wconv", TAPS), ("alog", STATES), ("vec", 3))}
        wdt = sb("wdt", [DT_RANK, 2, P])
        A = sb("A", [P, 2, STATES])
        lnp = sb("lnp", [P, 2])
        pick = sb("pick", [96, 2 * STATES])
        sel = sb("sel", [96, 2 * STATES, P], BF16)
        stats = sb("stats", [P, NT, 6])
        mv = sb("mv", [P, NT, 2])
        rstd = sb("rstd", [P, NT])
        hn = g.gate
        hT = sb("hT", [P, BATCH * SEQ])
        xp = sb("xp", [P, SEQ + 2 * PAD])
        cv = sb("cv", [P, TAPS, SEQ])
        xc = sb("xc", [P, 2, SEQ])
        zs = sb("zs", [P, 2, SEQ])
        dt4 = sb("dt4", [DT_RANK, SEQ])
        sp_a = sb("sp_a", [P, SEQ])
        sp_e = sb("sp_e", [P, SEQ])
        sp_l = sb("sp_l", [P, SEQ])
        sp_m = sb("sp_m", [P, SEQ])
        dt = sb("dt", [P, 2, SEQ])
        dtx = sb("dtx", [P, 2, SEQ])
        rest = sb("rest", [2 * STATES, 2, SEQ])
        part = sb("part", [2 * STATES, 3, SEQ], BF16)
        split = sb("split", [96, 2, SEQ], BF16)
        DA = 6
        dA = sb("dA", [P, DA, SEQ])
        ysum = sb("ysum", [P, SEQ])
        zero = sb("zero", [P, 1])
        dBx = sb("dBx", [P, 2, SEQ])
        hs = sb("hs", [P, 2, SEQ])
        hc = sb("hc", [P, 2, SEQ])
        yg = sb("yg", [P, SEQ])
        y = sb("y", [P, SEQ])
        res = sb("res", [P, TILES, D])
        loaded = once("loaded")
        pre = once("pre")
        zero_ready = once("zero_ready")
        var_ready = once("var_ready")
        rstd_ready = once("rstd_ready")
        hn_ready = once("hn_ready")
        h_turned = once("h_turned")
        hT_ready = once("hT_ready")
        A_ready = once("A_ready")
        dve_step = once("dve_step")
        act_step = once("act_step")
        in_ready = sem("in_ready")
        xp_ready = sem("xp_ready")
        zs_ready = sem("zs_ready")
        conv_ready = sem("conv_ready")
        xc_ready = sem("xc_ready")
        dbc_ready = sem("dbc_ready")
        dt4_ready = sem("dt4_ready")
        dt_product = sem("dt_product")
        soft_ready = sem("soft_ready")
        dt_ready = sem("dt_ready")
        split_ready = sem("split_ready")
        b_ready = sem("b_ready")
        c_ready = sem("c_ready")
        dA_ready = sem("dA_ready")
        dBx_ready = sem("dBx_ready")
        hs_ready = sem("hs_ready")
        hc_ready = sem("hc_ready")
        y_added = sem("y_added")
        y_ready = sem("y_ready")
        out_ready = sem("out_ready")
        res_ready = sem("res_ready")
        s_ready = sem("s_ready")
        block = stack.enter_context(nc.Block())
        names = ("Win", "Wx", "Wout", "Wconv", "Alog", "vec", "Wdt")
        LOADED = 16 * (2 * len(names) + 2)
        N = STATES

        def at(b, u, per, k):
            return CREDIT + u * per + k + b * 2 * per

        AT_IN, AT_LOW, AT_TIME = 1, 5, 9

        def both_ways(eng, scan, end=lambda: None):
            end()
            with eng.Fori(0, BATCH - 1) as b:
                scan(b, 0, (b, 1))
                scan(b, 1, (b + 1, 0))
                end()
            scan(BATCH - 1, 0, (BATCH - 1, 1))
            scan(BATCH - 1, 1, None)
            end()

        @block.sync
        def _(sp):
            start_counts(sp, sem)
            for u in range(2):
                for n in names:
                    dst = wdt[:, u] if n == "Wdt" else par[n.lower()][:, u]
                    sp.dma_start(dst, g.w[f"L2_m{u + 1}_{n}"]).then_inc(loaded, 16)
            sp.dma_start(lnp[:], g.w["L2_attn_ln"]).then_inc(loaded, 16)
            sp.dma_start(pick[:], g.c["pick"]).then_inc(loaded, 16)

        @block.gpsimd
        def _(pool):
            pool.wait_ge(var_ready, 1)
            nc.gpsimd.tensor_tensor(rstd[:], mv[:, :, 1], g.neghalf[:, 0:NT], ALU.pow).then_inc(rstd_ready, 1)

            def scan(b, u, ahead):
                for n in range(N):
                    pool.wait_ge(hc_ready, at(b, u, N, n + 1))
                    if n == 0:
                        pool.wait_ge(y_ready, at(b, u, 1, 0))
                        nc.gpsimd.tensor_tensor(ysum[:], hc[:, n % 2], zero[:].broadcast_to([P, SEQ]),
                                                ALU.add).then_inc(y_added, 1)
                    else:
                        pool.wait_ge(y_added, at(b, u, N, n))
                        nc.gpsimd.tensor_tensor(ysum[:], ysum[:], hc[:, n % 2], ALU.add).then_inc(y_added, 1)

            nc.gpsimd.memset(zero[:], 0.0).then_inc(zero_ready, 1)
            pool.wait_ge(zero_ready, 1)
            both_ways(pool, scan)

        @block.tensor
        def _(pe):
            for b in range(BATCH):
                if b >= 2:
                    pe.wait_ge(hT_ready, b - 1)
                pe.wait_ge(hn_ready, (b + 1) * TILES)
                for t in range(TILES):
                    ins = nc.tensor.transpose(g.ps[:, b % 2, t * P:(t + 1) * P], hn[:, b * TILES + t], g.ident[:])
                ins.then_inc(h_turned, 1)
            pe.wait_ge(hT_ready, BATCH)
            pe.wait_ge(loaded, LOADED)
            pe.wait_ge(pre, MAMBA_PRE)

            def inputs(b, u):
                pe.wait_ge(dt_ready, at(b, u, 1, 0))
                pe.wait_ge(split_ready, at(b, u, 1, 0))
                for c in range(2):
                    ins = nc.tensor.matmul(g.ps[:, 4 + 3 * c], par["win"][:, u, c * P:(c + 1) * P],
                                           hT[:, bass.ds(b * SEQ, SEQ)], start=True, stop=True)
                ins.then_inc(in_ready, 1)

            def low_rank(b, u):
                pe.wait_ge(xc_ready, at(b, u, 1, 1))
                pe.wait_ge(zs_ready, at(b, u, 1, 1))
                nc.tensor.matmul(g.ps[0:DT_RANK, 4], par["wx"][:, u, 0:DT_RANK], xc[:, u], start=True, stop=True)
                nc.tensor.matmul(g.ps[0:2 * N, 7], par["wx"][:, u, DT_RANK:], xc[:, u],
                                 start=True, stop=True).then_inc(dbc_ready, 1)

            def time_steps(b, u):
                pe.wait_ge(dt4_ready, at(b, u, 1, 1))
                nc.tensor.matmul(g.ps[:, 4], wdt[:, u], dt4[:], start=True, stop=True).then_inc(dt_product, 1)

            def spread(b, u, n):
                if n == 0:
                    pe.wait_ge(split_ready, at(b, u, 1, 1))
                if n < N:
                    pe.wait_ge(dBx_ready, at(b, u, N, n - 1))
                    nc.tensor.matmul(g.ps[:, n % 2], sel[:, n], split[:, u],
                                     start=True, stop=True).then_inc(b_ready, 1)
                    pe.wait_ge(hc_ready, at(b, u, N, n - 1))
                    nc.tensor.matmul(g.ps[:, 2 + n % 2], sel[:, N + n], split[:, u],
                                     start=True, stop=True).then_inc(c_ready, 1)

            def scan(b, u, ahead):
                for n in range(N):
                    spread(b, u, n + 2)
                    if ahead and n in (AT_IN, AT_LOW, AT_TIME):
                        {AT_IN: inputs, AT_LOW: low_rank, AT_TIME: time_steps}[n](*ahead)
                if ahead:
                    spread(*ahead, 0)
                    spread(*ahead, 1)
                pe.wait_ge(y_ready, at(b, u, 1, 1))
                if u == 0:
                    pe.wait_ge(res_ready, CREDIT + b)
                for t in range(TILES):
                    c0 = t * D + u * HALF
                    ins = nc.tensor.matmul(g.ps[:, 6, c0:c0 + HALF], y[:, t * P:(t + 1) * P], par["wout"][:, u],
                                           start=True, stop=True)
                ins.then_inc(out_ready, 1)

            inputs(0, 0)
            low_rank(0, 0)
            time_steps(0, 0)
            spread(0, 0, 0)
            spread(0, 0, 1)
            both_ways(pe, scan)

        @block.vector
        def _(dve):
            ch = Chain(dve, pre)
            for n in range(NT):
                ch.done(nc.vector.bn_stats(stats[:, n], g.xn[:, n]))
            ch.join()
            for n in range(NT):
                ch.done(nc.vector.bn_aggr(mv[:, n], stats[:, n]))
            ch.join()
            nc.vector.tensor_scalar(mv[:, :, 1], mv[:, :, 1], LN_EPS, None, ALU.add).then_inc(var_ready, 1)
            ch.done(nc.vector.memset(xp[:], 0.0))
            dve.wait_ge(loaded, LOADED)
            ch.done(nc.vector.tensor_copy(sel[:], pick[:].unsqueeze(2).broadcast_to([96, 2 * N, P])))
            dve.wait_ge(A_ready, 1)
            ch.done(nc.vector.tensor_scalar(A[:], A[:], -1.0, None, ALU.mult))
            dve.wait_ge(rstd_ready, 1)
            for n in range(NT):
                nc.vector.tensor_scalar(hn[:, n], g.xn[:, n], mv[:, n, 0:1], rstd[:, n:n + 1],
                                        ALU.subtract, ALU.mult).then_inc(hn_ready, 1)
            ch.join()
            assert ch.n == MAMBA_PRE
            ch = Chain(dve, dve_step)

            def convolve(b, u):
                dve.wait_ge(xp_ready, at(b, u, 1, 1))
                for k in range(TAPS):
                    k0 = 2 * PAD - k if u else k
                    w = par["wconv"][:, u, k:k + 1]
                    if k == 0:
                        ch.done(nc.vector.tensor_scalar(cv[:, 0], xp[:, k0:k0 + SEQ], w, None, ALU.mult))
                    else:
                        ch.join()
                        ins = nc.vector.scalar_tensor_tensor(cv[:, k], xp[:, k0:k0 + SEQ], w, cv[:, k - 1],
                                                             ALU.mult, ALU.add)
                        if k < TAPS - 1:
                            ch.done(ins)
                ins.then_inc(conv_ready, 1)

            def split_rows(b, u):
                dve.wait_ge(dbc_ready, at(b, u, 1, 1))
                rows = g.ps[0:2 * N, 7]
                ch.done(nc.vector.tensor_copy(part[:, 0], rows))
                ch.join()
                ch.done(nc.vector.tensor_tensor(rest[:, 0], rows, part[:, 0], ALU.subtract))
                ch.join()
                ch.done(nc.vector.tensor_copy(part[:, 1], rest[:, 0]))
                ch.join()
                ch.done(nc.vector.tensor_tensor(rest[:, 1], rest[:, 0], part[:, 1], ALU.subtract))
                ch.join()
                ch.done(nc.vector.tensor_copy(split[64:96, u], rest[:, 1]))
                ch.done(nc.vector.tensor_copy(split[32:64, u], part[:, 1]))
                ch.join()
                nc.vector.tensor_copy(split[0:32, u], part[:, 0]).then_inc(split_ready, 1)

            def time_steps(b, u):
                dve.wait_ge(dt_product, at(b, u, 1, 1))
                dve.wait_ge(soft_ready, at(b, u, 1, 1))
                ch.done(nc.vector.tensor_scalar(sp_m[:], g.ps[:, 4], par["vec"][:, u, 1:2], 0.0, ALU.add, ALU.max))
                ch.join()
                nc.vector.tensor_tensor(dt[:, u], sp_m[:], sp_l[:], ALU.add).then_inc(dt_ready, 1)
                dve.wait_ge(dt_ready, at(b, u, 1, 1))
                ch.done(nc.vector.tensor_tensor(dtx[:, u], dt[:, u], xc[:, u], ALU.mult))

            def input_part(b, u, n):
                dve.wait_ge(b_ready, at(b, u, N, n + 1))
                nc.vector.tensor_tensor(dBx[:, n % 2], g.ps[:, n % 2], dtx[:, u], ALU.mult).then_inc(dBx_ready, 1)

            def scan(b, u, ahead):
                way = slice(None, None, -1) if u else slice(None)
                for n in range(N):
                    dve.wait_ge(dBx_ready, at(b, u, N, n + 1))
                    dve.wait_ge(dA_ready, at(b, u, N, n + 1))
                    nc.vector.tensor_tensor_scan(hs[:, n % 2, way], dA[:, n % DA, way], dBx[:, n % 2, way], 0.0,
                                                 ALU.mult, ALU.add).then_inc(hs_ready, 1)
                    if n + 1 < N:
                        input_part(b, u, n + 1)
                    dve.wait_ge(c_ready, at(b, u, N, n + 1))
                    dve.wait_ge(hs_ready, at(b, u, N, n + 1))
                    dve.wait_ge(y_added, at(b, u, N, n - 1))
                    nc.vector.tensor_tensor(hc[:, n % 2], g.ps[:, 2 + n % 2], hs[:, n % 2], ALU.mult).then_inc(hc_ready, 1)
                    if ahead and n in (AT_IN + 1, AT_LOW + 1, AT_TIME + 2):
                        {AT_IN + 1: convolve, AT_LOW + 1: split_rows, AT_TIME + 2: time_steps}[n](*ahead)
                dve.wait_ge(y_added, at(b, u, N, N))
                ch.done(nc.vector.scalar_tensor_tensor(yg[:], xc[:, u], par["vec"][:, u, 2:3], ysum[:],
                                                       ALU.mult, ALU.add))
                dve.wait_ge(out_ready, at(b, u, 1, 0))
                ch.join()
                nc.vector.tensor_tensor(y[:, way], yg[:], zs[:, u], ALU.mult).then_inc(y_ready, 1)
                if ahead:
                    input_part(*ahead, 0)
                if u:
                    dve.wait_ge(out_ready, at(b, 1, 1, 1))
                    dve.wait_ge(s_ready, CREDIT + b)
                    nc.vector.tensor_tensor(res[:], g.ps[:, 6].rearrange("p (t d) -> p t d", t=TILES),
                                            g.xn[:, bass.ds(b * TILES, TILES), :], ALU.add).then_inc(res_ready, 1)

            convolve(0, 0)
            split_rows(0, 0)
            time_steps(0, 0)
            ch.join()
            input_part(0, 0, 0)
            both_ways(dve, scan, ch.restart)

        @block.scalar
        def _(act):
            act.wait_ge(loaded, LOADED)
            nc.scalar.activation(A[:], par["alog"][:], ACT.Exp).then_inc(A_ready, 1)
            for b in range(BATCH):
                act.wait_ge(h_turned, b + 1)
                nc.scalar.activation(hT[:, b * SEQ:(b + 1) * SEQ], g.ps[:, b % 2], ACT.Identity,
                                     bias=lnp[:, 1:2], scale=lnp[:, 0:1]).then_inc(hT_ready, 1)
            act.wait_ge(pre, MAMBA_PRE)
            ch = Chain(act, act_step)

            def halves(b, u):
                act.wait_ge(in_ready, at(b, u, 1, 1))
                nc.scalar.copy(xp[:, PAD:PAD + SEQ], g.ps[:, 4]).then_inc(xp_ready, 1)
                act.wait_ge(y_ready, at(b, u, 1, -1))
                nc.scalar.activation(zs[:, u], g.ps[:, 7], ACT.Silu).then_inc(zs_ready, 1)
                act.wait_ge(conv_ready, at(b, u, 1, 1))
                nc.scalar.activation(xc[:, u], cv[:, TAPS - 1], ACT.Silu, bias=par["vec"][:, u, 0:1]).then_inc(xc_ready, 1)

            def copy_low_rank(b, u):
                act.wait_ge(dbc_ready, at(b, u, 1, 1))
                nc.scalar.copy(dt4[:], g.ps[0:DT_RANK, 4]).then_inc(dt4_ready, 1)

            def soft(b, u):
                act.wait_ge(dt_product, at(b, u, 1, 1))
                ch.done(nc.scalar.activation(sp_a[:], g.ps[:, 4], ACT.Abs, bias=par["vec"][:, u, 1:2]))
                ch.join()
                ch.done(nc.scalar.activation(sp_e[:], sp_a[:], ACT.Exp, scale=-1.0))
                ch.join()
                nc.scalar.activation(sp_l[:], sp_e[:], ACT.Ln, bias=1.0).then_inc(soft_ready, 1)

            def scan(b, u, ahead):
                act.wait_ge(dt_ready, at(b, u, 1, 1))
                for n in range(N):
                    act.wait_ge(hs_ready, at(b, u, N, max(n - DA + 1, 0)))
                    nc.scalar.activation(dA[:, n % DA], dt[:, u], ACT.Exp, scale=A[:, u, n:n + 1]).then_inc(dA_ready, 1)
                    if ahead and n in (AT_IN + 2, AT_LOW + 2, AT_TIME + 2):
                        {AT_IN + 2: halves, AT_LOW + 2: copy_low_rank, AT_TIME + 2: soft}[n](*ahead)
                if u:
                    act.wait_ge(res_ready, CREDIT + b + 1)
                    nc.scalar.activation(g.s[:, bass.ds(b * TILES, TILES), :], res[:], ACT.Gelu).then_inc(s_ready, 1)

            halves(0, 0)
            copy_low_rank(0, 0)
            soft(0, 0)
            both_ways(act, scan, ch.restart)


MAMBA_PRE = 2 * NT + 3


DEPTH, WINDOW, DI = 6, 32, int(D * 4 * 2 / 3)


def l2_ffn_stage(g):
    nc = g.nc
    HD = HEADS * DH
    QB = 64
    KW = WINDOW + QB
    QBS = P // QB
    QUAD = 4
    QUADS = PAIRS // QUAD
    PER = QBS * QUADS
    STEPS2 = TILES * PER
    CH = [(0, P), (P, P), (2 * P, DI - 2 * P)]
    NLOAD = 12
    ITERATIONS = DEPTH * BATCH
    LOG_BATCH = BATCH.bit_length() - 1
    NONE = (None, None)
    assert BATCH == 1 << LOG_BATCH
    with ExitStack() as stack:
        sb, once, sem = scope(nc, stack, "l2f")
        wqkv = sb("wqkv", [P, 2, 3 * HD])
        wo = sb("wo", [P, 2, PAIRS, D])
        w1 = sb("w1", [P, 2, 2 * DI])
        w2 = sb("w2", [P, 2, 3, D])
        b1 = sb("b1", [P, 2, 2 * DI])
        b2 = sb("b2", [P, 2, D])
        qks = sb("qks", [P, 2, 2, DH])
        lnp = sb("lnp", [P, DEPTH + 1, 2])
        lnd = sb("lnd", [P, 2])
        rope = sb("rope", [P, 2, 2, TILES, DH])
        rot = sb("rot", [P, 2, 2, TILES, DH])
        band_f = sb("band_f", [P, 2, KW])
        band = sb("band", [P, 2, KW], BF16)
        step_down = sb("step_down", [P, 2, P])
        yb = sb("yb", [P, TILES, D])
        xsT = sb("xsT", [P, WINDOW + SEQ + 1])
        nrm = g.xnT[:].rearrange("p (k c) -> p k c", k=2)
        swp = g.xn[:].rearrange("p t d -> p (t d)").rearrange("p (k c) -> p k c", k=2)
        cosd = sb("cosd", [P, 2, HD])
        qz = sb("qz", [P, PAIRS, 2, QBS, 2, QB])
        kT = sb("kT", [P, PAIRS, WINDOW + SEQ])
        vw = sb("vw", [KW, 2 * QBS, HD])
        p = sb("p", [P, 2, QUAD, KW])
        pT = sb("pT", [KW, 2, QUAD, P])
        oT = sb("oT", [P, PAIRS, 2, P])
        ss = sb("ss", [P, 2, HEADS])
        rn = sb("rn", [P, 2, HEADS])
        negmax = sb("negmax", [P, STEPS2 * QUAD])
        rowsum = sb("rowsum", [P, STEPS2 * QUAD])
        rinv = sb("rinv", [P, STEPS2 * QUAD])
        stats = sb("stats", [P, 2, 6])
        mv = sb("mv", [P, 2])
        rstd = sb("rstd", [P, 1])
        xn2 = sb("xn2", [P, D])
        xnT2 = sb("xnT2", [P, P])
        ha = sb("ha", [P, DI])
        hg = sb("hg", [P, DI])
        hh = sb("hh", [P, DI])
        hT = sb("hT", [P, 3, P])
        yt = sb("yt", [P, D])
        const_loaded = once("const_loaded")
        loaded = once("loaded")
        y_started = once("y_started")
        band_ready = once("band_ready")
        pad_ready = once("pad_ready")
        dve_step = once("dve_step")
        act_step = once("act_step")
        rot_ready = sem("rot_ready")
        yb_ready = sem("yb_ready")
        lnd_ready = sem("lnd_ready")
        y_turned = sem("y_turned")
        xs_ready = sem("xs_ready")
        projected = sem("projected")
        sq_ready = sem("sq_ready")
        ss_ready = sem("ss_ready")
        rn_ready = sem("rn_ready")
        nrm_ready = sem("nrm_ready")
        cos_ready = sem("cos_ready")
        rotated = sem("rotated")
        qk_turned = sem("qk_turned")
        q_copied = sem("q_copied")
        k_copied = sem("k_copied")
        v_copied = sem("v_copied")
        scores_ready = sem("scores_ready")
        negmax_ready = sem("negmax_ready")
        probs_ready = sem("probs_ready")
        rinv_ready = sem("rinv_ready")
        scaled = sem("scaled")
        turned = sem("turned")
        pT_copied = sem("pT_copied")
        pv_done = sem("pv_done")
        oT_copied = sem("oT_copied")
        mixed = sem("mixed")
        y_mixed = sem("y_mixed")
        shifted = sem("shifted")
        moments = sem("moments")
        rstd_ready = sem("rstd_ready")
        xn2_ready = sem("xn2_ready")
        xn2_turned = sem("xn2_turned")
        xnT2_ready = sem("xnT2_ready")
        hid_ready = sem("hid_ready")
        hg_ready = sem("hg_ready")
        ha_ready = sem("ha_ready")
        gelu_ready = sem("gelu_ready")
        hh_ready = sem("hh_ready")
        hh_turned = sem("hh_turned")
        hT_ready = sem("hT_ready")
        ff_ready = sem("ff_ready")
        yt_ready = sem("yt_ready")
        y_ready = sem("y_ready")
        y_final = once("y_final")

        def at(it, per, k):
            return CREDIT + k + it * per

        def weight_slot(it):
            return (it >> LOG_BATCH) & 1

        def slots(it, first=False, last=False):
            for t in range(TILES):
                ahead = (it, t + 1) if t + 1 < TILES else NONE if last else (it + 1, 0)
                behind = (it, t - 1) if t else NONE if first else (it - 1, TILES - 1)
                yield ahead, (it, t), behind

        def all_iterations(eng, slot, end=lambda: None):
            slot((0, 0), NONE, NONE)
            for stages in slots(0, first=True):
                slot(*stages)
            end()
            with eng.Fori(1, ITERATIONS - 1) as it:
                for stages in slots(it):
                    slot(*stages)
                end()
            for stages in slots(ITERATIONS - 1, last=True):
                slot(*stages)
            slot(NONE, NONE, (ITERATIONS - 1, TILES - 1))
            end()

        def banks(b0, n):
            return g.ps[:, b0:b0 + n].rearrange("p a c -> p (a c)")

        def step_of(n):
            return n // PER, n % PER // QUADS, n % QUADS

        block = stack.enter_context(nc.Block())

        @block.sync
        def _(sp):
            start_counts(sp, sem)
            sp.dma_start(rope[:], g.c["rope"]).then_inc(const_loaded, 16)
            sp.dma_start(band_f[:], g.c["band"]).then_inc(const_loaded, 16)
            sp.dma_start(step_down[:], g.c["step_down"]).then_inc(const_loaded, 16)
            sp.dma_start(lnp[:, 0:DEPTH], g.w["L2_ffn_ln"]).then_inc(const_loaded, 16)
            for d in range(DEPTH):
                s = d % 2
                if d >= 1:
                    sp.wait_ge(loaded, 16 * NLOAD * d)
                if d >= 2:
                    sp.wait_ge(y_ready, CREDIT + (d - 1) * BATCH * TILES)
                for i, n in enumerate(("q_scale", "k_scale")):
                    sp.dma_start(qks[:, s, i], g.w[f"L2_ffn_{n}"][d].partition_broadcast(P)).then_inc(loaded, 16)
                for c in range(3):
                    sp.dma_start(wqkv[:, s, c * HD:(c + 1) * HD],
                                 g.w["L2_ffn_Wqkv"][d, :, c * HD:(c + 1) * HD]).then_inc(loaded, 16)
                sp.dma_start(wo[:, s], g.w["L2_ffn_Wo"][d]).then_inc(loaded, 16)
                sp.dma_start(w1[:, s], g.w["L2_ffn_W1"][d]).then_inc(loaded, 16)
                for c, (r0, rows) in enumerate(CH):
                    sp.dma_start(w2[0:rows, s, c], g.w["L2_ffn_W2"][d, r0:r0 + rows]).then_inc(loaded, 16)
                sp.dma_start(b1[:, s], g.w["L2_ffn_b1"][d].partition_broadcast(P)).then_inc(loaded, 16)
                sp.dma_start(b2[:, s], g.w["L2_ffn_b2"][d].partition_broadcast(P)).then_inc(loaded, 16)

        @block.gpsimd
        def _(pool):
            def inverse_norms(it, t, k):
                if t is not None:
                    pool.wait_ge(ss_ready, at(it, 2 * TILES, 2 * t + k + 1))
                    nc.gpsimd.tensor_tensor(rn[:, k], ss[:, k], g.neghalf[:, 0:HEADS], ALU.pow).then_inc(rn_ready, 1)

            def cosines(it, t, k):
                if t is not None:
                    pool.wait_ge(rot_ready, at(it, 6, 6))
                    pool.wait_ge(nrm_ready, at(it, 2 * TILES, 2 * t + k + 1))
                    nc.gpsimd.tensor_tensor(
                        cosd[:, k].rearrange("p (h d) -> p h d", d=DH), nrm[:, k].rearrange("p (h d) -> p h d", d=DH),
                        rot[:, k, 0, t].unsqueeze(1).broadcast_to([P, HEADS, DH]), ALU.mult).then_inc(cos_ready, 1)

            def scaled_rotary(it, t):
                if t == 0:
                    pool.wait_ge(loaded, (it >> LOG_BATCH) * (16 * NLOAD) + 16 * NLOAD)
                    pool.wait_ge(rotated, at(it, 2 * TILES, 0))
                    for k in range(2):
                        sc = qks[:, bass.ds(weight_slot(it), 1), k].broadcast_to([P, TILES, DH])
                        nc.gpsimd.tensor_tensor(rot[:, k, 0], rope[:, k, 0], sc, ALU.mult).then_inc(rot_ready, 1)
                        for to, frm in ((0, 32), (32, 0)):
                            sc = qks[:, bass.ds(weight_slot(it), 1), k, frm:frm + 32].broadcast_to([P, TILES, 32])
                            nc.gpsimd.tensor_tensor(rot[:, k, 1, :, to:to + 32], rope[:, k, 1, :, to:to + 32],
                                                    sc, ALU.mult).then_inc(rot_ready, 1)

            def inverse_deviation(it, t):
                if t is not None:
                    pool.wait_ge(moments, at(it, TILES, t + 1))
                    nc.gpsimd.tensor_tensor(rstd[:], mv[:, 1:2], g.neghalf[:, 0:1], ALU.pow).then_inc(rstd_ready, 1)

            def slot(ahead, now, behind):
                inverse_deviation(*behind)
                inverse_norms(*ahead, 0)
                scaled_rotary(*ahead)
                inverse_norms(*ahead, 1)
                cosines(*ahead, 0)
                cosines(*ahead, 1)

            pool.wait_ge(const_loaded, 64)
            all_iterations(pool, slot)

        @block.tensor
        def _(pe):
            pe.wait_ge(band_ready, 1)

            def turn_y(it, t):
                if t is not None:
                    pe.wait_ge(yb_ready, at(it, TILES, t + 1))
                    pe.wait_ge(yt_ready, at(it, TILES, t - 2))
                    nc.tensor.transpose(g.ps[:, 7, 0:P], yb[:, t], g.ident[:]).then_inc(y_turned, 1)

            def project(it, t, k):
                if t is None:
                    return
                if k == 0:
                    if t == 0:
                        pe.wait_ge(loaded, (it >> LOG_BATCH) * (16 * NLOAD) + 16 * NLOAD)
                    pe.wait_ge(xs_ready, at(it, 2 * TILES, 2 * t + 2))
                    pe.wait_ge(q_copied, at(it, 2 * TILES, 2 * t))
                elif k == 1:
                    pe.wait_ge(k_copied, at(it, TILES, t))
                else:
                    pe.wait_ge(nrm_ready, at(it, 2 * TILES, 2 * t + k - 1))
                if k < 2:
                    x, rows, c0 = xsT[:, WINDOW + t * P:WINDOW + (t + 1) * P], P, k * HD
                else:
                    w = QBS * t + k - 2
                    x, rows, c0 = xsT[:, w * QB:w * QB + KW], KW, 2 * HD
                for hf in range(2):
                    ins = nc.tensor.matmul(g.ps[0:rows, 2 * (k % 2) + hf], x,
                                           wqkv[:, bass.ds(weight_slot(it), 1), c0 + hf * 512:c0 + (hf + 1) * 512]
                                           .rearrange("p a c -> p (a c)"), start=True, stop=True)
                ins.then_inc(projected, 1)

            def turn_qk(it, t, k):
                if t is None:
                    return
                pe.wait_ge(rotated, at(it, 2 * TILES, 2 * t + k + 1))
                pe.wait_ge(v_copied, at(it, 2 * TILES, 2 * t + k + 1))
                for c in range(PAIRS):
                    ins = nc.tensor.transpose(g.ps[:, 2 * k + c // 4, (c % 4) * P:(c % 4 + 1) * P],
                                              cosd[:, k, c * P:(c + 1) * P], g.ident[:])
                ins.then_inc(qk_turned, 1)

            def scores(it, t, i):
                if t is None:
                    return
                n = PER * t + i
                _, j, quad = step_of(n)
                if i == 0:
                    pe.wait_ge(q_copied, at(it, 2 * TILES, 2 * t + 2))
                    pe.wait_ge(k_copied, at(it, TILES, t + 1))
                pe.wait_ge(probs_ready, at(it, STEPS2, n))
                out = g.ps[:, 4, 0:QUAD * KW]
                w = QBS * t + j
                nc.tensor.matmul(out, g.identb[:], band[:, 1 if w else 0].unsqueeze(1).broadcast_to([P, QUAD, KW]),
                                 start=True, stop=False)
                for c in range(QUAD):
                    pair = quad * QUAD + c
                    ins = nc.tensor.matmul(out[:, c * KW:(c + 1) * KW],
                                           qz[:, pair, t % 2, j].rearrange("p h q -> p (h q)"),
                                           kT[:, pair, w * QB:w * QB + KW], start=False, stop=(c == QUAD - 1))
                ins.then_inc(scores_ready, 1)

            def turn(it, t, i):
                if t is None:
                    return
                n = PER * t + i
                pe.wait_ge(scaled, at(it, STEPS2, n + 1))
                pe.wait_ge(pT_copied, at(it, STEPS2, n))
                for c in range(QUAD):
                    ins = nc.tensor.transpose(g.ps[0:KW, 5, c * P:(c + 1) * P], p[:, n % 2, c], g.ident[:])
                ins.then_inc(turned, 1)

            def pv(it, t, i):
                if t is None:
                    return
                n = PER * t + i
                _, j, quad = step_of(n)
                if i == 0:
                    pe.wait_ge(v_copied, at(it, 2 * TILES, 2 * t + 2))
                    pe.wait_ge(y_mixed, at(it, TILES, t))
                pe.wait_ge(pT_copied, at(it, STEPS2, n + 1))
                pe.wait_ge(oT_copied, at(it, 2 * STEPS2, 2 * n))
                for c in range(QUAD):
                    pair = quad * QUAD + c
                    ins = nc.tensor.matmul(g.ps[:, 6, c * P:(c + 1) * P],
                                           vw[:, (QBS * t + j) % (2 * QBS), pair * P:(pair + 1) * P],
                                           pT[:, n % 2, c], start=True, stop=True)
                ins.then_inc(pv_done, 1)

            def mix(it, t):
                if t is None:
                    return
                pe.wait_ge(oT_copied, at(it, 2 * STEPS2, 2 * PER * (t + 1)))
                for c in range(PAIRS):
                    ins = nc.tensor.matmul(g.ps[:, 6, 0:D], oT[:, c, t % 2],
                                           wo[:, bass.ds(weight_slot(it), 1), c].rearrange("p a c -> p (a c)"),
                                           start=(c == 0), stop=(c == PAIRS - 1))
                ins.then_inc(mixed, 1)

            def shift(it, t):
                if t is None:
                    return
                pe.wait_ge(y_mixed, at(it, TILES, t + 1))
                last = isinstance(it, int) and it == ITERATIONS - 1
                pe.wait_ge(xs_ready, at(it, 2 * TILES, 2 * min(t + 3, TILES if last else t + 3)))
                ins = nc.tensor.matmul(g.ps[:, 7, 0:D // 2], step_down[:, 0], yb[:, t, D // 2:D],
                                       start=True, stop=(t == 0))
                if t:
                    ins = nc.tensor.matmul(g.ps[:, 7, 0:D // 2], step_down[:, 1], yb[:, t - 1, D // 2:D],
                                           start=False, stop=True)
                ins.then_inc(shifted, 1)

            def turn_xn2(it, t):
                if t is None:
                    return
                pe.wait_ge(xn2_ready, at(it, 2 * TILES, 2 * t + 2))
                nc.tensor.transpose(g.ps[:, 7, 0:P], xn2[:], g.ident[:]).then_inc(xn2_turned, 1)

            def hidden(it, t, hf):
                if t is None:
                    return
                if hf:
                    pe.wait_ge(xnT2_ready, at(it, TILES, t + 1))
                else:
                    pe.wait_ge(hg_ready, at(it, TILES, t + 1))
                nc.tensor.matmul(g.ps[:, 7, 0:DI], xnT2[:],
                                 w1[:, bass.ds(weight_slot(it), 1), hf * DI:(hf + 1) * DI].rearrange("p a c -> p (a c)"),
                                 start=True, stop=True).then_inc(hid_ready, 1)

            def turn_hidden(it, t):
                if t is None:
                    return
                pe.wait_ge(hh_ready, at(it, TILES, t + 1))
                for c, (r0, rows) in enumerate(CH):
                    ins = nc.tensor.transpose(g.ps[0:rows, 7, c * P:(c + 1) * P], hh[:, r0:r0 + rows], g.ident[:])
                ins.then_inc(hh_turned, 1)

            def feed(it, t):
                if t is None:
                    return
                pe.wait_ge(hT_ready, at(it, 2 * TILES, 2 * t + 2))
                for c, (r0, rows) in enumerate(CH):
                    ins = nc.tensor.matmul(g.ps[:, 7, 0:D], hT[0:rows, c],
                                           w2[0:rows, bass.ds(weight_slot(it), 1), c].rearrange("p a c -> p (a c)"),
                                           start=(c == 0), stop=(c == 2))
                ins.then_inc(ff_ready, 1)

            def slot(ahead, now, behind):
                mix(*behind)
                turn_y(*ahead)
                scores(*now, 0)
                shift(*behind)
                project(*ahead, 0)
                scores(*now, 1)
                turn(*now, 0)
                project(*ahead, 1)
                turn_xn2(*behind)
                scores(*now, 2)
                turn(*now, 1)
                pv(*now, 0)
                hidden(*behind, 1)
                scores(*now, 3)
                project(*ahead, 2)
                turn(*now, 2)
                pv(*now, 1)
                hidden(*behind, 0)
                project(*ahead, 3)
                turn(*now, 3)
                pv(*now, 2)
                turn_hidden(*behind)
                turn_qk(*ahead, 0)
                pv(*now, 3)
                feed(*behind)
                turn_qk(*ahead, 1)

            all_iterations(pe, slot)

        @block.vector
        def _(dve):
            nc.vector.tensor_copy(g.gate[:], g.xn[:]).then_inc(y_started, 1)
            nc.vector.memset(xsT[:], 0.0)
            nc.vector.memset(qz[:], 0.0)
            nc.vector.memset(kT[:], 0.0).then_inc(pad_ready, 1)
            dve.wait_ge(const_loaded, 64)
            nc.vector.tensor_copy(band[:], band_f[:]).then_inc(band_ready, 1)
            dve.wait_ge(y_started, 1)
            dve.wait_ge(pad_ready, 1)
            SW = ((0, 32), (32, 0))

            def heads(x):
                return x.rearrange("p (h d) -> p h d", d=DH)

            def fetch(it, t):
                if t is None:
                    return
                dve.wait_ge(y_ready, at(it, TILES, t - 3))
                nc.vector.tensor_copy(yb[:, t], g.gate[:, bass.ds((it & (BATCH - 1)) * TILES + t, 1), :]
                                      .rearrange("p a d -> p (a d)")).then_inc(yb_ready, 1)

            def affine_of(it, t):
                if t == 0:
                    dve.wait_ge(xnT2_ready, at(it, TILES, 0))
                    nc.vector.tensor_copy(lnd[:], lnp[:, bass.ds(it >> LOG_BATCH, 1)]
                                          .rearrange("p a c -> p (a c)")).then_inc(lnd_ready, 1)

            def norms(ch, it, t, k):
                if t is None:
                    return
                dve.wait_ge(sq_ready, at(it, 2 * TILES, 2 * t + k + 1))
                ch.done(nc.vector.tensor_reduce(ss[:, k], heads(cosd[:, k]), AX_X, ALU.add))
                ch.join()
                nc.vector.tensor_scalar(ss[:, k], ss[:, k], 1e-24, None, ALU.max).then_inc(ss_ready, 1)

            def normalize(it, t, k):
                if t is None:
                    return
                dve.wait_ge(rn_ready, at(it, 2 * TILES, 2 * t + k + 1))
                nc.vector.tensor_tensor(heads(nrm[:, k]), heads(banks(2 * k, 2)),
                                        rn[:, k].unsqueeze(2).broadcast_to([P, HEADS, DH]), ALU.mult).then_inc(nrm_ready, 1)

            def swap(ch, it, t, k):
                if t is None:
                    return
                dve.wait_ge(rot_ready, at(it, 6, 6))
                dve.wait_ge(nrm_ready, at(it, 2 * TILES, 2 * t + k + 1))
                for to, frm in SW:
                    ch.done(nc.vector.tensor_tensor(
                        heads(swp[:, k])[:, :, to:to + 32], heads(nrm[:, k])[:, :, frm:frm + 32],
                        rot[:, k, 1, t, to:to + 32].unsqueeze(1).broadcast_to([P, HEADS, 32]), ALU.mult))

            def rotate(ch, it, t, k):
                if t is None:
                    return
                ch.join()
                dve.wait_ge(cos_ready, at(it, 2 * TILES, 2 * t + k + 1))
                nc.vector.tensor_tensor(cosd[:, k], cosd[:, k], swp[:, k], ALU.add).then_inc(rotated, 1)

            def maxima(it, t, i):
                if t is None:
                    return
                n = PER * t + i
                dve.wait_ge(scores_ready, at(it, STEPS2, n + 1))
                nc.vector.tensor_reduce(negmax[:, QUAD * n:QUAD * (n + 1)],
                                        g.ps[:, 4, 0:QUAD * KW].rearrange("p (c k) -> p c k", k=KW),
                                        AX_X, ALU.max, negate=True).then_inc(negmax_ready, 1)

            def scale(it, t, i):
                if t is None:
                    return
                n = PER * t + i
                dve.wait_ge(probs_ready, at(it, STEPS2, n + 1))
                nc.vector.reciprocal(rinv[:, QUAD * n:QUAD * (n + 1)],
                                     rowsum[:, QUAD * n:QUAD * (n + 1)]).then_inc(rinv_ready, 1)
                dve.wait_ge(rinv_ready, at(it, STEPS2, n + 1))
                nc.vector.tensor_tensor(
                    p[:, n % 2], p[:, n % 2],
                    rinv[:, QUAD * n:QUAD * (n + 1)].unsqueeze(2).broadcast_to([P, QUAD, KW]), ALU.mult).then_inc(scaled, 1)

            def copy_probs(it, t, i):
                if t is None:
                    return
                n = PER * t + i
                dve.wait_ge(turned, at(it, STEPS2, n + 1))
                dve.wait_ge(pv_done, at(it, STEPS2, n - 1))
                nc.vector.tensor_copy(pT[:, n % 2].rearrange("p c q -> p (c q)"), g.ps[0:KW, 5]).then_inc(pT_copied, 1)

            def moments_of(ch, it, t):
                if t is None:
                    return
                dve.wait_ge(y_mixed, at(it, TILES, t + 1))
                ch.done(nc.vector.bn_stats(stats[:, 0], yb[:, t, 0:D // 2]))
                dve.wait_ge(shifted, at(it, TILES, t + 1))
                ch.done(nc.vector.bn_stats(stats[:, 1], g.ps[:, 7, 0:D // 2]))
                ch.join()
                ch.done(nc.vector.bn_aggr(mv[:], stats[:]))
                ch.join()
                nc.vector.tensor_scalar(mv[:, 1:2], mv[:, 1:2], LN_EPS, None, ALU.add).then_inc(moments, 1)

            def normalize_shifted(it, t):
                if t is None:
                    return
                dve.wait_ge(rstd_ready, at(it, TILES, t + 1))
                nc.vector.tensor_scalar(xn2[:, 0:D // 2], yb[:, t, 0:D // 2], mv[:, 0:1], rstd[:],
                                        ALU.subtract, ALU.mult).then_inc(xn2_ready, 1)
                nc.vector.tensor_scalar(xn2[:, D // 2:D], g.ps[:, 7, 0:D // 2], mv[:, 0:1], rstd[:],
                                        ALU.subtract, ALU.mult).then_inc(xn2_ready, 1)

            def bias_hidden(it, t, hf):
                if t is None:
                    return
                dve.wait_ge(hid_ready, at(it, 2 * TILES, 2 * t + 2 - hf))
                nc.vector.tensor_tensor((ha, hg)[hf][:], g.ps[:, 7, 0:DI],
                                        b1[:, bass.ds(weight_slot(it), 1), hf * DI:(hf + 1) * DI].rearrange("p a c -> p (a c)"),
                                        ALU.add).then_inc((ha_ready, hg_ready)[hf], 1)

            def gate_hidden(it, t):
                if t is None:
                    return
                dve.wait_ge(ha_ready, at(it, TILES, t + 1))
                dve.wait_ge(gelu_ready, at(it, TILES, t + 1))
                nc.vector.tensor_tensor(hh[:], ha[:], hg[:], ALU.mult).then_inc(hh_ready, 1)

            def feed_out(it, t):
                if t is None:
                    return
                dve.wait_ge(ff_ready, at(it, TILES, t + 1))
                nc.vector.tensor_tensor(yt[:], g.ps[:, 7, 0:D], yb[:, t], ALU.add).then_inc(yt_ready, 1)
                dve.wait_ge(yt_ready, at(it, TILES, t + 1))
                nc.vector.tensor_tensor(g.gate[:, bass.ds((it & (BATCH - 1)) * TILES + t, 1), :].rearrange("p a d -> p (a d)"),
                                        yt[:], b2[:, bass.ds(weight_slot(it), 1), :].rearrange("p a d -> p (a d)"),
                                        ALU.add).then_inc(y_ready, 1)

            def mix_out(it, t):
                if t is None:
                    return
                dve.wait_ge(mixed, at(it, TILES, t + 1))
                nc.vector.tensor_tensor(yb[:, t], yb[:, t], g.ps[:, 6, 0:D], ALU.add).then_inc(y_mixed, 1)

            def slot(ahead, now, behind):
                fetch(*ahead)
                mix_out(*behind)
                maxima(*now, 0)
                affine_of(*behind)
                moments_of(ch, *behind)
                scale(*now, 0)
                normalize_shifted(*behind)
                maxima(*now, 1)
                norms(ch, *ahead, 0)
                copy_probs(*now, 0)
                scale(*now, 1)
                maxima(*now, 2)
                norms(ch, *ahead, 1)
                copy_probs(*now, 1)
                normalize(*ahead, 0)
                scale(*now, 2)
                maxima(*now, 3)
                bias_hidden(*behind, 1)
                swap(ch, *ahead, 0)
                normalize(*ahead, 1)
                scale(*now, 3)
                copy_probs(*now, 2)
                bias_hidden(*behind, 0)
                rotate(ch, *ahead, 0)
                gate_hidden(*behind)
                swap(ch, *ahead, 1)
                copy_probs(*now, 3)
                rotate(ch, *ahead, 1)
                feed_out(*behind)

            ch = Chain(dve, dve_step)
            all_iterations(dve, slot, ch.restart)
            dve.wait_ge(y_ready, CREDIT + DEPTH * BATCH * TILES)

        @block.scalar
        def _(act):
            act.wait_ge(pad_ready, 1)

            def shift_copies(it, t):
                if t is not None:
                    act.wait_ge(y_turned, at(it, TILES, t + 1))
                    c0 = WINDOW + t * P
                    nc.scalar.copy(xsT[0:64, c0:c0 + P], g.ps[0:64, 7, 0:P]).then_inc(xs_ready, 1)
                    nc.scalar.copy(xsT[64:P, c0 + 1:c0 + P + 1], g.ps[64:P, 7, 0:P]).then_inc(xs_ready, 1)

            def squares(it, t, k):
                if t is not None:
                    act.wait_ge(projected, at(it, 4 * TILES, 4 * t + k + 1))
                    nc.scalar.activation(cosd[:, k], banks(2 * k, 2), ACT.Square).then_inc(sq_ready, 1)

            def copy_values(it, t, j):
                if t is not None:
                    act.wait_ge(projected, at(it, 4 * TILES, 4 * t + j + 3))
                    nc.scalar.copy(vw[:, (QBS * t + j) % (2 * QBS)], banks(2 * j, 2)[0:KW]).then_inc(v_copied, 1)

            def copy_q(it, t):
                if t is not None:
                    act.wait_ge(qk_turned, at(it, 2 * TILES, 2 * t + 1))
                    for hf in range(2):
                        rows = slice(hf * DH, (hf + 1) * DH)
                        for c in range(0, PAIRS, 4):
                            ins = nc.scalar.copy(qz[rows, c:c + 4, t % 2, :, hf],
                                                 g.ps[rows, c // 4].rearrange("p (c j q) -> p c j q", c=4, q=QB))
                        ins.then_inc(q_copied, 1)

            def copy_k(it, t):
                if t is not None:
                    act.wait_ge(qk_turned, at(it, 2 * TILES, 2 * t + 2))
                    nc.scalar.copy(kT[:, :, WINDOW + t * P:WINDOW + (t + 1) * P],
                                   banks(2, 2).rearrange("p (c q) -> p c q", c=PAIRS)).then_inc(k_copied, 1)

            def exps(ch, it, t, i):
                if t is None:
                    return
                n = PER * t + i
                act.wait_ge(negmax_ready, at(it, STEPS2, n + 1))
                act.wait_ge(turned, at(it, STEPS2, n - 1))
                for c in range(QUAD):
                    col = QUAD * n + c
                    ins = nc.scalar.activation(p[:, n % 2, c], g.ps[:, 4, c * KW:(c + 1) * KW], ACT.Exp,
                                               bias=negmax[:, col:col + 1], accum_out=rowsum[:, col:col + 1])
                    if c < QUAD - 1:
                        ch.done(ins)
                ins.then_inc(probs_ready, 1)

            def copy_outputs(it, t, i):
                if t is None:
                    return
                n = PER * t + i
                _, j, quad = step_of(n)
                act.wait_ge(pv_done, at(it, STEPS2, n + 1))
                for hf in range(2):
                    rows = slice(hf * DH, (hf + 1) * DH)
                    nc.scalar.copy(oT[rows, quad * QUAD:(quad + 1) * QUAD, t % 2, j * QB:(j + 1) * QB],
                                   g.ps[rows, 6].rearrange("p (c h q) -> p c h q", h=2, q=QB)[:, :, hf]).then_inc(oT_copied, 1)

            def affine(it, t):
                if t is not None:
                    act.wait_ge(lnd_ready, at(it, 1, 1))
                    act.wait_ge(xn2_turned, at(it, TILES, t + 1))
                    nc.scalar.activation(xnT2[:], g.ps[:, 7, 0:P], ACT.Identity, bias=lnd[:, 1:2],
                                         scale=lnd[:, 0:1]).then_inc(xnT2_ready, 1)

            def gelu(it, t):
                if t is not None:
                    act.wait_ge(hg_ready, at(it, TILES, t + 1))
                    nc.scalar.activation(hg[:], hg[:], ACT.Gelu).then_inc(gelu_ready, 1)

            def copy_hidden(it, t):
                if t is not None:
                    act.wait_ge(hh_turned, at(it, TILES, t + 1))
                    nc.scalar.copy(hT[:, 0:2], g.ps[:, 7, 0:2 * P].rearrange("p (c n) -> p c n", c=2)).then_inc(hT_ready, 1)
                    nc.scalar.copy(hT[0:CH[2][1], 2], g.ps[0:CH[2][1], 7, 2 * P:3 * P]).then_inc(hT_ready, 1)

            def slot(ahead, now, behind):
                shift_copies(*ahead)
                exps(ch, *now, 0)
                squares(*ahead, 0)
                exps(ch, *now, 1)
                squares(*ahead, 1)
                affine(*behind)
                copy_outputs(*now, 0)
                exps(ch, *now, 2)
                exps(ch, *now, 3)
                copy_outputs(*now, 1)
                gelu(*behind)
                copy_values(*ahead, 0)
                copy_values(*ahead, 1)
                copy_outputs(*now, 2)
                copy_hidden(*behind)
                copy_q(*ahead)
                copy_outputs(*now, 3)
                copy_k(*ahead)

            ch = Chain(act, act_step)
            all_iterations(act, slot, ch.restart)
            act.wait_ge(y_ready, CREDIT + DEPTH * BATCH * TILES)
            nc.scalar.activation(g.gate[:], g.gate[:], ACT.Silu).then_inc(y_final, 1)


def l3_attn_stage(g):
    nc = g.nc
    W = D // HEADS
    QB = P // HEADS
    GROUP = 8
    M = SEQ // W
    with ExitStack() as stack:
        sb, once, sem = scope(nc, stack, "l3a")
        wq = sb("wq", [P, D])
        heads = sb("heads", [P, HEADS])
        wk = sb("wk", [P, D])
        wv = sb("wv", [P, D])
        kF = sb("kF", [P, BATCH, W, M])
        kT_all = sb("kT_all", [P, BATCH, SEQ])
        xb = sb("xb", [P, SEQ])
        qT = sb("qT", [P, SEQ])
        qz = sb("qz", [P, SEQ // QB, HEADS, QB])
        kT = sb("kT", [P, SEQ])
        v = sb("v", [P, TILES, D])
        own = sb("own", [P, 2, GROUP, HEADS, QB])
        oT = sb("oT", [P, SEQ])
        kd = nc.dram_tensor("k_turn", (BATCH, P, W, M), F32).ap()
        loaded = once("loaded")
        zeroed = once("zeroed")
        kF_product = once("kF_product")
        kF_ready = once("kF_ready")
        kd_stored = once("kd_stored")
        kT_loaded = once("kT_loaded")
        xb_ready = sem("xb_ready")
        kT_ready = sem("kT_ready")
        q_ready = sem("q_ready")
        q_copied = sem("q_copied")
        qz_ready = sem("qz_ready")
        summed = sem("summed")
        o_turned = sem("o_turned")
        v_ready = sem("v_ready")
        v_copied = sem("v_copied")
        o_stored = sem("o_stored")
        GROUPS = SEQ // QB // GROUP

        def collect(dve, b, n):
            i, j = n // GROUP, n % GROUP
            dve.wait_ge(at.pv_done, at.at(b, n + 1))
            nc.vector.tensor_tensor(own[:, i % 2, j], g.ps[:, 6 + n % 2, 0:P].rearrange("p (h q) -> p h q", q=QB),
                                    heads[:].unsqueeze(2).broadcast_to([P, HEADS, QB]), ALU.mult).then_inc(at.collected, 1)
            if j == GROUP - 1:
                dve.wait_ge(at.collected, at.at(b, n + 1))
                dve.wait_ge(o_turned, CREDIT + b)
                nc.vector.tensor_reduce(oT[:, i * GROUP * QB:(i + 1) * GROUP * QB].rearrange("p (j q) -> p j q", q=QB),
                                        own[:, i % 2].rearrange("p j h q -> p j q h"), AX_X, ALU.add).then_inc(summed, 1)

        at = Softmax(g, sb, sem, steps=SEQ // QB, keys=lambda n: QB * (n + 1),
                     q=lambda n: qz[:, n].rearrange("p h q -> p (h q)"), k=lambda n, c0, c1: kT[:, c0:c1],
                     v=lambda n, c, rows: v[0:rows, c], mask=lambda n: g.causal8[:], collect=collect, copier="act")
        block = stack.enter_context(nc.Block())
        w = g.w["L3_attn_qkv_weights"]

        @block.sync
        def _(sp):
            start_counts(sp, sem)
            sp.dma_start(wk[:], w[:, D:2 * D]).then_inc(loaded, 16)
            sp.dma_start(wv[:], w[:, 2 * D:3 * D]).then_inc(loaded, 16)
            sp.dma_start(wq[:], w[:, 0:D]).then_inc(loaded, 16)
            sp.dma_start(heads[:], g.c["heads"]).then_inc(loaded, 16)
            for b in range(BATCH):
                sp.wait_ge(kF_ready, b + 1)
                sp.dma_start(kd[b], kF[:, b]).then_inc(kd_stored, 16)
            sp.wait_ge(kd_stored, 16 * BATCH)
            for b in range(BATCH):
                for h in range(HEADS):
                    sp.dma_start(kT_all[h * W:(h + 1) * W, b].rearrange("c (d m) -> c d m", d=W),
                                 kd[b, h * W:(h + 1) * W].rearrange("d c m -> c d m")).then_inc(kT_loaded, 16)

        @block.gpsimd
        def _(pool):
            with pool.Fori(0, BATCH) as b:
                pool.wait_ge(v_ready, CREDIT + b)
                nc.gpsimd.tensor_copy(xb[:], g.xnT[:, bass.ds(b * SEQ, SEQ)]).then_inc(xb_ready, 1)
                at.pool(pool, b)

        @block.tensor
        def _(pe):
            pe.wait_ge(loaded, 16 * 4)
            for b in range(BATCH):
                nc.tensor.matmul(g.ps[:, b], wk[:], g.xnT[:, b * SEQ:(b + 1) * SEQ],
                                 start=True, stop=True).then_inc(kF_product, 1)
            pe.wait_ge(kF_ready, BATCH)
            with pe.Fori(0, BATCH) as b:
                pe.wait_ge(xb_ready, CREDIT + b + 1)
                nc.tensor.matmul(g.ps[:, 4], wq[:], xb[:], start=True, stop=True).then_inc(q_ready, 1)
                for t in range(TILES):
                    ins = nc.tensor.matmul(g.ps[:, 6, t * P:(t + 1) * P], xb[:, t * P:(t + 1) * P], wv[:],
                                           start=True, stop=True)
                ins.then_inc(v_ready, 1)
                pe.wait_ge(qz_ready, CREDIT + (b + 1) * TILES)
                pe.wait_ge(v_copied, CREDIT + b + 1)
                pe.wait_ge(kT_ready, CREDIT + b + 1)
                at.tensor(pe, b)
                pe.wait_ge(summed, CREDIT + (b + 1) * GROUPS)
                for t in range(TILES):
                    ins = nc.tensor.transpose(g.ps[:, 5, t * P:(t + 1) * P], oT[:, t * P:(t + 1) * P], g.ident[:])
                ins.then_inc(o_turned, 1)
                pe.wait_ge(o_stored, CREDIT + b + 1)

        @block.vector
        def _(dve):
            for b in range(BATCH):
                dve.wait_ge(kF_product, b + 1)
                nc.vector.tensor_copy(kF[:, b], g.ps[:, b].rearrange("p (m c) -> p c m", c=W)).then_inc(kF_ready, 1)
            dve.wait_ge(kT_loaded, 16 * BATCH * HEADS)
            dve.wait_ge(loaded, 16 * 4)
            nc.vector.memset(at.p[:], 0.0).then_inc(zeroed, 1)
            with dve.Fori(0, BATCH) as b:
                dve.wait_ge(at.scores_ready, at.at(b, 0))
                nc.vector.tensor_copy(kT[:], kT_all[:, bass.ds(b, 1)].rearrange("p a n -> p (a n)")).then_inc(kT_ready, 1)
                dve.wait_ge(v_ready, CREDIT + b + 1)
                nc.vector.tensor_copy(v[:].rearrange("p t d -> p (t d)"), g.ps[:, 6]).then_inc(v_copied, 1)
                dve.wait_ge(q_copied, CREDIT + b + 1)
                for t in range(TILES):
                    steps = slice(t * P // QB, (t + 1) * P // QB)
                    nc.vector.tensor_tensor(qz[:, steps],
                                            qT[:, t * P:(t + 1) * P].rearrange("p (i q) -> p i q", q=QB)
                                            .unsqueeze(2).broadcast_to([P, P // QB, HEADS, QB]),
                                            heads[:].unsqueeze(1).unsqueeze(3).broadcast_to([P, P // QB, HEADS, QB]),
                                            ALU.mult).then_inc(qz_ready, 1)
                at.vector(dve, b)
                dve.wait_ge(o_turned, CREDIT + b + 1)
                nc.vector.tensor_copy(g.s[:, bass.ds(b * TILES, TILES), :].rearrange("p t d -> p (t d)"),
                                      g.ps[:, 5]).then_inc(o_stored, 1)

        @block.scalar
        def _(act):
            act.wait_ge(zeroed, 1)
            with act.Fori(0, BATCH) as b:
                act.wait_ge(q_ready, CREDIT + b + 1)
                nc.scalar.activation(qT[:], g.ps[:, 4], ACT.Copy, scale=W ** -0.5).then_inc(q_copied, 1)
                at.scalar(act, b)


class Mixture:

    def __init__(self, nc, g, tag, experts, chunks, swiglu, biased, routing):
        self.g, self.tag = g, tag
        self.E, self.HC, self.swiglu, self.biased, self.routing = experts, chunks, swiglu, biased, routing
        self.run()

    def run(self):
        g, nc = self.g, self.g.nc
        E, HC, swiglu, biased, routing = self.E, self.HC, self.swiglu, self.biased, self.routing
        HIN = 2 if swiglu else HC
        K = E
        R = EXPERTS
        W = g.w
        L = self.tag[:2].upper()
        with ExitStack() as stack:
            sb, once, sem = scope(nc, stack, self.tag)
            w1 = sb("w1", [P, E, HIN * P])
            w2 = sb("w2", [P, E, HC, D])
            wg = sb("wg", [P, R])
            b1 = sb("b1", [P, E * HIN]) if biased else None
            b2 = sb("b2", [K, D]) if biased else None
            bg = sb("bg", [P, 2, R]) if biased else None
            iota = sb("iota", [P, R])
            xb = sb("xb", [P, SEQ])
            h = sb("h", [P, 2, HC, SEQ])
            sa = sb("sa", [P, 2, SEQ]) if swiglu else None
            acc = sb("acc", [P, TILES, D])
            z = sb("z", [P, TILES, R])
            zm = sb("zm", [P, TILES])
            pr = sb("pr", [P, TILES, R])
            top = sb("top", [P, TILES, 8])
            idx = sb("idx", [P, TILES, 8], U32)
            idxf = sb("idxf", [P, TILES, 8])
            pick = sb("pick", [P, 2, TILES, R])
            rw = sb("rw", [P, TILES, K])
            rwT = sb("rwT", [K, TILES, P]) if biased else None
            loaded = once("loaded")
            dve_step = once("dve_step")
            xb_ready = sem("xb_ready")
            logits_ready = sem("logits_ready")
            z_ready = sem("z_ready")
            probs_ready = sem("probs_ready")
            rw_ready = sem("rw_ready")
            rw_turned = sem("rw_turned")
            rwT_ready = sem("rwT_ready")
            bias_ready = sem("bias_ready")
            hid_ready = sem("hid_ready")
            half_ready = sem("half_ready")
            h_ready = sem("h_ready")
            out_ready = sem("out_ready")
            acc_step = sem("acc_step")
            gate_ready = sem("gate_ready")
            block = stack.enter_context(nc.Block())
            A = E * TILES + (1 if biased else 0)
            NH = HC * E if not swiglu else E
            PER = HIN if not swiglu else 1

            loads = [(w1, W[f"{L}_w1"]), (w2, W[f"{L}_w2"]), (wg, W[f"{L}_wg"]), (iota, g.c["iota"])]
            if biased:
                loads += [(b1, W[f"{L}_b1"]), (b2, W[f"{L}_b2"]), (bg, W[f"{L}_bg"].partition_broadcast(P))]

            @block.sync
            def _(sp):
                start_counts(sp, sem)
                for dst, src in loads[2:] + loads[:2]:
                    sp.dma_start(dst[:], src).then_inc(loaded, 16)

            @block.gpsimd
            def _(pool):
                with pool.Fori(0, BATCH) as b:
                    pool.wait_ge(hid_ready, CREDIT + b * E * HIN)
                    nc.gpsimd.tensor_copy(xb[:], g.xnT[:, bass.ds(b * SEQ, SEQ)]).then_inc(xb_ready, 1)

            def hidden(pe, b, e):
                for c in range(HIN):
                    i = e * HIN + c
                    if swiglu:
                        pe.wait_ge(h_ready, CREDIT + b * NH + e - 1)
                    else:
                        pe.wait_ge(h_ready, CREDIT + b * NH + i - 3)
                    nc.tensor.matmul(g.ps[:, i % 4], w1[:, e, c * P:(c + 1) * P], xb[:],
                                     start=True, stop=True).then_inc(hid_ready, 1)

            def outputs(pe, b, e):
                pe.wait_ge(h_ready, CREDIT + b * NH + (e + 1) * PER)
                pe.wait_ge(acc_step, CREDIT + b * A + (A - E * TILES) + (e - 1) * TILES if e >= 1 else CREDIT + b * A)
                for t in range(TILES):
                    for c in range(HC):
                        ins = nc.tensor.matmul(g.ps[:, 4 + e % 2, t * D:(t + 1) * D], h[:, e % 2, c, t * P:(t + 1) * P],
                                               w2[:, e, c], start=(c == 0), stop=(c == HC - 1))
                ins.then_inc(out_ready, 1)

            @block.tensor
            def _(pe):
                pe.wait_ge(loaded, 16 * len(loads))
                with pe.Fori(0, BATCH) as b:
                    pe.wait_ge(xb_ready, CREDIT + b + 1)
                    for t in range(TILES):
                        ins = nc.tensor.matmul(g.ps[:, 6, t * R:(t + 1) * R], xb[:, t * P:(t + 1) * P], wg[:],
                                               start=True, stop=True)
                    ins.then_inc(logits_ready, 1)
                    hidden(pe, b, 0)
                    for e in range(E):
                        if e + 1 < E:
                            hidden(pe, b, e + 1)
                        if e == 0 and biased:
                            pe.wait_ge(rw_ready, CREDIT + b + 1)
                            for t in range(TILES):
                                ins = nc.tensor.transpose(g.ps[0:K, 7, t * P:(t + 1) * P], rw[:, t], g.ident[:])
                            ins.then_inc(rw_turned, 1)
                            pe.wait_ge(rwT_ready, CREDIT + b + 1)
                            for t in range(TILES):
                                ins = nc.tensor.matmul(g.ps[:, 6, t * D:(t + 1) * D], rwT[:, t], b2[:],
                                                       start=True, stop=True)
                            ins.then_inc(bias_ready, 1)
                        outputs(pe, b, e)
                    pe.wait_ge(acc_step, CREDIT + b * A + A)

            def route(dve, b):
                ch = Chain(dve, dve_step)
                dve.sem_clear(dve_step)
                dve.wait_ge(logits_ready, CREDIT + b + 1)
                if E > R:
                    ch.done(nc.vector.memset(rw[:, :, R:E], 1.0))
                lg = g.ps[:, 6, 0:TILES * R].rearrange("p (t r) -> p t r", t=TILES)
                if biased:
                    ch.done(nc.vector.tensor_tensor(z[:], lg, bg[:, 0].unsqueeze(1).broadcast_to([P, TILES, R]), ALU.add))
                else:
                    ch.done(nc.vector.tensor_copy(z[:], lg))
                ch.join()
                if routing == "sigmoid":
                    nc.vector.tensor_tensor(z[:], z[:], bg[:, 1].unsqueeze(1).broadcast_to([P, TILES, R]),
                                            ALU.add).then_inc(z_ready, 1)
                    dve.wait_ge(probs_ready, CREDIT + b + 1)
                    ch.done(nc.vector.tensor_copy(z[:], pr[:]))
                    ch.join()
                else:
                    ch.done(nc.vector.tensor_reduce(zm[:], z[:], AX_X, ALU.max))
                    ch.join()
                    nc.vector.tensor_tensor(z[:], z[:], zm[:].unsqueeze(2).broadcast_to([P, TILES, R]),
                                            ALU.subtract).then_inc(z_ready, 1)
                    dve.wait_ge(probs_ready, CREDIT + b + 1)
                    ch.done(nc.vector.tensor_reduce(zm[:], pr[:], AX_X, ALU.add))
                    ch.join()
                    ch.done(nc.vector.reciprocal(zm[:], zm[:]))
                    ch.join()
                    ch.done(nc.vector.tensor_tensor(pr[:], pr[:], zm[:].unsqueeze(2).broadcast_to([P, TILES, R]), ALU.mult))
                    ch.join()
                for t in range(TILES):
                    ch.done(nc.vector.max(top[:, t], pr[:, t]))
                ch.join()
                for t in range(TILES):
                    ch.done(nc.vector.max_index(idx[:, t], top[:, t], pr[:, t]))
                ch.join()
                ch.done(nc.vector.tensor_copy(idxf[:], idx[:]))
                if routing == "renormalized":
                    ch.done(nc.vector.tensor_tensor(zm[:], top[:, :, 0], top[:, :, 1], ALU.add))
                    ch.join()
                    ch.done(nc.vector.reciprocal(zm[:], zm[:]))
                    ch.join()
                    ch.done(nc.vector.tensor_tensor(top[:, :, 0:2], top[:, :, 0:2],
                                                    zm[:].unsqueeze(2).broadcast_to([P, TILES, 2]), ALU.mult))
                ch.join()
                for k in range(2):
                    ch.done(nc.vector.tensor_tensor(pick[:, k], iota[:].unsqueeze(1).broadcast_to([P, TILES, R]),
                                                    idxf[:, :, k:k + 1].broadcast_to([P, TILES, R]), ALU.is_equal))
                ch.join()
                for k in range(2):
                    ch.done(nc.vector.tensor_tensor(pick[:, k], pick[:, k],
                                                    top[:, :, k:k + 1].broadcast_to([P, TILES, R]), ALU.mult))
                ch.join()
                nc.vector.tensor_tensor(rw[:, :, 0:R], pick[:, 0], pick[:, 1], ALU.add).then_inc(rw_ready, 1)
                dve.wait_ge(rw_ready, CREDIT + b + 1)
                ch.join()

            def add_up(dve, b, e):
                dve.wait_ge(out_ready, CREDIT + b * E + e + 1)
                if e == 0 and not biased:
                    dve.wait_ge(gate_ready, CREDIT + b)
                for t in range(TILES):
                    ps = g.ps[:, 4 + e % 2, t * D:(t + 1) * D]
                    if e == 0 and not biased:
                        ins = nc.vector.tensor_scalar(acc[:, t], ps, rw[:, t, 0:1], None, ALU.mult)
                    else:
                        dve.wait_ge(acc_step, CREDIT + b * A + (A - E * TILES) + (e * TILES + t - TILES + 1 if e else 0))
                        ins = nc.vector.scalar_tensor_tensor(acc[:, t], ps, rw[:, t, e:e + 1], acc[:, t],
                                                             ALU.mult, ALU.add)
                    ins.then_inc(acc_step, 1)

            @block.vector
            def _(dve):
                dve.wait_ge(loaded, 16 * len(loads))
                with dve.Fori(0, BATCH) as b:
                    route(dve, b)
                    if biased:
                        dve.wait_ge(rw_turned, CREDIT + b + 1)
                        nc.vector.tensor_copy(rwT[:].rearrange("k t p -> k (t p)"), g.ps[0:K, 7]).then_inc(rwT_ready, 1)
                        dve.wait_ge(bias_ready, CREDIT + b + 1)
                        dve.wait_ge(gate_ready, CREDIT + b)
                        nc.vector.tensor_copy(acc[:].rearrange("p t d -> p (t d)"), g.ps[:, 6]).then_inc(acc_step, 1)
                    for e in range(E):
                        if swiglu:
                            dve.wait_ge(half_ready, CREDIT + b * E + e + 1)
                            dve.wait_ge(hid_ready, CREDIT + b * E * HIN + (e + 1) * HIN)
                            dve.wait_ge(out_ready, CREDIT + b * E + e - 1)
                            nc.vector.scalar_tensor_tensor(h[:, e % 2, 0], g.ps[:, (2 * e + 1) % 4],
                                                           b1[:, 2 * e + 1:2 * e + 2], sa[:, e % 2],
                                                           ALU.add, ALU.mult).then_inc(h_ready, 1)
                        if e >= 1:
                            add_up(dve, b, e - 1)
                    add_up(dve, b, E - 1)

            @block.scalar
            def _(act):
                act.wait_ge(loaded, 16 * len(loads))
                with act.Fori(0, BATCH) as b:
                    act.wait_ge(z_ready, CREDIT + b + 1)
                    nc.scalar.activation(pr[:], z[:], ACT.Sigmoid if routing == "sigmoid" else ACT.Exp).then_inc(probs_ready, 1)
                    for e in range(E):
                        for c in range(1 if swiglu else HIN):
                            i = e * HIN + c
                            act.wait_ge(hid_ready, CREDIT + b * E * HIN + i + 1)
                            if swiglu:
                                act.wait_ge(h_ready, CREDIT + b * NH + e - 1)
                                nc.scalar.activation(sa[:, e % 2], g.ps[:, i % 4], ACT.Silu,
                                                     bias=b1[:, i:i + 1]).then_inc(half_ready, 1)
                            else:
                                act.wait_ge(out_ready, CREDIT + b * E + e - 1)
                                bias = b1[:, i:i + 1] if biased else 0.0
                                nc.scalar.activation(h[:, e % 2, c], g.ps[:, i % 4], ACT.Gelu,
                                                     bias=bias).then_inc(h_ready, 1)
                    act.wait_ge(acc_step, CREDIT + b * A + A)
                    nc.scalar.activation(g.gate[:, bass.ds(b * TILES, TILES), :], acc[:], ACT.Silu).then_inc(gate_ready, 1)


def l0_ffn_stage(g):
    Mixture(g.nc, g, "l0f", EXPERTS + 1, 4, False, True, "sigmoid")


def l1_ffn_stage(g):
    Mixture(g.nc, g, "l1f", EXPERTS + 1, 1, True, True, "softmax")


def l3_ffn_stage(g):
    Mixture(g.nc, g, "l3f", EXPERTS, 4, False, False, "renormalized")


def more_constants():
    q, j = np.arange(P)[:, None] % 64, np.arange(WINDOW + 64)[None] - WINDOW
    outside = (j > q) | (j < q - WINDOW)
    band = np.where(np.stack([outside | (j < 0), outside], 1), -1e30, 0).astype(np.float32)
    step_down = np.zeros((P, 2, P), np.float32)
    step_down[:, 0] = np.eye(P, k=1)
    step_down[P - 1, 1, 0] = 1
    return {"rope": rotary_constants(), "band": band, "step_down": step_down, "pick": np.tile(np.eye(32, dtype=np.float32), (3, 1)), "iota": np.tile(np.arange(EXPERTS, dtype=np.float32), (P, 1))}


def more_layouts(a, out, rows, cols):
    H = a["L0_ffn_W1"].shape[1]
    w1 = np.concatenate([a["L0_ffn_W1"], a["L0_ffn_Ws1"][None]])
    w2 = np.concatenate([a["L0_ffn_W2"], a["L0_ffn_Ws2"][None]])
    out["L0_w1"] = w1.transpose(2, 0, 1)
    out["L0_w2"] = w2.transpose(2, 0, 1).reshape(H // P, P, EXPERTS + 1, D).transpose(1, 2, 0, 3)
    out["L0_wg"] = a["L0_ffn_Wg"].T
    out["L0_bg"] = np.stack([a["L0_ffn_bg"], a["L0_ffn_bias"]])
    out["L0_b1"] = cols(np.concatenate([a["L0_ffn_b1"], a["L0_ffn_bs1"][None]]).reshape(-1))
    out["L0_b2"] = np.concatenate([a["L0_ffn_b2"], a["L0_ffn_bs2"][None]])
    out["L1_w1"] = np.concatenate([a["L1_ffn_rw1"], a["L1_ffn_sw1"]]).transpose(1, 0, 2)
    out["L1_w2"] = np.concatenate([a["L1_ffn_rw2"], a["L1_ffn_sw2"]]).transpose(1, 0, 2)[:, :, None]
    out["L1_wg"] = a["L1_ffn_gate_w"]
    out["L1_bg"] = np.stack([a["L1_ffn_gate_b"], a["L1_ffn_gate_b"]])
    out["L1_b1"] = cols(np.concatenate([a["L1_ffn_rb1"], a["L1_ffn_sb1"]]).reshape(-1))
    out["L1_b2"] = np.concatenate([a["L1_ffn_rb2"], a["L1_ffn_sb2"]])
    F = a["L3_ffn_w1"].shape[2]
    out["L3_w1"] = a["L3_ffn_w1"].transpose(1, 0, 2)
    out["L3_w2"] = a["L3_ffn_w2"].reshape(EXPERTS, F // P, P, D).transpose(2, 0, 1, 3)
    out["L3_wg"] = a["L3_ffn_gate_w"]
    out["L0_attn_Wq"] = a["L0_attn_Wq"]
    out["L0_attn_Wkv"] = a["L0_attn_Wkv"]
    out["L0_attn_Wout"] = rows(a["L0_attn_Wout"])
    for n in ("gamma", "q_scale", "k_scale"):
        out[f"L0_attn_{n}"] = a[f"L0_attn_{n}"][:, None]
    out["L0_attn_null_kv"] = a["L0_attn_null_kv"]
    out["L3_attn_qkv_weights"] = a["L3_attn_qkv_weights"]
    for u in (1, 2):
        m = f"L2_attn_m{u}_"
        for n in ("Win", "Wx", "Wout", "Wconv", "Alog", "Wdt"):
            out[f"L2_m{u}_{n}"] = a[m + n]
        out[f"L2_m{u}_vec"] = np.stack([a[m + "bconv"], a[m + "bdt"], a[m + "Dp"]], 1)
    out["L2_attn_ln"] = np.stack([a["L2_attn_ln_g"], a["L2_attn_ln_b"]], 1)
    for n in ("Wqkv", "q_scale", "k_scale", "W1", "b1", "W2", "b2"):
        out[f"L2_ffn_{n}"] = a[f"L2_ffn_{n}"]
    out["L2_ffn_Wo"] = a["L2_ffn_Wo"].reshape(DEPTH, PAIRS, P, D).transpose(0, 2, 1, 3)
    out["L2_ffn_ln"] = np.stack([a["L2_ffn_ln_g"], a["L2_ffn_ln_b"]], 2).transpose(1, 0, 2)


def rotary_constants():
    f = np.float32
    half = np.arange(0, DH, 2, dtype=f)
    inv_freq = f(1) / f(10000) ** (half / f(DH))
    t = np.arange(SEQ, dtype=f)
    freqs = t[:, None] * inv_freq[None]
    freqs = np.concatenate([freqs, freqs], -1)
    base = (half + f(0.4 * DH)) / f(1.4 * DH)
    power = (t - SEQ // 2) / f(WINDOW // 2)
    scale = base[None] ** power[:, None]
    scale = np.concatenate([scale, scale], -1)
    sign = np.where(np.arange(DH) < DH // 2, -1, 1).astype(f)
    cos, sin = np.cos(freqs), np.sin(freqs) * sign
    q = np.stack([cos * scale, sin * scale]) * f(8)
    k = np.stack([cos / scale, sin / scale])
    return np.stack([q, k]).astype(f).reshape(2, 2, TILES, P, DH).transpose(3, 0, 1, 2, 4)


ATTN = (l0_attn_stage, l1_attn_stage, l2_attn_stage, l3_attn_stage)
FFN = (l0_ffn_stage, l1_ffn_stage, l2_ffn_stage, l3_ffn_stage)


def finish_stage(g, gate_tensor, last):
    nc = g.nc
    tag = f"upd{g.serial}"
    g.serial += 1
    with ExitStack() as stack:
        sb, sem, _ = scope(nc, stack, tag)
        prod_done = sem("prod_done")
        x_ready = sem("x_ready")
        stored = sem("stored")
        block = stack.enter_context(nc.Block())

        @block.vector
        def _(dve):
            nc.vector.tensor_tensor(g.s[:], g.s[:], gate_tensor[:], ALU.mult).then_inc(prod_done, 1)
            dve.wait_ge(prod_done, 1)
            nc.vector.tensor_tensor(g.x[:], g.x[:], g.s[:], ALU.add).then_inc(x_ready, 1)

        @block.sync
        def _(sp):
            if last:
                sp.wait_ge(x_ready, 1)
                sp.dma_start(g.out.rearrange("b (t p) d -> p (b t) d", p=P), g.x[:]).then_inc(stored, 16)
                sp.wait_ge(stored, 16)


def four_gated_layers(nc, x_in, weights, consts, out):
    g = Ctx()
    g.nc, g.x_in, g.w, g.c, g.out, g.serial = nc, x_in, weights, consts, out, 0
    with ExitStack() as stack:
        def sb(name, shape, dt=F32):
            return stack.enter_context(nc.sbuf_tensor(name, shape, dt))

        g.x = sb("x", [P, NT, D])
        g.xn = sb("xn", [P, NT, D])
        g.xnT = sb("xnT", [P, BATCH * SEQ])
        g.s = sb("s", [P, NT, D])
        g.gate = sb("gate", [P, NT, D])
        g.ident = sb("ident", [P, P])
        g.identb = sb("identb", [P, P], BF16)
        g.causal64 = sb("causal64", [P, 64], BF16)
        g.causal8 = sb("causal8", [P, 8], BF16)
        g.neghalf = sb("neghalf", [P, 64])
        g.ps = stack.enter_context(nc.psum_tensor("ps", [P, 8, 512], F32))
        load_stage(g)
        run_stages(g)


def run_stages(g):
    for k in range(4):
        norm_stage(g, f"n{k}")
        ATTN[k](g)
        FFN[k](g)
        finish_stage(g, g.gate, k == 3)


def constants():
    i = np.arange(P)

    def causal(n):
        return np.where(np.arange(n)[None] > i[:, None] % n, np.float32(-1e30), np.float32(0))

    heads = (i[:, None] // (D // HEADS) == np.arange(HEADS)[None]).astype(np.float32)
    return {"ident": np.eye(P, dtype=np.float32), "causal64": causal(64), "causal8": causal(8), "heads": heads,
            **more_constants()}


def layouts(a):
    def rows(w):
        return w.reshape(-1, P, w.shape[-1]).transpose(1, 0, 2)

    def cols(v):
        return v.reshape(-1, P).T

    HD = HEADS * DH
    out = {}
    for n in ("q", "k", "v"):
        out[f"L1_attn_W{n}"] = a[f"L1_attn_W{n}"].transpose(1, 0, 2).reshape(D, HD)
    out["L1_attn_Wo"] = rows(a["L1_attn_Wo"].reshape(HD, D))
    out["L1_attn_bq"] = cols(a["L1_attn_bq"].reshape(HD))
    out["L1_attn_bk"] = cols(a["L1_attn_bk"].reshape(HD))
    out["L1_attn_bv"] = a["L1_attn_bv"].reshape(HD)
    out["L1_attn_bo"] = a["L1_attn_bo"]
    more_layouts(a, out, rows, cols)
    return out


def kernel(**inputs):
    import concourse.bacc as _bacc
    from concourse.bass_utils import run_bass_kernel_spmd as _run

    nc = _bacc.Bacc("TRN2", target_bir_lowering=False, num_devices=1)
    arrays = {}

    def dram(name, a):
        a = np.ascontiguousarray(a)
        arrays[name] = a
        return nc.dram_tensor(name, a.shape, mybir.dt.from_np(a.dtype), kind="ExternalInput").ap()

    x = dram("x_dram", inputs["L0_attn_x"])
    weights = {n: dram(f"{n}_dram", a) for n, a in layouts({k: np.asarray(v) for k, v in inputs.items()}).items()}
    consts = {n: dram(f"{n}_const", a) for n, a in constants().items()}
    out = nc.dram_tensor("out_dram", (BATCH, SEQ, D), F32, kind="ExternalOutput").ap()
    four_gated_layers(nc, x, weights, consts, out)
    r = _run(nc, [arrays], core_ids=[0])
    return r.results[0]["out_dram"]
```
